# Optimizing a Trainium2 kernel written in Bass

```python
import numpy as np
import jax
import jax.numpy as jnp

def _softmax(x, axis=-1):
    return jax.nn.softmax(x, axis=axis)

def _gelu(x):
    return jax.nn.gelu(x, approximate=True)

def _silu(x):
    return jax.nn.silu(x)

def _sigmoid(x):
    return jax.nn.sigmoid(x)

def _layernorm(x, axis=-1, eps=1e-05):
    m = jnp.mean(x, axis=axis, keepdims=True)
    v = jnp.var(x, axis=axis, keepdims=True)
    return (x - m) / jnp.sqrt(v + eps)

def _scatter_add(tgt, idx, src, axis=0):
    return tgt.at[idx].add(src)

def _segment_sum(src, seg, n):
    return jax.ops.segment_sum(src, seg, n)
kernel_name = 'mk_metaformer_d1_conv_nhwc256_r2_ea769a'

def setup_inputs(seed: int=0):
    np.random.seed(seed)
    _w = jnp.asarray

    def _rec_inputs():
        import jax
        import jax.numpy as jnp
        _gk = jax.random.key(seed)
        x = -0.0003929 + 0.9999 * jax.random.normal(jax.random.fold_in(_gk, 1), (4, 64, 64, 128), jnp.float32)
        return x
    x = _rec_inputs()

    def _L0_conv_setup():
        import jax, jax.numpy as jnp
        import numpy as np
        F = 128
        K = 3
        G = 16
        RR = 4
        BN_EPS = 0.001
        key = jax.random.key(seed)
        ks = jax.random.split(key, 8)
        C = 128
        Cr = F // RR
        KKG = K * K * G
        s = lambda k, sh, fan: jax.random.normal(k, sh, jnp.float32) * (1.0 / np.sqrt(fan))
        return {'x': jax.random.normal(ks[0], (4, 64, 64, C), jnp.float32), 'Wr': s(ks[1], (C, Cr), C), 'br': jnp.zeros((Cr,), jnp.float32), 'gamma': jnp.ones((Cr,), jnp.float32), 'beta': jnp.zeros((Cr,), jnp.float32), 'mean': jax.random.normal(ks[2], (Cr,), jnp.float32) * 0.1, 'var': jax.random.uniform(ks[3], (Cr,), jnp.float32, 0.5, 1.5), 'Ws': s(ks[4], (Cr, KKG), Cr), 'bs': jnp.zeros((KKG,), jnp.float32), 'Wi': s(ks[5], (C, F), C), 'bi': jnp.zeros((F,), jnp.float32)}
    _L0_conv_all = _L0_conv_setup()
    _L0_conv_in = {k: v for k, v in _L0_conv_all.items() if k in ('Wr', 'br', 'gamma', 'beta', 'mean', 'var', 'Ws', 'bs', 'Wi', 'bi')}
    del _L0_conv_all

    def _L0_ffn_setup():
        import jax, jax.numpy as jnp
        import numpy as np
        B, N, D = (16, 2048, 128)
        NUM_EXPERTS, TOP_K, HEADS = (4, 2, 4)
        N_EDGES = 524288
        LN_EPS = 1e-05

        def _layernorm(x, g, b):
            mu = x.mean(-1, keepdims=True)
            var = ((x - mu) ** 2).mean(-1, keepdims=True)
            return (x - mu) * jax.lax.rsqrt(var + LN_EPS) * g + b

        def _forward(x, edge_index, W_gat, att_src, att_dst, b_gat, ln_gamma, ln_beta, W1, b1, W2, b2):
            Bc, Nc, Dc = x.shape
            M = Bc * Nc
            x_flat = x.reshape(M, Dc)
            h = (x_flat @ W_gat).reshape(M, HEADS, NUM_EXPERTS)
            loops = jnp.arange(M, dtype=edge_index.dtype)
            src = jnp.concatenate([edge_index[0], loops])
            dst = jnp.concatenate([edge_index[1], loops])
            a_src = (h * att_src).sum(-1)
            a_dst = (h * att_dst).sum(-1)
            e = jax.nn.leaky_relu(a_src[src] + a_dst[dst], negative_slope=0.2)
            e_max = jax.ops.segment_max(e, dst, num_segments=M)
            ee = jnp.exp(e - e_max[dst])
            denom = jax.ops.segment_sum(ee, dst, num_segments=M)
            alpha = ee / (denom[dst] + 1e-16)
            msg = h[src] * alpha[:, :, None]
            agg = jax.ops.segment_sum(msg, dst, num_segments=M).reshape(M, HEADS * NUM_EXPERTS) + b_gat
            scores = _layernorm(agg, ln_gamma, ln_beta).reshape(M, HEADS, NUM_EXPERTS).mean(1)
            scores = scores.reshape(Bc, Nc, NUM_EXPERTS)
            topk_s, topk_i = jax.lax.top_k(scores, TOP_K)
            w = jax.nn.softmax(topk_s, axis=-1)
            out = jnp.zeros_like(x)
            for ei in range(NUM_EXPERTS):
                g = jnp.where(topk_i == ei, w, 0.0).sum(-1)
                hh = jax.nn.gelu(x @ W1[ei] + b1[ei], approximate=False)
                out = out + g[..., None] * (hh @ W2[ei] + b2[ei])
            return out
        key = jax.random.key(seed)
        ks = jax.random.split(key, 8)
        s = 0.05
        return {'x': jax.random.normal(ks[0], (B, N, D), jnp.float32), 'W_gat': jax.random.normal(ks[1], (D, HEADS * NUM_EXPERTS), jnp.float32) * s, 'att_src': jax.random.normal(ks[2], (HEADS, NUM_EXPERTS), jnp.float32) * s, 'att_dst': jax.random.normal(ks[3], (HEADS, NUM_EXPERTS), jnp.float32) * s, 'b_gat': jnp.zeros((HEADS * NUM_EXPERTS,), jnp.float32), 'ln_gamma': jnp.ones((HEADS * NUM_EXPERTS,), jnp.float32), 'ln_beta': jnp.zeros((HEADS * NUM_EXPERTS,), jnp.float32), 'W1': jax.random.normal(ks[4], (NUM_EXPERTS, D, 2 * D), jnp.float32) * s, 'b1': jnp.zeros((NUM_EXPERTS, 2 * D), jnp.float32), 'W2': jax.random.normal(ks[5], (NUM_EXPERTS, 2 * D, D), jnp.float32) * s, 'b2': jnp.zeros((NUM_EXPERTS, D), jnp.float32), 'edge_index': jax.random.randint(ks[6], (2, N_EDGES), 0, B * N, jnp.int32)}
    _L0_ffn_all = _L0_ffn_setup()
    _L0_ffn_in = {k: v for k, v in _L0_ffn_all.items() if k in ('W_gat', 'att_src', 'att_dst', 'b_gat', 'ln_gamma', 'ln_beta', 'W1', 'b1', 'W2', 'b2', 'edge_index')}
    del _L0_ffn_all
    return {'x': x, 'L0_conv_Wr': _L0_conv_in['Wr'], 'L0_conv_br': _L0_conv_in['br'], 'L0_conv_gamma': _L0_conv_in['gamma'], 'L0_conv_beta': _L0_conv_in['beta'], 'L0_conv_mean': _L0_conv_in['mean'], 'L0_conv_var': _L0_conv_in['var'], 'L0_conv_Ws': _L0_conv_in['Ws'], 'L0_conv_bs': _L0_conv_in['bs'], 'L0_conv_Wi': _L0_conv_in['Wi'], 'L0_conv_bi': _L0_conv_in['bi'], 'L0_ffn_W_gat': _L0_ffn_in['W_gat'], 'L0_ffn_att_src': _L0_ffn_in['att_src'], 'L0_ffn_att_dst': _L0_ffn_in['att_dst'], 'L0_ffn_b_gat': _L0_ffn_in['b_gat'], 'L0_ffn_ln_gamma': _L0_ffn_in['ln_gamma'], 'L0_ffn_ln_beta': _L0_ffn_in['ln_beta'], 'L0_ffn_W1': _L0_ffn_in['W1'], 'L0_ffn_b1': _L0_ffn_in['b1'], 'L0_ffn_W2': _L0_ffn_in['W2'], 'L0_ffn_b2': _L0_ffn_in['b2'], 'L0_ffn_edge_index': _L0_ffn_in['edge_index']}

def reference(x, L0_conv_Wr, L0_conv_br, L0_conv_gamma, L0_conv_beta, L0_conv_mean, L0_conv_var, L0_conv_Ws, L0_conv_bs, L0_conv_Wi, L0_conv_bi, L0_ffn_W_gat, L0_ffn_att_src, L0_ffn_att_dst, L0_ffn_b_gat, L0_ffn_ln_gamma, L0_ffn_ln_beta, L0_ffn_W1, L0_ffn_b1, L0_ffn_W2, L0_ffn_b2, L0_ffn_edge_index):
    import jax
    import jax.numpy as jnp

    def _L0_conv_ref(x, Wr, br, gamma, beta, mean, var, Ws, bs, Wi, bi):
        import jax, jax.numpy as jnp
        import numpy as np
        F = 128
        K = 3
        G = 16
        RR = 4
        BN_EPS = 0.001
        B, H, W, _ = x.shape
        KK = K * K
        r = jnp.einsum('bhwc,cd->bhwd', x, Wr) + br
        r = jax.nn.relu((r - mean) * jax.lax.rsqrt(var + BN_EPS) * gamma + beta)
        w = jnp.einsum('bhwd,dk->bhwk', r, Ws) + bs
        w = w.reshape(B, H, W, G, KK)[:, :, :, :, None, :]
        xi = jnp.einsum('bhwc,cf->bhwf', x, Wi) + bi
        pad = (K - 1) // 2
        xp = jnp.pad(xi, ((0, 0), (pad, pad), (pad, pad), (0, 0)))
        patches = jnp.stack([xp[:, i:i + H, j:j + W, :] for i in range(K) for j in range(K)], axis=3)
        patches = patches.reshape(B, H, W, G, F // G, KK)
        out = jnp.sum(w * patches, axis=-1)
        return out.reshape(B, H, W, F)

    def _L0_ffn_ref(x, W_gat, att_src, att_dst, b_gat, ln_gamma, ln_beta, W1, b1, W2, b2, edge_index):
        import jax, jax.numpy as jnp
        import numpy as np
        B, N, D = (16, 2048, 128)
        NUM_EXPERTS, TOP_K, HEADS = (4, 2, 4)
        N_EDGES = 524288
        LN_EPS = 1e-05

        def _layernorm(x, g, b):
            mu = x.mean(-1, keepdims=True)
            var = ((x - mu) ** 2).mean(-1, keepdims=True)
            return (x - mu) * jax.lax.rsqrt(var + LN_EPS) * g + b

        def _forward(x, edge_index, W_gat, att_src, att_dst, b_gat, ln_gamma, ln_beta, W1, b1, W2, b2):
            Bc, Nc, Dc = x.shape
            M = Bc * Nc
            x_flat = x.reshape(M, Dc)
            h = (x_flat @ W_gat).reshape(M, HEADS, NUM_EXPERTS)
            loops = jnp.arange(M, dtype=edge_index.dtype)
            src = jnp.concatenate([edge_index[0], loops])
            dst = jnp.concatenate([edge_index[1], loops])
            a_src = (h * att_src).sum(-1)
            a_dst = (h * att_dst).sum(-1)
            e = jax.nn.leaky_relu(a_src[src] + a_dst[dst], negative_slope=0.2)
            e_max = jax.ops.segment_max(e, dst, num_segments=M)
            ee = jnp.exp(e - e_max[dst])
            denom = jax.ops.segment_sum(ee, dst, num_segments=M)
            alpha = ee / (denom[dst] + 1e-16)
            msg = h[src] * alpha[:, :, None]
            agg = jax.ops.segment_sum(msg, dst, num_segments=M).reshape(M, HEADS * NUM_EXPERTS) + b_gat
            scores = _layernorm(agg, ln_gamma, ln_beta).reshape(M, HEADS, NUM_EXPERTS).mean(1)
            scores = scores.reshape(Bc, Nc, NUM_EXPERTS)
            topk_s, topk_i = jax.lax.top_k(scores, TOP_K)
            w = jax.nn.softmax(topk_s, axis=-1)
            out = jnp.zeros_like(x)
            for ei in range(NUM_EXPERTS):
                g = jnp.where(topk_i == ei, w, 0.0).sum(-1)
                hh = jax.nn.gelu(x @ W1[ei] + b1[ei], approximate=False)
                out = out + g[..., None] * (hh @ W2[ei] + b2[ei])
            return out
        return _forward(x, edge_index, W_gat, att_src, att_dst, b_gat, ln_gamma, ln_beta, W1, b1, W2, b2)

    def _gn(v, G=32, eps=1e-05):
        B_, H_, W_, C_ = v.shape
        g = v.reshape(B_, H_, W_, G, C_ // G)
        m = jnp.mean(g, axis=(1, 2, 4), keepdims=True)
        s = jnp.var(g, axis=(1, 2, 4), keepdims=True)
        return ((g - m) / jnp.sqrt(s + eps)).reshape(v.shape)

    def _ln_c(v, eps=1e-06):
        m = jnp.mean(v, axis=-1, keepdims=True)
        s = jnp.var(v, axis=-1, keepdims=True)
        return (v - m) / jnp.sqrt(s + eps)

    def _ln_t(v, eps=1e-05):
        m = jnp.mean(v, axis=-1, keepdims=True)
        s = jnp.var(v, axis=-1, keepdims=True)
        return (v - m) / jnp.sqrt(s + eps)

    def _to_tokens(v):
        B_, H_, W_, C_ = v.shape
        return v.reshape(B_, H_ * W_, C_)

    def _from_tokens(t, like):
        return t.reshape(like.shape)
    x = x + _L0_conv_ref(_ln_c(x), L0_conv_Wr, L0_conv_br, L0_conv_gamma, L0_conv_beta, L0_conv_mean, L0_conv_var, L0_conv_Ws, L0_conv_bs, L0_conv_Wi, L0_conv_bi)
    t = _to_tokens(x)
    t = t + _L0_ffn_ref(_ln_t(t), L0_ffn_W_gat, L0_ffn_att_src, L0_ffn_att_dst, L0_ffn_b_gat, L0_ffn_ln_gamma, L0_ffn_ln_beta, L0_ffn_W1, L0_ffn_b1, L0_ffn_W2, L0_ffn_b2, L0_ffn_edge_index)
    x = _from_tokens(t, x)
    return x

_drawn_inputs = setup_inputs


def setup_inputs(seed=0):
    import zlib

    import numpy as np

    out = dict(_drawn_inputs(seed))
    spreads = {'L0_conv_br': (0.0, 0.1),
     'L0_conv_gamma': (1.0, 0.2),
     'L0_conv_beta': (0.0, 0.1),
     'L0_conv_bs': (0.0, 0.1),
     'L0_conv_bi': (0.0, 0.1),
     'L0_ffn_b_gat': (0.0, 0.1),
     'L0_ffn_ln_gamma': (1.0, 0.542),
     'L0_ffn_ln_beta': (0.0, 0.699),
     'L0_ffn_b1': (0.0, 0.617),
     'L0_ffn_b2': (0.0, 0.292)}
    factors = {'L0_ffn_att_src': 8.0, 'L0_ffn_att_dst': 8.0}
    for name, (base, spread) in spreads.items():
        noise = np.random.default_rng([zlib.crc32(name.encode()), seed]).standard_normal(out[name].shape)
        drawn = base * np.exp(spread * noise) if base else spread * noise
        out[name] = jnp.asarray(drawn.astype(out[name].dtype))
    for name, factor in factors.items():
        out[name] = (out[name] * factor).astype(out[name].dtype)
    return out
```

```python
from contextlib import ExitStack

import concourse.bass as bass
from concourse import mybir

F32 = mybir.dt.float32
I32 = mybir.dt.int32
ALU = mybir.AluOpType
ACT = mybir.ActivationFunctionType
AX = mybir.AxisListType

P = 128
NB, NY, NX, C = 4, 64, 64, 128
M = NB * NY * NX
PAIRS = NB // 2
TILES = M // P
EDGES = 524288
COLS = EDGES // P
LOG_E, LOG_C = 19, 12
SRC_BITS = 14
SINK = M
KEY_BASE = 2 * M
DROPPED = 4 * M
KK, GROUPS = 9, 16
TAPS = KK * C
CR = 32
HEADS, EXPERTS, HID = 4, 4, 256
HE = HEADS * EXPERTS
ROW = HE + HEADS
NODE = ROW + HEADS
ST = 2 * HEADS + HE
T = 64
BIG = 1.0e30
ROWS = 4
CHUNKS = NY // ROWS
TOK = ROWS * P
LV = 64
SKIP = float(1 << 20)
TR, FA = True, False


def some(n):
    return not isinstance(n, int) or n > 0


def metaformer_block(nc, x, Wr, br, gamma, beta, mean, var, Ws, bs, Wi, bi,
                     W_gat, att_src, att_dst, b_gat, ln_gamma, ln_beta,
                     W1, b1, W2, b2, edge_index, out):
    ctx = ExitStack()
    with ctx:
        def sb(name, shape, dt=F32, where=ctx):
            return where.enter_context(nc.sbuf_tensor("sb_" + name, shape, dt))

        def dram(name, shape, dt=F32):
            return nc.dram_tensor("scr_" + name, shape, dt, kind="Internal").ap()

        def sem(name):
            return ctx.enter_context(nc.semaphore(name))

        ds = bass.ds

        keys_d = dram("keys", [EDGES + COLS])
        runs_d = dram("runs", [P, COLS])
        level1_d = dram("level1", [P])
        level2_d = dram("level2", [P, LV])
        ends_d = dram("ends", [2, M + 1])
        node_d = dram("node", [M, ROW])
        adst_d = dram("adst", [M, HEADS])
        starts_d = dram("adst_at_starts", [EDGES, HEADS])
        state_d = dram("state", [EDGES, ST])
        tails_d = dram("tails", [P, ST])
        chain_d = dram("chain", [P + 1, ST])
        x2_d = dram("x2", [PAIRS * CHUNKS, P, TOK])
        tnT_d = dram("tnT", [PAIRS * CHUNKS, C, TOK])

        ident = sb("ident", [P, P])
        node = sb("node", [P, TILES, NODE])
        part = sb("part", [P, 1], I32)
        partf = sb("partf", [P, 1])
        sign_i = sb("sign_i", [P, LOG_E - LOG_C], I32)
        signs = sb("signs", [P, LOG_E - LOG_C])
        wr = sb("wr", [C, CR])
        ws = sb("ws", [CR + 1, KK * GROUPS])
        wi = sb("wi", [C, C])
        valid = sb("valid", [3, NX, 2])
        bi3 = sb("bi3", [3, 3 * C])
        bn = sb("bn", [CR, 8])
        wgat = sb("wgat", [C, NODE])
        att = sb("att", [P, 2, HE])
        eps = sb("eps", [P, 3])
        ends = sb("ends", [P, 2, P])

        bank = [ctx.enter_context(nc.psum_tensor(f"bank{i}", [P, 512], F32)) for i in range(8)]

        early = ExitStack()
        xi = sb("xi", [P, (NY + 2) * 3 * C], F32, early)
        xa = sb("xa", [P, 2, ROWS, C], F32, early)
        xb = sb("xb", [P, 2, ROWS, C], F32, early)
        xn = sb("xn", [P, 2, ROWS, C], F32, early)
        xnT = sb("xnT", [C, 2, ROWS, P + 4], F32, early)
        rT = sb("rT", [CR + 1, 2, TOK], F32, early)
        wv = sb("wv", [P, 2, ROWS, KK * GROUPS], F32, early)
        prod = sb("prod", [P, 2, TAPS], F32, early)
        inv = sb("inv", [P, ROWS, C], F32, early)
        tn = sb("tn", [P, ROWS, C], F32, early)
        tnT = sb("tnT", [C, 2, TOK], F32, early)
        stats = sb("stats", [P, 2, ROWS, 6], F32, early)
        mv = sb("mv", [P, 2, ROWS, 2], F32, early)
        sd = sb("sd", [P, 2, ROWS], F32, early)
        rstd = sb("rstd", [P, 2, ROWS], F32, early)
        found = sb("found", [P, P * LV], F32, early)
        samples = sb("samples", [P, P], F32, early)
        target = sb("target", [P, 2, P], I32, early)
        rank1 = sb("rank1", [P, 2, P], F32, early)
        rank2 = sb("rank2", [P, 2, P], F32, early)
        row1 = sb("row1", [P, 2, P], I32, early)
        row2 = sb("row2", [P, 2, P], I32, early)
        lvl2 = sb("lvl2", [P, LV], F32, early)
        zero = sb("zero", [P, 512], F32, early)
        key_bufs = [xi[:, 0:COLS], xi[:, COLS:2 * COLS]]
        tmp_a, tmp_b = xi[:, 2 * COLS:3 * COLS], xi[:, 3 * COLS:4 * COLS]
        early.close()

        runk = sb("runk", [P, COLS], I32)
        srci = sb("srci", [P, COLS], I32)
        step_i = sb("step_i", [P, 2, T], I32)
        clsi = sb("clsi", [P, COLS], I32)
        same = sb("same", [P, COLS])
        reset = sb("reset", [P, COLS])
        rows_g = sb("rows_g", [P, 2, T, ROW])
        dch = sb("dch", [P, 2, T, HEADS])
        df = sb("df", [P, T + 1, HEADS])
        score = sb("score", [P, T, HEADS])
        ex = sb("ex", [P, T, 2, HEADS])
        pv = sb("pv", [P, T, HE])
        state = sb("state", [P, 2, T + 1, ST])
        endT = sb("endT", [P, 4, P])
        endO = sb("endO", [P, 4, P])
        endG = sb("endG", [P, 4, TILES])
        nonempty = sb("nonempty", [P, 1, TILES])
        pos = sb("pos", [P, 2, TILES])
        quo = sb("quo", [P, 2, TILES])
        fit = sb("fit", [P, 2, TILES])
        quoi = sb("quoi", [P, 2, TILES], I32)
        posi = sb("posi", [P, 2, TILES], I32)
        cnt = sb("cnt", [P, 8])
        cnti = sb("cnti", [P, 4], I32)
        edge_i = sb("edge_i", [P, 10], I32)
        edge_f = sb("edge_f", [P, 12])
        adst0 = sb("adst0", [P, HEADS])
        chk = sb("chk", [1, 2, P], I32)
        chf = sb("chf", [1, 5, P])
        cprev = sb("cprev", [P, ST])
        fixs = sb("fixs", [P, ST])
        fixo = sb("fixo", [P, ST])
        fixe = sb("fixe", [P, 2, HEADS])
        endf = sb("endf", [P, 1])
        last_row = sb("last_row", [P, ROW])
        gat_p = sb("gat_p", [P, 3, HE])
        agg = sb("agg", [P, TILES, ST])
        one4 = sb("one4", [P, 4, TILES])
        gate = sb("gate", [P, TILES, EXPERTS])
        w1 = sb("w1", [C, EXPERTS, HID])
        w2 = sb("w2", [P, EXPERTS, 2, C])
        b1c = sb("b1c", [P, EXPERTS, 2])
        b2r = sb("b2r", [1, EXPERTS * C])
        ones = sb("ones", [1, P])
        tails = same[0:1, 0:P * ST].rearrange("p (n f) -> p n f", f=ST)
        chx = reset[0:1, 0:(P + 1) * ST].rearrange("p (n f) -> p n f", f=ST)
        chp = srci[:].bitcast(F32)[0:1, 0:P * ROW].rearrange("p (n f) -> p n f", f=ROW)
        che = clsi[:].bitcast(F32)[0:1, 0:P * 2 * HEADS].rearrange("p (n a h) -> p n a h", a=2, h=HEADS)
        wide = same[:, 0:2 * TILES * HE].rearrange("p (a t f) -> p a t f", a=2, f=HE)
        hx = reset[:, 0:5 * TILES * HEADS].rearrange("p (a t h) -> p a t h", a=5, h=HEADS)
        hid = [srci[:].bitcast(F32).rearrange("p (a t) -> p a t", a=8),
               clsi[:].bitcast(F32).rearrange("p (a t) -> p a t", a=8)]
        tnT_in = runk[:].bitcast(F32)[:, 0:2 * TOK].rearrange("p (u t) -> p u t", u=2)
        x2_in = runk[:].bitcast(F32)[:, 2 * TOK:4 * TOK].rearrange("p (u t) -> p u t", u=2)

        def sems(names):
            return [sem(n) for n in names.split()]

        (ident_zero, consts_made, dst_loaded, src_loaded, params_loaded, small_ready,
         bn_root, bn_ready, found_zero, zeros_stored) = sems(
            "ident_zero consts_made dst_loaded src_loaded params_loaded small_ready "
            "bn_root bn_ready found_zero zeros_stored")
        (phase_sorted, flipped, act_placed, keys_final, keys_stored, levels_stored,
         samples_loaded, ranked) = sems(
            "phase_sorted flipped act_placed keys_final keys_stored levels_stored "
            "samples_loaded ranked")
        rows_found = sems("rows_found0 rows_found1")
        (stats1, root1, normed1, turned1, xnT_ready, r_psum, rT_ready, xi_psum, xi_ready,
         w_psum, w_ready, pe_chunk, conv_done, root2, normed2, turned2, tnT_ready,
         node_psum, node_ready) = sems(
            "stats1 root1 normed1 turned1 xnT_ready r_psum rT_ready xi_psum xi_ready "
            "w_psum w_ready pe_chunk conv_done root2 normed2 turned2 tnT_ready "
            "node_psum node_ready")
        xa_in, xb_in, x2_out, tnT_out = (sems(f"{n}0 {n}1") for n in
                                         ("xa_in", "xb_in", "x2_out", "tnT_out"))
        (node_stored, ends_stored, ends_loaded, ends_ordered, ends_turned, counted, runs_stored, runk_loaded,
         prev_zero, border_loaded, border_ready, adst0_loaded, sources_ready, grid_ready,
         starts_scattered, first_stored) = sems(
            "node_stored ends_stored ends_loaded ends_ordered ends_turned counted runs_stored runk_loaded "
            "prev_zero border_loaded border_ready adst0_loaded sources_ready grid_ready "
            "starts_scattered first_stored")
        dch_in, dch_used, rows_in, rows_used, state_out = (
            sems(f"{n}0 {n}1") for n in ("dch_in", "dch_used", "rows_in", "rows_used", "state_out"))
        (scored, weighed, state_ready, tails_stored, tails_loaded, chain_scored, chain_weighed,
         chain_ready, chain_stored, cprev_loaded, end_found, fix_placed, fix_got, fix_scored,
         fix_weighed, fix_ready, fix_stored, agg_cleared, agg_got) = sems(
            "scored weighed state_ready tails_stored tails_loaded chain_scored chain_weighed "
            "chain_ready chain_stored cprev_loaded end_found fix_placed fix_got fix_scored "
            "fix_weighed fix_ready fix_stored agg_cleared agg_got")
        (late_loaded, joined, join_weighed, agg_var, agg_root, top_ready, top_weighed, gates_ready,
         hid_psum, hid_ready, hid_used, y_psum, mixed) = sems(
            "late_loaded joined join_weighed agg_var agg_root top_ready top_weighed gates_ready "
            "hid_psum hid_ready hid_used y_psum mixed")
        tokens_in, out_stored = (sems(f"{n}0 {n}1") for n in ("tokens_in", "out_stored"))

        def pair_rows(t, q, i2, c):
            return t[2 * q + i2, ds(c * ROWS, ROWS), :, :].rearrange("r x f -> x r f")

        def by_tile(t, i):
            return t.rearrange("(q a y x) -> q y a x", q=PAIRS, a=2, x=NX)[i]

        starts_runs = starts_d.rearrange("(p c) h -> p c h", p=P)
        state_runs = state_d.rearrange("(p c) f -> p c f", p=P)
        key_rows = keys_d.rearrange("(r k) -> r k", k=LV)
        out_v, x_v = out, x

        def over(row, n, where=1):
            v = row.unsqueeze(where)
            shape = list(v.shape)
            shape[where] = n
            return v.to_broadcast(shape)

        def sort_plan():
            steps, before = LOG_C * (LOG_C - 1) // 2 + 1 + LOG_C, []
            for k in range(LOG_C + 1, LOG_E + 1):
                before.append(steps % 2)
                steps += 1 + k - LOG_C
                before.append(steps % 2)
                steps += 1 + LOG_C
            return before, steps % 2

        key_before, key_at_end = sort_plan()
        sorted_keys = key_bufs[key_at_end]

        def params():
            col = [(bn[:, k:k + 1], v.unsqueeze(1)) for k, v in enumerate((br, gamma, beta, mean, var))]
            return col + [
                (wr[:, :], Wr), (ws[0:CR, :], Ws), (ws[CR:CR + 1, :], bs.unsqueeze(0)), (wi[:, :], Wi),
                (wgat[:, 0:HE], W_gat),
                (att[:, 0], att_src.rearrange("h e -> (h e)").partition_broadcast(P)),
                (att[:, 1], att_dst.rearrange("h e -> (h e)").partition_broadcast(P)),
            ] + [(bi3[j:j + 1, j * C:(j + 1) * C], bi.unsqueeze(0)) for j in range(3)]

        def late_params():
            return ([(gat_p[:, k], v.partition_broadcast(P)) for k, v in enumerate((b_gat, ln_gamma, ln_beta))]
                    + [(w1[:, e], W1[e]) for e in range(EXPERTS)]
                    + [(w2[:, e], W2[e].rearrange("(a p) f -> p a f", a=2)) for e in range(EXPERTS)]
                    + [(b2r[:, :], b2.rearrange("e f -> (e f)").unsqueeze(0))]
                    + [(b1c[:, e], b1[e].rearrange("(a p) -> p a", a=2)) for e in range(EXPERTS)])

        def more(i, n):
            return not isinstance(i, int) or i + n < PAIRS * CHUNKS

        def after(q, c, n):
            if isinstance(c, int) and c + n >= CHUNKS:
                return q + 1, c + n - CHUNKS
            return q, c + n

        def over_chunks(engine, step):
            last = CHUNKS // 2 - 2
            for q in range(PAIRS):
                if q == 0:
                    for u in (0, 1):
                        step(q, 0, u)
                with engine.Fori(1 if q == 0 else 0, last) as c2:
                    for u in (0, 1):
                        step(q, c2, u)
                for c in range(2 * last, CHUNKS):
                    step(q, c // 2, c % 2)

        def halves(ap, g):
            return ap.rearrange("p (h d l) -> p h d l", d=2, l=1 << g)

        block = ctx.enter_context(nc.Block())

        @block.sync
        def _(sp):
            def put(to, of, s):
                sp.dma_start(to, of).then_inc(s, 16)

            put(key_bufs[0].bitcast(I32), edge_index[1].rearrange("(p c) -> p c", p=P), dst_loaded)
            put(key_bufs[1].bitcast(I32), edge_index[0].rearrange("(p c) -> p c", p=P), src_loaded)
            sp.wait_ge(ident_zero, 3)
            with nc.allow_non_contiguous_dma(reason="columns of a few numbers"):
                for to, of in params():
                    put(to, of, params_loaded)

            def load_xa(q, c, u):
                for i2 in (0, 1):
                    put(xa[i2::2, u], pair_rows(x_v, q, i2, c), xa_in[u])

            def load_xb(q, c, u):
                for i2 in (0, 1):
                    put(xb[i2::2, u], pair_rows(x_v, q, i2, c), xb_in[u])

            for u in (0, 1):
                load_xa(0, u, u)
                load_xb(0, u, u)

            sp.wait_ge(keys_final, 1)
            sk = sorted_keys
            put(keys_d[0:EDGES].rearrange("(p c) -> p c", p=P), sk, keys_stored)
            put(keys_d[EDGES:EDGES + COLS].unsqueeze(0), sk[P - 1:P, :], keys_stored)
            with nc.allow_non_contiguous_dma(reason="one key per partition"):
                put(level1_d.unsqueeze(1), sk[:, COLS - 1:COLS], levels_stored)
            put(level2_d, lvl2[:, :], levels_stored)
            sp.wait_ge(levels_stored, 32)
            put(samples[:, :], level1_d.partition_broadcast(P), samples_loaded)

            def step(q, c2, u):
                c, i = 2 * c2 + u, CHUNKS * q + 2 * c2 + u
                turn = CHUNKS // 2 * q + c2
                if more(i, 4):
                    sp.wait_ge(normed1, i + 3)
                    load_xa(*after(q, c, 4), u)
                sp.wait_ge(conv_done, i + 1)
                put(x2_d[ds(i, 1)].squeeze(0), xb[:, u].rearrange("p r f -> p (r f)"), x2_out[u])
                sp.wait_ge(tnT_ready, i + 1)
                put(tnT_d[ds(i, 1)].squeeze(0), tnT[:, u], tnT_out[u])
                if more(i, 2):
                    sp.wait_ge(normed2, i + 1)
                    sp.wait_ge(x2_out[u], 16 * (turn + 1))
                    load_xb(*after(q, c, 2), u)

            for u in (0, 1):
                sp.wait_ge(normed1, u + 1)
                load_xa(0, 2 + u, u)
            over_chunks(sp, step)

            sp.wait_ge(node_ready, PAIRS * CHUNKS)
            for q in range(PAIRS):
                for i2 in (0, 1):
                    b = (2 * q + i2) * NY * NX
                    part_of = node[i2::2, q * NY:(q + 1) * NY]
                    put(node_d[b:b + NY * NX].rearrange("(y x) f -> x y f", x=NX),
                        part_of[:, :, 0:ROW], node_stored)
                    put(adst_d[b:b + NY * NX].rearrange("(y x) f -> x y f", x=NX),
                        part_of[:, :, ROW:NODE], node_stored)
            sp.wait_ge(ranked, 9)
            for k in (0, 1):
                put(ends_d[k, 1:M + 1].rearrange("(p c) -> p c", p=P), ends[:, k], ends_stored)
            put(ends_d[0, 0:1].unsqueeze(0), zero[0:1, 0:1], ends_stored)
            put(ends_d[1, 0:1].unsqueeze(0), ends[P - 1:P, 0, P - 1:P], ends_stored)
            sp.wait_ge(ends_stored, 64)
            put(cnt[:, 0:1], ends_d[0, M:M + 1].partition_broadcast(P), ends_loaded)
            for k, v in enumerate((ends_d[0, 1:M + 1], ends_d[0, 0:M],
                                   ends_d[1, 1:M + 1], ends_d[1, 0:M])):
                for q in range(PAIRS):
                    put(endT[q * NY:(q + 1) * NY, k].rearrange("p (a x) -> p a x", a=2),
                        by_tile(v, q), ends_loaded)
            sp.wait_ge(counted, 1)
            run = sp.value_load(cnti[0:1, 1:2], min_val=2 * T, max_val=COLS)
            steps = sp.value_load(cnti[0:1, 0:1], min_val=1, max_val=COLS // (2 * T))
            for p in range(P):
                put(runs_d[p:p + 1, :], keys_d[ds(run * p, COLS)].unsqueeze(0), runs_stored)
            sp.wait_ge(runs_stored, 16 * P)
            put(runk[:, :], runs_d.bitcast(I32), runk_loaded)
            sp.wait_ge(prev_zero, 1)
            ri = runs_d.bitcast(I32)
            with nc.allow_non_contiguous_dma(reason="one key per run"):
                put(edge_i[:, 0:1], ri[:, 0:1], border_loaded)
                put(edge_i[:, 1:2], ri[:, ds(run - 1, 1)], border_loaded)
                put(edge_i[1:P, 2:3], ri[0:P - 1, ds(run - 1, 1)], border_loaded)
                put(chk[0:1, 0], ri[:, 0:1].rearrange("p a -> a p"), border_loaded)
                put(chk[0:1, 1], ri[:, ds(run - 1, 1)].rearrange("p a -> a p"), border_loaded)
            sp.wait_ge(node_stored, 16 * 8)
            put(last_row[:, :], node_d[M - 1].partition_broadcast(P), late_loaded)
            with nc.allow_non_contiguous_dma(reason="columns of a few numbers"):
                for to, of in late_params():
                    put(to, of, late_loaded)
            sp.wait_ge(adst0_loaded, 16)
            sp.wait_ge(starts_scattered, 16 * TILES)
            put(starts_runs[:, 0], adst0[:, :], first_stored)
            sp.wait_ge(first_stored, 16)

            def edge_step(k):
                for u in (0, 1):
                    if some(k):
                        sp.wait_ge(dch_used[u], k)
                    put(dch[:, u], starts_runs[:, ds((2 * k + u) * T, T)], dch_in[u])
                for u in (0, 1):
                    sp.wait_ge(state_ready, 2 * k + u + 1)
                    put(state_runs[:, ds((2 * k + u) * T, T)], state[:, u, 1:], state_out[u])

            edge_step(0)
            with sp.Fori(1, steps) as k:
                edge_step(k)
            for u in (0, 1):
                sp.wait_ge(state_out[u], 16 * steps)
            put(tails_d, state[:, 1, T], tails_stored)
            sp.wait_ge(tails_stored, 16)
            put(tails, tails_d.unsqueeze(0), tails_loaded)
            sp.wait_ge(chain_ready, 1)
            put(chain_d.unsqueeze(0), chx, chain_stored)
            sp.wait_ge(chain_stored, 16)
            put(cprev[:, :], chain_d[0:P], cprev_loaded)

            for g in (0, 1):
                put(tnT_in[:, g], tnT_d[g], tokens_in[g])
                put(x2_in[:, g], x2_d[g], tokens_in[g])

            def store_step(q, c2, u, more):
                c = 2 * c2 + u
                g = CHUNKS * q + c
                turn = CHUNKS // 2 * q + c2
                sp.wait_ge(mixed, g + 1)
                for i2 in (0, 1):
                    put(pair_rows(out_v, q, i2, c),
                        x2_in[i2::2, u].rearrange("p (r f) -> p r f", f=C),
                        out_stored[u])
                if more:
                    put(tnT_in[:, u], tnT_d[ds(g + 2, 1)].squeeze(0), tokens_in[u])
                    sp.wait_ge(out_stored[u], 32 * (turn + 1))
                    put(x2_in[:, u], x2_d[ds(g + 2, 1)].squeeze(0), tokens_in[u])

            for q in range(PAIRS):
                with sp.Fori(0, CHUNKS // 2 - 1) as c2:
                    for u in (0, 1):
                        store_step(q, c2, u, True)
                for u in (0, 1):
                    store_step(q, CHUNKS // 2 - 1, u, q + 1 < PAIRS)
            for u in (0, 1):
                sp.wait_ge(out_stored[u], 32 * PAIRS * CHUNKS // 2)

        @block.gpsimd
        def _(pool):
            pool.memset(ident[:, :], 0.0).then_inc(ident_zero, 1)
            pool.memset(valid[:, :, :], 1.0).then_inc(ident_zero, 1)
            pool.memset(bi3[:, :], 0.0).then_inc(ident_zero, 1)
            pool.iota(part[:, :], pattern=[[0, 1]], base=0, channel_multiplier=1).then_inc(consts_made, 1)
            for k in (0, 1):
                pool.iota(target[:, k], pattern=[[1, P]], base=1 + KEY_BASE + k * SINK,
                          channel_multiplier=P).then_inc(consts_made, 1)
            pool.wait_ge(ident_zero, 3)
            pool.affine_select(out=ident[:, :], in_=ident[:, :], compare_op=ALU.not_equal, fill=1.0,
                               base=0, pattern=[[-1, P]], channel_multiplier=1).then_inc(consts_made, 1)
            pool.affine_select(out=valid[:, :, :], in_=valid[:, :, :], compare_op=ALU.not_equal,
                               fill=0.0, base=0, pattern=[[1, NX], [0, 2]],
                               channel_multiplier=NX).then_inc(ident_zero, 1)
            pool.wait_ge(ident_zero, 4)
            pool.affine_select(out=valid[:, :, :], in_=valid[:, :, :], compare_op=ALU.not_equal,
                               fill=0.0, base=-(3 * NX - 1), pattern=[[1, NX], [0, 2]],
                               channel_multiplier=NX).then_inc(consts_made, 1)

            pool.memset(found[:, :], 0.0).then_inc(found_zero, 1)
            pool.wait_ge(found_zero, 1)
            for flat in (starts_d, state_d):
                flat = flat.rearrange("(p c) h -> p (c h)", p=P)
                for k in range(0, flat.shape[1], P * LV):
                    pool.dma_start(flat[:, k:k + P * LV], found[:, :]).then_inc(zeros_stored, 16)
            zeros = COLS * (HEADS + ST) // (P * LV)

            def gather(to, table, index, s, bound=None):
                kw = {} if bound is None else dict(bounds_check=bound, oob_is_err=False)
                pool.indirect_dma_start(to, None, table, bass.IndirectOffsetOnAxis(ap=index, axis=0),
                                        **kw).then_inc(s, 16)

            def scatter(table, index, of, s, bound):
                pool.indirect_dma_start(table, bass.IndirectOffsetOnAxis(ap=index, axis=0), of, None,
                                        bounds_check=bound, oob_is_err=False).then_inc(s, 16)

            pool.wait_ge(levels_stored, 32)
            pool.wait_ge(keys_stored, 32)
            for n in range(8):
                level, k, h = n // 4, n // 2 % 2, n % 2
                pool.wait_ge(ranked, max(1, n))
                table, index = (level2_d, row1) if level == 0 else (key_rows, row2)
                for c in range(h * P // 2, (h + 1) * P // 2):
                    gather(found[:, c * LV:(c + 1) * LV], table, index[:, k, c:c + 1], rows_found[h])

            pool.wait_ge(border_ready, 1)
            pool.wait_ge(node_stored, 16 * 8)
            gather(adst0[:, :], adst_d, edge_i[:, 6:7], adst0_loaded)
            gather(endf[:, :], ends_d[0].unsqueeze(1), edge_i[:, 8:9], end_found)
            pool.wait_ge(grid_ready, 1)
            pool.wait_ge(zeros_stored, 16 * zeros)
            for t in range(TILES):
                scatter(starts_d, posi[:, 1, t:t + 1], node[:, t, ROW:NODE], starts_scattered, EDGES - 1)
            pool.wait_ge(sources_ready, 1)
            steps = pool.value_load(cnti[0:1, 0:1], min_val=1, max_val=COLS // (2 * T))

            def edge_gathers(k):
                for u in (0, 1):
                    if some(k):
                        pool.wait_ge(rows_used[u], k)
                    pool.tensor_copy(step_i[:, u], srci[:, ds((2 * k + u) * T, T)])
                    pool.drain()
                    for j in range(T):
                        gather(rows_g[:, u, j], node_d, step_i[:, u, j:j + 1], rows_in[u])

            edge_gathers(0)
            with pool.Fori(1, steps) as k:
                edge_gathers(k)
            pool.wait_ge(end_found, 16)
            pool.wait_ge(fix_placed, 1)
            pool.wait_ge(cprev_loaded, 16)
            gather(fixs[:, :], state_d, edge_i[:, 7:8], fix_got, EDGES - 1)
            pool.wait_ge(fix_ready, 1)
            scatter(state_d, edge_i[:, 7:8], fixo[:, :], fix_stored, EDGES - 1)
            pool.wait_ge(fix_stored, 16)
            pool.wait_ge(agg_cleared, 1)
            for t in range(TILES):
                gather(agg[:, t], state_d, posi[:, 0, t:t + 1], agg_got, EDGES - 1)

        @block.tensor
        def _(pe):
            pe.wait_ge(consts_made, 5)
            for n in range(2 * (LOG_E - LOG_C)):
                pe.wait_ge(phase_sorted, n + 1)
                src = key_bufs[key_before[n]]
                for b in range(8):
                    for m in range(4):
                        last = pe.transpose(bank[b][:, m * P:(m + 1) * P],
                                            src[:, (4 * b + m) * P:(4 * b + m + 1) * P], ident[:, :])
                    last.then_inc(flipped, 1)

            pe.wait_ge(params_loaded, 16 * len(params()))
            pe.wait_ge(bn_ready, 2)

            def turn_conv(i, u):
                pe.wait_ge(normed1, i + 1)
                if some(i):
                    pe.wait_ge(xnT_ready, i)
                for r in range(ROWS):
                    last = pe.transpose(bank[0][:, r * P:(r + 1) * P], xn[:, u, r], ident[:, :])
                last.then_inc(turned1, 1)

            def conv_products(i, u):
                pe.wait_ge(xnT_ready, i + 1)
                if some(i):
                    pe.wait_ge(rT_ready, i)
                pe.matmul(bank[1][0:CR, :], wr[:, :], xnT[:, u, :, 2:P + 2],
                          start=TR, stop=TR).then_inc(r_psum, 1)
                for r in range(ROWS):
                    po = bank[4 + r % 2]
                    if some(ROWS * i + r - 1):
                        pe.wait_ge(xi_ready, ROWS * i + r - 1)
                    pe.matmul(po[:, 0:3 * C], valid[:, :, :].rearrange("p x a -> p (x a)"), bi3[:, :], start=TR, stop=FA)
                    for j in range(3):
                        last = pe.matmul(po[:, j * C:(j + 1) * C], xnT[:, u, r, 2 * j:2 * j + P], wi[:, :],
                                         start=FA, stop=j == 2)
                    last.then_inc(xi_psum, 1)
                pe.wait_ge(rT_ready, i + 1)
                if some(i):
                    pe.wait_ge(w_ready, i)
                for r in range(ROWS):
                    po = bank[2 + r // 2][:, r % 2 * KK * GROUPS:(r % 2 + 1) * KK * GROUPS]
                    last = pe.matmul(po, rT[:, u, r * P:(r + 1) * P], ws[:, :], start=TR, stop=TR)
                last.then_inc(w_psum, 1)

            def turn_tokens(i):
                pe.wait_ge(normed2, i + 1)
                if some(i):
                    pe.wait_ge(tnT_ready, i)
                for r in range(ROWS):
                    last = pe.transpose(bank[6][:, r * P:(r + 1) * P], tn[:, r], ident[:, :])
                last.then_inc(turned2, 1)

            def node_products(i, u):
                pe.wait_ge(tnT_ready, i + 1)
                if some(i):
                    pe.wait_ge(node_ready, i)
                for r in range(ROWS):
                    last = pe.matmul(bank[7][:, r * NODE:(r + 1) * NODE], tnT[:, u, r * P:(r + 1) * P],
                                     wgat[:, :], start=TR, stop=TR)
                last.then_inc(node_psum, 1)

            def chunk_products(q, c2, u):
                i = CHUNKS * q + 2 * c2 + u
                if some(i):
                    turn_tokens(i - 1)
                if more(i, 2):
                    turn_conv(i + 2, u)
                if some(i):
                    node_products(i - 1, 1 - u)
                if more(i, 2):
                    conv_products(i + 2, u)

            for u in (0, 1):
                turn_conv(u, u)
                conv_products(u, u)
            over_chunks(pe, chunk_products)
            turn_tokens(PAIRS * CHUNKS - 1)
            node_products(PAIRS * CHUNKS - 1, 1)

            pe.wait_ge(ends_ordered, 1)
            for k in range(4):
                last = pe.transpose(bank[0][:, k * P:(k + 1) * P], endO[:, k], ident[:, :])
            last.then_inc(ends_turned, 1)

            pe.wait_ge(late_loaded, 16 * (1 + len(late_params())))
            pe.wait_ge(gates_ready, 1)

            def experts(g, u, turn):
                pe.wait_ge(tokens_in[u], 32 * (turn + 1))
                for e in range(EXPERTS):
                    for a in (0, 1):
                        n = 2 * e + a
                        if some(8 * g + n - 3):
                            pe.wait_ge(hid_ready, 8 * g + n - 3)
                        pe.matmul(bank[n % 4][:, :], w1[:, e, a * P:(a + 1) * P], tnT_in[:, u],
                                  start=TR, stop=TR).then_inc(hid_psum, 1)
                pe.wait_ge(hid_ready, 8 * g + 8)
                for r in range(ROWS):
                    if some(g):
                        pe.wait_ge(mixed, g)
                    po = bank[4 + r]
                    pe.matmul(po[:, :], ones[:, :], b2r[:, :], start=TR, stop=FA)
                    for e in range(EXPERTS):
                        for a in (0, 1):
                            last = pe.matmul(po[:, e * C:(e + 1) * C],
                                             hid[u][:, 2 * e + a, r * P:(r + 1) * P], w2[:, e, a],
                                             start=FA, stop=e == EXPERTS - 1 and a == 1)
                    last.then_inc(y_psum, 1)

            experts(0, 0, 0)
            experts(1, 1, 0)
            with pe.Fori(1, PAIRS * CHUNKS // 2) as g2:
                for u in (0, 1):
                    experts(2 * g2 + u, u, g2)

        @block.scalar
        def _(act):
            act.wait_ge(params_loaded, 16 * len(params()))
            act.wait_ge(small_ready, 1)
            act.activation(bn[:, 5:6], bn[:, 4:5], ACT.Sqrt, bias=eps[0:CR, 2:3]).then_inc(bn_root, 1)
            n = 0
            for k in range(LOG_C + 1, LOG_E + 1):
                for way in (0, 1):
                    to = key_bufs[1 - key_before[n]]
                    for b in range(0, 8, 2):
                        act.wait_ge(flipped, 8 * n + b + 1)
                        blk = to[:, b * 512:(b + 1) * 512]
                        if way == 0:
                            for d in (0, 1):
                                last = act.activation(halves(blk, k - 1 - LOG_C)[:, :, d],
                                                      halves(bank[b][:, :], k - 1 - LOG_C)[:, :, d],
                                                      ACT.Copy, scale=1.0 - 2 * d)
                            last.then_inc(act_placed, 1)
                        elif k < LOG_E:
                            act.activation(blk, bank[b][:, :], ACT.Copy,
                                           scale=signs[:, k - LOG_C:k - LOG_C + 1]).then_inc(act_placed, 1)
                        else:
                            act.activation(blk, bank[b][:, :], ACT.Copy).then_inc(act_placed, 1)
                    n += 1

            act.wait_ge(bn_ready, 2)

            def first_root(i):
                act.wait_ge(stats1, i + 1)
                act.activation(sd[:, 0], mv[:, 0, :, 1], ACT.Sqrt, bias=eps[:, 0:1]).then_inc(root1, 1)

            def take_conv(i, u):
                act.wait_ge(turned1, i + 1)
                if some(i - 1):
                    act.wait_ge(w_psum, i - 1)
                act.activation(xnT[:, u, :, 2:P + 2], bank[0][:, :].rearrange("p (r t) -> p r t", t=P),
                               ACT.Copy).then_inc(xnT_ready, 1)

            def conv_copies(q, c, u, ahead):
                i = CHUNKS * q + c
                act.wait_ge(r_psum, i + 1)
                act.activation(rT[0:CR, u], bank[1][0:CR, :], ACT.Relu, bias=bn[:, 6:7],
                               scale=bn[:, 5:6]).then_inc(rT_ready, 1)
                for r in range(ROWS):
                    act.wait_ge(xi_psum, ROWS * i + r + 1)
                    if q:
                        act.wait_ge(conv_done, CHUNKS * (q - 1) + c + 2)
                    act.activation(xi[:, ds((ROWS * c + r + 1) * 3 * C, 3 * C)],
                                   bank[4 + r % 2][:, 0:3 * C], ACT.Copy).then_inc(xi_ready, 1)
                if ahead:
                    first_root(i + 1)
                act.wait_ge(w_psum, i + 1)
                if some(i - 1):
                    act.wait_ge(conv_done, i - 1)
                for b in (0, 1):
                    last = act.activation(wv[:, u, 2 * b:2 * b + 2].rearrange("p r k -> p (r k)"),
                                          bank[2 + b][:, 0:2 * KK * GROUPS], ACT.Copy)
                last.then_inc(w_ready, 1)

            def take_tokens(i, u, turn):
                act.wait_ge(conv_done, i + 1)
                act.activation(sd[:, 1], mv[:, 1, :, 1], ACT.Sqrt, bias=eps[:, 1:2]).then_inc(root2, 1)
                act.wait_ge(turned2, i + 1)
                if some(i - 1):
                    act.wait_ge(node_psum, i - 1)
                if some(turn):
                    act.wait_ge(tnT_out[u], 16 * turn)
                act.activation(tnT[:, u], bank[6][:, :], ACT.Copy).then_inc(tnT_ready, 1)

            def node_copies(i):
                act.wait_ge(node_psum, i + 1)
                act.activation(node[:, ds(ROWS * i, ROWS)].rearrange("p r f -> p (r f)"),
                               bank[7][:, 0:ROWS * NODE], ACT.Copy).then_inc(node_ready, 1)

            def chunk_copies(q, c2, u):
                c, i, turn = 2 * c2 + u, CHUNKS * q + 2 * c2 + u, CHUNKS // 2 * q + c2
                if some(i):
                    take_tokens(i - 1, 1 - u, turn if u else turn - 1)
                if more(i, 2):
                    take_conv(i + 2, u)
                if some(i):
                    node_copies(i - 1)
                if more(i, 2):
                    conv_copies(*after(q, c, 2), u, more(i, 3))

            first_root(0)
            first_root(1)
            for u in (0, 1):
                take_conv(u, u)
                conv_copies(0, u, u, u == 1)
            over_chunks(act, chunk_copies)
            take_tokens(PAIRS * CHUNKS - 1, 1, PAIRS * CHUNKS // 2 - 1)
            node_copies(PAIRS * CHUNKS - 1)

            act.wait_ge(counted, 1)
            steps = act.value_load(cnti[0:1, 0:1], min_val=1, max_val=COLS // (2 * T))
            with act.Fori(0, steps) as k:
                for u in (0, 1):
                    act.wait_ge(scored, 2 * k + u + 1)
                    act.activation(ex[:, :, :, :], ex[:, :, :, :], ACT.Exp).then_inc(weighed, 1)
            act.wait_ge(chain_scored, 1)
            act.activation(che, che, ACT.Exp).then_inc(chain_weighed, 1)
            act.wait_ge(fix_scored, 1)
            act.activation(fixe[:, :, :], fixe[:, :, :], ACT.Exp).then_inc(fix_weighed, 1)
            act.wait_ge(joined, 1)
            act.activation(hx[:, 0:3], hx[:, 0:3], ACT.Exp).then_inc(join_weighed, 1)
            act.wait_ge(agg_var, 1)
            act.activation(one4[:, 1], one4[:, 0], ACT.Sqrt, bias=eps[:, 1:2]).then_inc(agg_root, 1)
            act.wait_ge(top_ready, 1)
            act.activation(one4[:, 1], one4[:, 0], ACT.Exp).then_inc(top_weighed, 1)

            act.wait_ge(late_loaded, 16 * (1 + len(late_params())))

            def gelus(g, u):
                for n in range(8):
                    act.wait_ge(hid_psum, 8 * g + n + 1)
                    if n == 0 and some(g - 1):
                        act.wait_ge(y_psum, 4 * (g - 1))
                    act.activation(hid[u][:, n], bank[n % 4][:, :], ACT.Gelu,
                                   bias=b1c[:, n // 2, n % 2:n % 2 + 1]).then_inc(hid_ready, 1)

            gelus(0, 0)
            gelus(1, 1)
            with act.Fori(1, PAIRS * CHUNKS // 2) as g2:
                for u in (0, 1):
                    gelus(2 * g2 + u, u)

        @block.vector
        def _(dve):
            flush = dve.drain

            dve.wait_ge(consts_made, 5)
            for k in range(LOG_E - LOG_C):
                dve.tensor_scalar(sign_i[:, k:k + 1], part[:, :], k, 1,
                                  ALU.logical_shift_right, ALU.bitwise_and)
            dve.tensor_copy(partf[:, :], part[:, :])
            for k, v in enumerate((1e-6, 1e-5, 1e-3)):
                dve.memset(eps[:, k:k + 1], v)
            dve.memset(zero[:, :], 0.0)
            for k in (0, 1):
                dve.tensor_scalar(target[:, k], target[:, k], SRC_BITS, None, ALU.logical_shift_left)
            flush()
            dve.tensor_scalar(signs[:, :], sign_i[:, :], -2.0, 1.0, ALU.mult, ALU.add).then_inc(small_ready, 1)

            dve.wait_ge(dst_loaded, 16)
            dve.wait_ge(src_loaded, 16)
            dst, src = key_bufs[0].bitcast(I32), key_bufs[1].bitcast(I32)
            cls, gone = tmp_a.bitcast(I32), tmp_b.bitcast(I32)
            dve.tensor_scalar(src, src, 0, M - 1, ALU.max, ALU.min)
            dve.tensor_scalar(gone, dst, M, DROPPED, ALU.is_ge, ALU.mult)
            flush()
            dve.tensor_scalar(dst, dst, M, None, ALU.min)
            dve.tensor_scalar(cls, src, M - 1, SINK, ALU.is_ge, ALU.mult)
            flush()
            dve.scalar_tensor_tensor(out=dst, in0=dst, scalar=KEY_BASE, in1=cls, op0=ALU.add, op1=ALU.add)
            flush()
            dve.tensor_tensor(dst, dst, gone, ALU.max)
            flush()
            dve.tensor_scalar(dst, dst, SRC_BITS, None, ALU.logical_shift_left)
            flush()
            dve.tensor_tensor(dst, dst, src, ALU.bitwise_or)
            flush()
            bufs = list(key_bufs)

            def compare(cmp_bit, dir_bit):
                a, b = bufs
                if dir_bit is None:
                    va, vb = halves(a, cmp_bit), halves(b, cmp_bit)
                    dve.tensor_tensor(vb[:, :, 0], va[:, :, 0], va[:, :, 1], ALU.min)
                    last = dve.tensor_tensor(vb[:, :, 1], va[:, :, 0], va[:, :, 1], ALU.max)
                else:
                    cut = dict(d=2, m=1 << (dir_bit - 1 - cmp_bit), c=2, l=1 << cmp_bit)
                    va, vb = (z.rearrange("p (h d m c l) -> p h d m c l", **cut) for z in (a, b))
                    for d in (0, 1):
                        for c in (0, 1):
                            last = dve.tensor_tensor(vb[:, :, d, :, c], va[:, :, d, :, 0], va[:, :, d, :, 1],
                                                     ALU.min if c == d else ALU.max)
                bufs.reverse()
                return last

            for k in range(1, LOG_C):
                for j in reversed(range(k)):
                    compare(j, k)
                    flush()
            dve.tensor_scalar(bufs[1], bufs[0], signs[:, 0:1], None, ALU.mult)
            bufs.reverse()
            flush()
            for j in reversed(range(LOG_C)):
                last = compare(j, None)
                if j:
                    flush()
            n = 0
            for k in range(LOG_C + 1, LOG_E + 1):
                for way in (0, 1):
                    assert bufs[0] is key_bufs[key_before[n]]
                    last.then_inc(phase_sorted, 1)
                    for b in range(1, 8, 2):
                        dve.wait_ge(flipped, 8 * n + b + 1)
                        blk = bufs[1][:, b * 512:(b + 1) * 512]
                        if way == 0:
                            for d in (0, 1):
                                dve.tensor_scalar(halves(blk, k - 1 - LOG_C)[:, :, d],
                                                  halves(bank[b][:, :], k - 1 - LOG_C)[:, :, d],
                                                  1.0 - 2 * d, None, ALU.mult)
                        elif k < LOG_E:
                            dve.tensor_scalar(blk, bank[b][:, :], signs[:, k - LOG_C:k - LOG_C + 1],
                                              None, ALU.mult)
                        else:
                            dve.tensor_copy(blk, bank[b][:, :])
                    n += 1
                    bufs.reverse()
                    dve.wait_ge(act_placed, 4 * n)
                    flush()
                    if way == 0:
                        for j in reversed(range(LOG_C, k)):
                            last = compare(j - LOG_C, k - LOG_C if k < LOG_E else None)
                            if j > LOG_C:
                                flush()
                    else:
                        for j in reversed(range(LOG_C)):
                            last = compare(j, None)
                            if j:
                                flush()
            assert bufs[0] is sorted_keys
            flush()
            dve.tensor_copy(lvl2[:, :], sorted_keys[:, LV - 1:COLS:LV]).then_inc(keys_final, 1)

            dve.wait_ge(params_loaded, 16 * len(params()))
            for k in (0, 1):
                dve.tensor_tensor(prod[:, k, 0:HE], att[:, k], wgat[:, 0:HE], ALU.mult)
            dve.wait_ge(bn_root, 1)
            dve.reciprocal(bn[:, 5:6], bn[:, 5:6])
            flush()
            for k in (0, 1):
                dve.tensor_reduce(wgat[:, HE + k * HEADS:HE + (k + 1) * HEADS],
                                  prod[:, k, 0:HE].rearrange("p (h e) -> p h e", e=EXPERTS), AX.X, ALU.add)
            dve.tensor_tensor(bn[:, 5:6], bn[:, 5:6], bn[:, 1:2], ALU.mult)
            dve.tensor_tensor(bn[:, 6:7], bn[:, 0:1], bn[:, 3:4], ALU.subtract)
            flush()
            dve.tensor_tensor(bn[:, 6:7], bn[:, 6:7], bn[:, 5:6], ALU.mult)
            flush()
            dve.tensor_tensor(bn[:, 6:7], bn[:, 6:7], bn[:, 2:3], ALU.add).then_inc(bn_ready, 1)

            dve.wait_ge(samples_loaded, 16)
            dve.wait_ge(zeros_stored, 16 * (COLS * (HEADS + ST) // (P * LV)))
            half = P * LV // P
            for k in (0, 1):
                tg = target[:, k].bitcast(F32)
                for s in range(P // half):
                    v = found[:, :].rearrange("p (c s) -> p c s", s=P)
                    dve.tensor_tensor(v, over(samples[:, :], half), over(tg[:, s * half:(s + 1) * half], P, 2),
                                      ALU.is_lt)
                    flush()
                    dve.tensor_reduce(rank1[:, k, s * half:(s + 1) * half], v, AX.X, ALU.add)
                    flush()
            dve.tensor_scalar(rank1[:, :], rank1[:, :], float(P - 1), None, ALU.min)
            flush()
            dve.tensor_copy(row1[:, :], rank1[:, :]).then_inc(ranked, 1)

            def rank(n):
                level, k, h = n // 4, n // 2 % 2, n % 2
                cols = slice(h * P // 2, (h + 1) * P // 2)
                tg = target[:, k, cols].bitcast(F32)
                v = found[:, h * P // 2 * LV:(h + 1) * P // 2 * LV].rearrange("p (c s) -> p c s", s=LV)
                dve.wait_ge(rows_found[h], 16 * P // 2 * (n // 2 + 1))
                dve.tensor_tensor(v, v, over(tg, LV, 2), ALU.is_lt)
                flush()
                dve.tensor_reduce(rank2[:, k, cols], v, AX.X, ALU.add)
                flush()
                if level == 0:
                    dve.tensor_scalar(rank2[:, k, cols], rank2[:, k, cols], float(LV - 1), None, ALU.min)
                    flush()
                    dve.scalar_tensor_tensor(out=rank1[:, k, cols], in0=rank1[:, k, cols], scalar=float(LV),
                                             in1=rank2[:, k, cols], op0=ALU.mult, op1=ALU.add)
                    flush()
                    dve.tensor_copy(row2[:, k, cols], rank1[:, k, cols]).then_inc(ranked, 1)
                else:
                    dve.scalar_tensor_tensor(out=ends[:, k, cols], in0=rank1[:, k, cols], scalar=float(LV),
                                             in1=rank2[:, k, cols], op0=ALU.mult, op1=ALU.add).then_inc(ranked, 1)

            dve.wait_ge(keys_stored, 32)
            dve.wait_ge(levels_stored, 32)
            dve.memset(xi[:, 0:3 * C], 0.0)
            dve.memset(xi[:, (NY + 1) * 3 * C:], 0.0)
            for side in (0, P + 2):
                dve.memset(xnT[:, :, :, side:side + 2], 0.0)
            dve.memset(rT[CR:CR + 1], 1.0).then_inc(bn_ready, 1)
            flush()

            def statistics(k, rows, done):
                for r in range(ROWS):
                    dve.bn_stats(stats[:, k, r], rows(r))
                flush()
                for r in range(ROWS):
                    last = dve.bn_aggr(mv[:, k, r], stats[:, k, r])
                last.then_inc(done, 1)

            def first_stats(i, u, turn):
                dve.wait_ge(xa_in[u], 32 * (turn + 1))
                statistics(0, lambda r: xa[:, u, r], stats1)

            def first_norm(i, u):
                dve.wait_ge(root1, i + 1)
                dve.reciprocal(rstd[:, 0], sd[:, 0])
                flush()
                if some(i - 1):
                    dve.wait_ge(turned1, i - 1)
                for r in range(ROWS):
                    last = dve.tensor_scalar(xn[:, u, r], xa[:, u, r], mv[:, 0, r, 0:1],
                                             rstd[:, 0, r:r + 1], ALU.subtract, ALU.mult)
                last.then_inc(normed1, 1)

            def involve(c, u, r):
                patch = xi[:, ds((ROWS * c + r) * 3 * C, TAPS)]
                dve.tensor_tensor(prod[:, r % 2].rearrange("p (g f k) -> p g f k", g=GROUPS, k=KK),
                                  patch.rearrange("p (g f k) -> p g f k", g=GROUPS, k=KK),
                                  over(wv[:, u, r].rearrange("p (g k) -> p g k", k=KK), C // GROUPS, 2),
                                  ALU.mult)
                flush()
                dve.tensor_reduce(inv[:, r], prod[:, r % 2].rearrange("p (o k) -> p o k", k=KK),
                                  AX.X, ALU.add)

            def second_norm(i, u):
                dve.wait_ge(root2, i + 1)
                dve.reciprocal(rstd[:, 1], sd[:, 1])
                flush()
                if some(i):
                    dve.wait_ge(turned2, i)
                for r in range(ROWS):
                    last = dve.tensor_scalar(tn[:, r], xb[:, u, r], mv[:, 1, r, 0:1],
                                             rstd[:, 1, r:r + 1], ALU.subtract, ALU.mult)
                last.then_inc(normed2, 1)

            def conv_step(q, c2, u):
                c, i, turn = 2 * c2 + u, CHUNKS * q + 2 * c2 + u, CHUNKS // 2 * q + c2
                dve.wait_ge(xi_ready, ROWS * (i + 1) + (1 if more(i, 1) else 0))
                dve.wait_ge(w_ready, i + 1)
                involve(c, u, 0)
                if some(i):
                    second_norm(i - 1, 1 - u)
                if more(i, 2):
                    first_norm(i + 2, u)
                if more(i, 3):
                    first_stats(i + 3, 1 - u, turn + 1 + u)
                for r in range(1, ROWS):
                    involve(c, u, r)
                flush()
                dve.wait_ge(xb_in[u], 32 * (turn + 1))
                dve.tensor_tensor(xb[:, u], xb[:, u], inv[:, :], ALU.add)
                flush()
                statistics(1, lambda r: xb[:, u, r], conv_done)

            for u in (0, 1):
                first_stats(u, u, 0)
                first_norm(u, u)
            first_stats(2, 0, 1)
            for u in (0, 1):
                conv_step(0, 0, u)
            for n in range(4 * 2):
                q, c0 = n // 4, n % 4 * (CHUNKS // 8)
                if n < 7:
                    with dve.Fori(max(c0, 1 if q == 0 else 0), c0 + CHUNKS // 8) as c2:
                        for u in (0, 1):
                            conv_step(q, c2, u)
                else:
                    for c in range(2 * c0, CHUNKS):
                        conv_step(q, c // 2, c % 2)
                    second_norm(PAIRS * CHUNKS - 1, 1)
                rank(n)

            dve.memset(edge_i[:, 2:3], 0).then_inc(prev_zero, 1)
            dve.wait_ge(ends_loaded, 16 * 9)
            for k in range(4):
                last = dve.tensor_copy(endO[:, k].rearrange("p (x a) -> p a x", a=2),
                                       endT[:, k].rearrange("p (a x) -> p a x", a=2))
            last.then_inc(ends_ordered, 1)
            per_step = float(2 * T * P)

            def c_(k):
                return cnt[:, k:k + 1]

            dve.tensor_scalar(cnti[:, 0:1], c_(0), 1.0 / per_step, None, ALU.mult)
            flush()
            dve.tensor_copy(c_(2), cnti[:, 0:1])
            flush()
            dve.scalar_tensor_tensor(out=c_(3), in0=c_(2), scalar=per_step, in1=c_(0), op0=ALU.mult, op1=ALU.is_lt)
            flush()
            dve.tensor_tensor(c_(2), c_(2), c_(3), ALU.add)
            flush()
            dve.tensor_scalar(c_(4), c_(2), 1.0, per_step, ALU.subtract, ALU.mult)
            flush()
            dve.tensor_tensor(c_(3), c_(4), c_(0), ALU.is_ge)
            flush()
            dve.tensor_tensor(c_(2), c_(2), c_(3), ALU.subtract)
            flush()
            dve.tensor_scalar(c_(2), c_(2), 1.0, None, ALU.max)
            flush()
            dve.tensor_scalar(c_(4), c_(2), float(2 * T), None, ALU.mult)
            flush()
            dve.tensor_scalar(c_(5), c_(4), -1.0, float(COLS), ALU.mult, ALU.add)
            dve.reciprocal(c_(6), c_(4))
            dve.tensor_copy(cnti[:, 0:1], c_(2))
            dve.tensor_copy(cnti[:, 1:2], c_(4)).then_inc(counted, 1)
            dve.wait_ge(ends_turned, 1)
            dve.tensor_copy(endG[:, :, :].rearrange("p k t -> p (k t)"), bank[0][:, :])
            flush()
            dve.tensor_tensor(nonempty[:, 0], endG[:, 0], endG[:, 1], ALU.is_gt)
            dve.tensor_scalar(pos[:, 0], endG[:, 0], 1.0, None, ALU.subtract)
            dve.tensor_copy(pos[:, 1], endG[:, 1])
            flush()
            dve.tensor_scalar(quoi[:, :], pos[:, :], c_(6), None, ALU.mult)
            flush()
            dve.tensor_copy(quo[:, :], quoi[:, :])
            flush()
            dve.scalar_tensor_tensor(out=fit[:, :], in0=quo[:, :], scalar=c_(4), in1=pos[:, :], op0=ALU.mult, op1=ALU.is_gt)
            flush()
            dve.tensor_tensor(quo[:, :], quo[:, :], fit[:, :], ALU.subtract)
            flush()
            dve.tensor_scalar(fit[:, :], quo[:, :], 1.0, c_(4), ALU.add, ALU.mult)
            flush()
            dve.tensor_tensor(fit[:, :], fit[:, :], pos[:, :], ALU.is_le)
            flush()
            dve.tensor_tensor(quo[:, :], quo[:, :], fit[:, :], ALU.add)
            flush()
            dve.scalar_tensor_tensor(out=pos[:, :], in0=quo[:, :], scalar=c_(5), in1=pos[:, :], op0=ALU.mult, op1=ALU.add)
            flush()
            dve.scalar_tensor_tensor(out=pos[:, :], in0=pos[:, :], scalar=-SKIP,
                                     in1=over(nonempty[:, 0], 2), op0=ALU.add, op1=ALU.mult)
            flush()
            dve.tensor_scalar(posi[:, :], pos[:, :], SKIP, None, ALU.add).then_inc(grid_ready, 1)

            dve.wait_ge(border_loaded, 16 * 5)
            dve.tensor_scalar(edge_i[:, 3:6], edge_i[:, 0:3], SRC_BITS, None, ALU.logical_shift_right)
            dve.tensor_scalar(chk[:, :], chk[:, :], SRC_BITS, None, ALU.logical_shift_right)
            flush()

            def e_(k):
                return edge_f[:, k:k + 1]

            dve.tensor_scalar(edge_f[:, 0:3], edge_i[:, 3:6], float(-KEY_BASE), None, ALU.add)
            dve.tensor_copy(chf[:, 0:2], chk[:, :])
            flush()
            dve.tensor_scalar(edge_i[:, 8:9], e_(0), 1.0, float(M), ALU.add, ALU.min)
            dve.tensor_scalar(edge_i[:, 6:7], e_(0), float(M - 1), None, ALU.min).then_inc(border_ready, 1)
            dve.wait_ge(runk_loaded, 16)
            dve.tensor_scalar(srci[:, :], runk[:, :], M - 1, None, ALU.bitwise_and).then_inc(sources_ready, 1)
            dve.tensor_scalar(clsi[:, :], runk[:, :], SRC_BITS, None, ALU.logical_shift_right)
            flush()
            dve.memset(same[:, 0:1], 0.0)
            dve.memset(ones[:, :], 1.0)
            dve.tensor_tensor(same[:, 1:], clsi[:, 1:], clsi[:, :COLS - 1], ALU.is_equal)
            flush()
            dve.tensor_scalar(reset[:, :], same[:, :], -1.0, BIG, ALU.add, ALU.mult)
            dve.memset(df[:, T], 0.0)
            dve.memset(state[:, 1, T, 0:HEADS], -BIG)
            dve.memset(state[:, 1, T, HEADS:ST], 0.0)
            flush()

            steps = dve.value_load(cnti[0:1, 0:1], min_val=1, max_val=COLS // (2 * T))

            def edge_scans(k):
                for u in (0, 1):
                    col = (2 * k + u) * T
                    dve.tensor_copy(df[:, 0], df[:, T])
                    if some(k):
                        dve.wait_ge(state_out[u], 16 * k)
                    dve.tensor_copy(state[:, u, 0], state[:, 1 - u, T])
                    flush()
                    dve.wait_ge(dch_in[u], 16 * (k + 1))
                    for h in range(HEADS):
                        last = dve.tensor_tensor_scan(df[:, 1:, h], same[:, ds(col, T)], dch[:, u, :, h],
                                                      df[:, 0, h:h + 1], ALU.mult, ALU.add)
                    last.then_inc(dch_used[u], 1)
                    flush()
                    dve.wait_ge(rows_in[u], 16 * T * (k + 1))
                    dve.tensor_tensor(score[:, :, :], rows_g[:, u, :, HE:ROW], df[:, 1:], ALU.add)
                    flush()
                    dve.scalar_tensor_tensor(out=score[:, :, :], in0=score[:, :, :], scalar=0.2,
                                             in1=score[:, :, :], op0=ALU.mult, op1=ALU.max)
                    flush()
                    for h in range(HEADS):
                        dve.tensor_tensor_scan(state[:, u, 1:, h], reset[:, ds(col, T)], score[:, :, h],
                                               state[:, u, 0, h:h + 1], ALU.add, ALU.max)
                    flush()
                    dve.tensor_tensor(ex[:, :, 0], state[:, u, 0:T, 0:HEADS], state[:, u, 1:, 0:HEADS], ALU.subtract)
                    dve.tensor_tensor(ex[:, :, 1], score[:, :, :], state[:, u, 1:, 0:HEADS], ALU.subtract)
                    flush()
                    dve.tensor_tensor(ex[:, :, 0], ex[:, :, 0], over(reset[:, ds(col, T)], HEADS, 2),
                                      ALU.add).then_inc(scored, 1)
                    dve.wait_ge(weighed, 2 * k + u + 1)
                    dve.tensor_tensor(pv[:, :, :].rearrange("p t (h e) -> p t h e", e=EXPERTS),
                                      rows_g[:, u, :, 0:HE].rearrange("p t (h e) -> p t h e", e=EXPERTS),
                                      over(ex[:, :, 1], EXPERTS, 3), ALU.mult).then_inc(rows_used[u], 1)
                    flush()
                    for h in range(HEADS):
                        for e in range(-1, EXPERTS):
                            f = HEADS + h if e < 0 else 2 * HEADS + EXPERTS * h + e
                            new = ex[:, :, 1, h] if e < 0 else pv[:, :, EXPERTS * h + e]
                            last = dve.tensor_tensor_scan(state[:, u, 1:, f], ex[:, :, 0, h], new,
                                                          state[:, u, 0, f:f + 1], ALU.mult, ALU.add)
                    last.then_inc(state_ready, 1)
                    flush()

            edge_scans(0)
            with dve.Fori(1, steps) as k:
                edge_scans(k)

            dve.tensor_tensor(chf[:, 2], chf[:, 0], chf[:, 1], ALU.is_equal)
            dve.memset(chf[:, 3, 0:1], 0.0)
            dve.tensor_tensor(chf[:, 3, 1:], chf[:, 0, 1:], chf[:, 1, :P - 1], ALU.is_equal)
            flush()
            dve.tensor_tensor(chf[:, 2], chf[:, 2], chf[:, 3], ALU.mult)
            flush()
            dve.tensor_scalar(chf[:, 4], chf[:, 2], -1.0, BIG, ALU.add, ALU.mult)
            dve.wait_ge(tails_loaded, 16)
            dve.memset(chx[:, 0, 0:HEADS], -BIG)
            dve.memset(chx[:, 0, HEADS:ST], 0.0)
            flush()
            for h in range(HEADS):
                dve.tensor_tensor_scan(chx[:, 1:, h], chf[:, 4], tails[:, :, h], chx[:, 0, h:h + 1],
                                       ALU.add, ALU.max)
            flush()
            dve.tensor_tensor(che[:, :, 0], chx[:, 0:P, 0:HEADS], chx[:, 1:, 0:HEADS], ALU.subtract)
            dve.tensor_tensor(che[:, :, 1], tails[:, :, 0:HEADS], chx[:, 1:, 0:HEADS], ALU.subtract)
            flush()
            dve.tensor_tensor(che[:, :, 0], che[:, :, 0], over(chf[:, 4], HEADS, 2), ALU.add).then_inc(chain_scored, 1)
            dve.wait_ge(chain_weighed, 1)
            dve.tensor_tensor(chp[:, :, 0:HEADS], tails[:, :, HEADS:2 * HEADS], che[:, :, 1], ALU.mult)
            dve.tensor_tensor(chp[:, :, HEADS:].rearrange("p t (h e) -> p t h e", e=EXPERTS),
                              tails[:, :, 2 * HEADS:].rearrange("p t (h e) -> p t h e", e=EXPERTS),
                              over(che[:, :, 1], EXPERTS, 3), ALU.mult)
            flush()
            for h in range(HEADS):
                for e in range(-1, EXPERTS):
                    f = HEADS + h if e < 0 else 2 * HEADS + EXPERTS * h + e
                    last = dve.tensor_tensor_scan(chx[:, 1:, f], che[:, :, 0, h], chp[:, :, f - HEADS],
                                                  chx[:, 0, f:f + 1], ALU.mult, ALU.add)
            last.then_inc(chain_ready, 1)

            dve.memset(fixs[:, :], 0.0)
            dve.wait_ge(end_found, 16)
            dve.tensor_scalar(e_(3), endf[:, :], 1.0, None, ALU.subtract)
            dve.tensor_tensor(e_(4), e_(0), e_(2), ALU.is_equal)
            dve.tensor_scalar(e_(5), e_(0), float(M), None, ALU.is_lt)
            dve.tensor_scalar(e_(6), partf[:, :], 1.0, c_(4), ALU.add, ALU.mult)
            dve.tensor_scalar(e_(7), partf[:, :], c_(5), None, ALU.mult)
            flush()
            dve.tensor_tensor(e_(4), e_(4), e_(5), ALU.mult)
            dve.tensor_tensor(e_(6), e_(3), e_(6), ALU.is_lt)
            dve.scalar_tensor_tensor(out=e_(7), in0=e_(3), scalar=-SKIP, in1=e_(7), op0=ALU.add, op1=ALU.add)
            flush()
            dve.tensor_tensor(e_(4), e_(4), e_(6), ALU.mult)
            flush()
            dve.tensor_tensor(e_(7), e_(7), e_(4), ALU.mult)
            flush()
            dve.tensor_scalar(edge_i[:, 7:8], e_(7), SKIP, None, ALU.add).then_inc(fix_placed, 1)
            dve.memset(agg[:, :, 0:HEADS], -BIG)
            dve.memset(agg[:, :, HEADS:ST], 0.0).then_inc(agg_cleared, 1)
            dve.wait_ge(fix_got, 16)
            dve.wait_ge(cprev_loaded, 16)
            dve.tensor_tensor(fixo[:, 0:HEADS], cprev[:, 0:HEADS], fixs[:, 0:HEADS], ALU.max)
            flush()
            dve.tensor_tensor(fixe[:, 0], cprev[:, 0:HEADS], fixo[:, 0:HEADS], ALU.subtract)
            dve.tensor_tensor(fixe[:, 1], fixs[:, 0:HEADS], fixo[:, 0:HEADS], ALU.subtract).then_inc(fix_scored, 1)
            dve.wait_ge(fix_weighed, 1)
            for z, a in ((cprev, 0), (fixs, 1)):
                dve.tensor_tensor(z[:, HEADS:2 * HEADS], z[:, HEADS:2 * HEADS], fixe[:, a], ALU.mult)
                dve.tensor_tensor(z[:, 2 * HEADS:].rearrange("p (h e) -> p h e", e=EXPERTS),
                                  z[:, 2 * HEADS:].rearrange("p (h e) -> p h e", e=EXPERTS),
                                  over(fixe[:, a], EXPERTS, 2), ALU.mult)
            flush()
            dve.tensor_tensor(fixo[:, HEADS:], cprev[:, HEADS:], fixs[:, HEADS:], ALU.add).then_inc(fix_ready, 1)

            dve.wait_ge(late_loaded, 16 * (1 + len(late_params())))
            a_src, a_dst, h_all = node[:, :, HE:ROW], node[:, :, ROW:NODE], node[:, :, 0:HE]
            n_sink, lone = one4[:, 2], one4[:, 3]
            dve.tensor_tensor(hx[:, 1], a_src, a_dst, ALU.add)
            dve.tensor_tensor(hx[:, 2], a_dst, over(last_row[:, HE:ROW], TILES), ALU.add)
            dve.tensor_tensor(n_sink, endG[:, 2], endG[:, 3], ALU.subtract)
            flush()
            for k in (1, 2):
                dve.scalar_tensor_tensor(out=hx[:, k], in0=hx[:, k], scalar=0.2, in1=hx[:, k],
                                         op0=ALU.mult, op1=ALU.max)
            dve.tensor_scalar(lone, n_sink, 0.0, -BIG, ALU.is_equal, ALU.mult)
            flush()
            dve.tensor_tensor(hx[:, 2], hx[:, 2], over(lone, HEADS, 2), ALU.add)
            flush()
            dve.tensor_tensor(hx[:, 3], hx[:, 1], hx[:, 2], ALU.max)
            dve.wait_ge(agg_got, 16 * TILES)
            flush()
            dve.tensor_tensor(hx[:, 3], hx[:, 3], agg[:, :, 0:HEADS], ALU.max)
            flush()
            dve.tensor_tensor(hx[:, 0], agg[:, :, 0:HEADS], hx[:, 3], ALU.subtract)
            dve.tensor_tensor(hx[:, 1], hx[:, 1], hx[:, 3], ALU.subtract)
            dve.tensor_tensor(hx[:, 2], hx[:, 2], hx[:, 3], ALU.subtract).then_inc(joined, 1)
            dve.wait_ge(join_weighed, 1)
            dve.tensor_tensor(hx[:, 2], hx[:, 2], over(n_sink, HEADS, 2), ALU.mult)
            dve.tensor_tensor(hx[:, 3], hx[:, 0], agg[:, :, HEADS:2 * HEADS], ALU.mult)

            def heads(v):
                return v.rearrange("p t (h e) -> p t h e", e=EXPERTS)

            dve.tensor_tensor(heads(wide[:, 0]), heads(agg[:, :, 2 * HEADS:]), over(hx[:, 0], EXPERTS, 3), ALU.mult)
            dve.tensor_tensor(heads(wide[:, 1]), heads(h_all), over(hx[:, 1], EXPERTS, 3), ALU.mult)
            flush()
            dve.tensor_tensor(wide[:, 0], wide[:, 0], wide[:, 1], ALU.add)
            dve.tensor_tensor(hx[:, 3], hx[:, 3], hx[:, 1], ALU.add)
            flush()
            dve.tensor_tensor(heads(wide[:, 1]), heads(over(last_row[:, 0:HE], TILES)), over(hx[:, 2], EXPERTS, 3), ALU.mult)
            dve.scalar_tensor_tensor(out=hx[:, 3], in0=hx[:, 3], scalar=1e-16, in1=hx[:, 2], op0=ALU.add, op1=ALU.add)
            flush()
            dve.tensor_tensor(wide[:, 0], wide[:, 0], wide[:, 1], ALU.add)
            dve.reciprocal(hx[:, 3], hx[:, 3])
            flush()
            dve.tensor_tensor(heads(wide[:, 0]), heads(wide[:, 0]), over(hx[:, 3], EXPERTS, 3), ALU.mult)
            flush()
            dve.tensor_tensor(wide[:, 0], wide[:, 0], over(gat_p[:, 0], TILES), ALU.add)
            flush()
            dve.tensor_reduce(one4[:, 0], wide[:, 0], AX.X, ALU.add)
            flush()
            dve.tensor_scalar(one4[:, 0], one4[:, 0], 1.0 / HE, None, ALU.mult)
            flush()
            dve.tensor_tensor(wide[:, 0], wide[:, 0], over(one4[:, 0], HE, 2), ALU.subtract)
            flush()
            dve.tensor_tensor(wide[:, 1], wide[:, 0], wide[:, 0], ALU.mult)
            flush()
            dve.tensor_reduce(one4[:, 0], wide[:, 1], AX.X, ALU.add)
            flush()
            dve.tensor_scalar(one4[:, 0], one4[:, 0], 1.0 / HE, None, ALU.mult).then_inc(agg_var, 1)
            dve.wait_ge(agg_root, 1)
            dve.reciprocal(one4[:, 1], one4[:, 1])
            flush()
            dve.tensor_tensor(wide[:, 0], wide[:, 0], over(one4[:, 1], HE, 2), ALU.mult)
            flush()
            dve.tensor_tensor(wide[:, 0], wide[:, 0], over(gat_p[:, 1], TILES), ALU.mult)
            flush()
            dve.tensor_tensor(wide[:, 0], wide[:, 0], over(gat_p[:, 2], TILES), ALU.add)
            flush()
            dve.tensor_reduce(hx[:, 0], wide[:, 0].rearrange("p t (h e) -> p t e h", e=EXPERTS), AX.X, ALU.add)
            flush()
            dve.tensor_scalar(hx[:, 0], hx[:, 0], 1.0 / HEADS, None, ALU.mult)
            flush()

            def pick(scores, best, chosen, taken):
                dve.tensor_reduce(best, scores, AX.X, ALU.max)
                flush()
                dve.tensor_tensor(chosen, scores, over(best, EXPERTS, 2), ALU.is_equal)
                dve.memset(taken, 1.0)
                flush()
                for e in range(EXPERTS):
                    dve.tensor_tensor(chosen[:, :, e], chosen[:, :, e], taken, ALU.mult)
                    flush()
                    dve.tensor_tensor(taken, taken, chosen[:, :, e], ALU.subtract)
                    flush()

            pick(hx[:, 0], one4[:, 1], hx[:, 1], one4[:, 2])
            dve.scalar_tensor_tensor(out=hx[:, 0], in0=hx[:, 1], scalar=-BIG, in1=hx[:, 0], op0=ALU.mult, op1=ALU.add)
            flush()
            pick(hx[:, 0], one4[:, 0], hx[:, 2], one4[:, 2])
            dve.tensor_tensor(one4[:, 0], one4[:, 0], one4[:, 1], ALU.subtract).then_inc(top_ready, 1)
            dve.wait_ge(top_weighed, 1)
            dve.tensor_scalar(one4[:, 2], one4[:, 1], 1.0, None, ALU.add)
            flush()
            dve.reciprocal(one4[:, 2], one4[:, 2])
            flush()
            dve.tensor_tensor(one4[:, 3], one4[:, 1], one4[:, 2], ALU.mult)
            dve.tensor_tensor(hx[:, 1], hx[:, 1], over(one4[:, 2], EXPERTS, 2), ALU.mult)
            flush()
            dve.tensor_tensor(hx[:, 2], hx[:, 2], over(one4[:, 3], EXPERTS, 2), ALU.mult)
            flush()
            dve.tensor_tensor(gate[:, :, :], hx[:, 1], hx[:, 2], ALU.add).then_inc(gates_ready, 1)
            flush()

            def mix(g, u, turn):
                dve.wait_ge(tokens_in[u], 32 * (turn + 1))
                for e in range(EXPERTS):
                    for r in range(ROWS):
                        if e == 0:
                            dve.wait_ge(y_psum, ROWS * g + r + 1)
                        acc = x2_in[:, u, r * C:(r + 1) * C]
                        last = dve.scalar_tensor_tensor(
                            out=acc, in0=bank[4 + r][:, e * C:(e + 1) * C],
                            scalar=gate[:, ds(ROWS * g + r, 1), e], in1=acc, op0=ALU.mult, op1=ALU.add)
                    if e < EXPERTS - 1:
                        flush()
                last.then_inc(mixed, 1)

            with dve.Fori(0, PAIRS * CHUNKS // 2) as g2:
                for u in (0, 1):
                    mix(2 * g2 + u, u, g2)


_NAMES = ['x', 'L0_conv_Wr', 'L0_conv_br', 'L0_conv_gamma', 'L0_conv_beta', 'L0_conv_mean',
          'L0_conv_var', 'L0_conv_Ws', 'L0_conv_bs', 'L0_conv_Wi', 'L0_conv_bi', 'L0_ffn_W_gat',
          'L0_ffn_att_src', 'L0_ffn_att_dst', 'L0_ffn_b_gat', 'L0_ffn_ln_gamma',
          'L0_ffn_ln_beta', 'L0_ffn_W1', 'L0_ffn_b1', 'L0_ffn_W2', 'L0_ffn_b2',
          'L0_ffn_edge_index']


def kernel(**inputs):
    import numpy as np
    import concourse.bacc as bacc
    from concourse.bass_utils import run_bass_kernel_spmd

    nc = bacc.Bacc("TRN2", target_bir_lowering=False, num_devices=1)
    arrays, args = {}, []
    for name in _NAMES:
        a = np.ascontiguousarray(inputs[name])
        arrays[f"in_{name}"] = a
        args.append(nc.dram_tensor(f"in_{name}", a.shape, mybir.dt.from_np(a.dtype),
                                   kind="ExternalInput").ap())
    out = nc.dram_tensor("out_x", (NB, NY, NX, C), F32, kind="ExternalOutput").ap()
    metaformer_block(nc, *args, out)
    result = run_bass_kernel_spmd(nc, [arrays], core_ids=[0])
    return result.results[0]["out_x"]
```

```python
from contextlib import ExitStack

import concourse.bass as bass
from concourse import mybir

F32 = mybir.dt.float32
I32 = mybir.dt.int32
ALU = mybir.AluOpType
ACT = mybir.ActivationFunctionType
AX = mybir.AxisListType

P = 128
NB, NY, NX, C = 4, 64, 64, 128
M = NB * NY * NX
PAIRS = NB // 2
TILES = M // P
EDGES = 524288
COLS = EDGES // P
LOG_E, LOG_C = 19, 12
SRC_BITS = 14
SINK = M
KEY_BASE = 2 * M
DROPPED = 4 * M
KK, GROUPS = 9, 16
TAPS = KK * C
CR = 32
HEADS, EXPERTS, HID = 4, 4, 256
HE = HEADS * EXPERTS
ROW = HE + HEADS
NODE = ROW + HEADS
ST = 2 * HEADS + HE
T = 64
MIN_STEPS = 3
BIG = 1.0e30
ROWS = 4
CHUNKS = NY // ROWS
TOK = ROWS * P
LV = 64
SKIP = float(1 << 20)
TR, FA = True, False


def some(n):
    return not isinstance(n, int) or n > 0


def metaformer_block(nc, x, Wr, br, gamma, beta, mean, var, Ws, bs, Wi, bi,
                     W_gat, att_src, att_dst, b_gat, ln_gamma, ln_beta,
                     W1, b1, W2, b2, edge_index, out):
    ctx = ExitStack()
    with ctx:
        def sb(name, shape, dt=F32, where=ctx):
            return where.enter_context(nc.sbuf_tensor("sb_" + name, shape, dt))

        def dram(name, shape, dt=F32):
            return nc.dram_tensor("scr_" + name, shape, dt, kind="Internal").ap()

        def sem(name):
            return ctx.enter_context(nc.semaphore(name))

        ds = bass.ds

        keys_d = dram("keys", [EDGES + COLS])
        borders_d = dram("borders", [P, 2], I32)
        level1_d = dram("level1", [P])
        level2_d = dram("level2", [P, LV])
        ends_d = dram("ends", [2, M + 1])
        node_d = dram("node", [M, ROW])
        adst_d = dram("adst", [M, HEADS])
        starts_d = dram("adst_at_starts", [EDGES, HEADS])
        state_d = dram("state", [EDGES, ST])
        tails_d = dram("tails", [P, ST])
        chain_d = dram("chain", [P + 1, ST])
        x2_d = dram("x2", [PAIRS * CHUNKS, P, TOK])
        tnT_d = dram("tnT", [PAIRS * CHUNKS, C, TOK])
        y_d = dram("expert_out", [PAIRS * CHUNKS, P, ROWS * EXPERTS * C])

        ident = sb("ident", [P, P])
        node = sb("node", [P, TILES, NODE])
        part = sb("part", [P, 1], I32)
        partf = sb("partf", [P, 1])
        sign_i = sb("sign_i", [P, LOG_E - LOG_C], I32)
        signs = sb("signs", [P, LOG_E - LOG_C])
        wr = sb("wr", [C, CR])
        ws = sb("ws", [CR + 1, KK * GROUPS])
        wi = sb("wi", [C, C])
        valid = sb("valid", [3, NX, 2])
        bi3 = sb("bi3", [3, 3 * C])
        bn = sb("bn", [CR, 8])
        wgat = sb("wgat", [C, NODE])
        att = sb("att", [P, 2, HE])
        eps = sb("eps", [P, 3])
        ends = sb("ends", [P, 2, P])
        endT = sb("endT", [P, 2, P])
        endO = sb("endO", [P, 2, P])
        endG = sb("endG", [P, 4, TILES])
        posi = sb("posi", [P, 2, TILES], I32)
        cnt = sb("cnt", [P, 8])
        cnti = sb("cnti", [P, 4], I32)
        keys_at = sb("keys_at", [P, 1], I32)
        border_f = sb("border_f", [P, 2])
        border_at = sb("border_at", [P, 2], I32)
        keyb = sb("keyb", [P, 1 + 2 * T], I32)

        bank = [ctx.enter_context(nc.psum_tensor(f"bank{i}", [P, 512], F32)) for i in range(8)]

        early = ExitStack()
        xi = sb("xi", [P, (NY + 2) * 3 * C], F32, early)
        xa = sb("xa", [P, 2, ROWS, C], F32, early)
        xb = sb("xb", [P, 2, ROWS, C], F32, early)
        xn = sb("xn", [P, 2, ROWS, C], F32, early)
        xnT = sb("xnT", [C, 2, ROWS, P + 4], F32, early)
        rT = sb("rT", [CR + 1, 2, TOK], F32, early)
        wv = sb("wv", [P, 2, ROWS, KK * GROUPS], F32, early)
        prod2 = sb("prod", [P, 2 * TAPS], F32, early)
        prod = prod2[:, :]
        inv = sb("inv", [P, ROWS, C], F32, early)
        tn = sb("tn", [P, ROWS, C], F32, early)
        tnT = sb("tnT", [C, 2, TOK], F32, early)
        stats = sb("stats", [P, 2, ROWS, 6], F32, early)
        mv = sb("mv", [P, 2, ROWS, 2], F32, early)
        sd = sb("sd", [P, 2, ROWS], F32, early)
        rstd = sb("rstd", [P, 2, ROWS], F32, early)
        found = sb("found", [P, P * LV], F32, early)
        samples = sb("samples", [P, P], F32, early)
        target = sb("target", [P, 2, P], I32, early)
        rank1 = sb("rank1", [P, 2, P], F32, early)
        rank2 = sb("rank2", [P, 2, P], F32, early)
        row1 = sb("row1", [P, 2, P], I32, early)
        row2 = sb("row2", [P, 2, P], I32, early)
        lvl2 = sb("lvl2", [P, LV], F32, early)
        zero = sb("zero", [1, 1], F32, early)
        key_bufs = [xi[:, 0:COLS], xi[:, COLS:2 * COLS]]
        tmp_a, tmp_b = xi[:, 2 * COLS:3 * COLS], xi[:, 3 * COLS:4 * COLS]
        pos, quo, fit = (prod[:, 2 * TILES * k:2 * TILES * (k + 1)].rearrange("p (a t) -> p a t", a=2)
                         for k in range(3))
        quoi = prod[:, 6 * TILES:8 * TILES].bitcast(I32).rearrange("p (a t) -> p a t", a=2)
        nonempty = prod[:, 8 * TILES:9 * TILES].unsqueeze(1)
        early.close()

        srcs = sb("srcs", [P, 2, T], I32)
        step_i = sb("step_i", [P, 2, T], I32)
        no_offset = sb("no_offset", [P, T], I32)
        clsi = sb("clsi", [P, T + 1], I32)
        same = sb("same", [P, 2, T])
        reset = sb("reset", [P, 2, T])
        rows_g = sb("rows_g", [P, 2, T, ROW])
        dch = sb("dch", [P, 2, T, HEADS])
        df = sb("df", [P, T + 1, HEADS])
        score = sb("score", [P, T, HEADS])
        ex = sb("ex", [P, T, 2, HEADS])
        pv = sb("pv", [P, T, HE])
        state = sb("state", [P, 2, T + 1, ST])
        edge_i = sb("edge_i", [P, 10], I32)
        edge_f = sb("edge_f", [P, 12])
        adst0 = sb("adst0", [P, HEADS])
        chk = sb("chk", [1, 2, P], I32)
        chf = sb("chf", [1, 5, P])
        cprev = sb("cprev", [P, ST])
        fixs = sb("fixs", [P, ST])
        fixo = sb("fixo", [P, ST])
        fixe = sb("fixe", [P, 2, HEADS])
        endf = sb("endf", [P, 1])
        last_row = sb("last_row", [P, ROW])
        gat_p = sb("gat_p", [P, 3, HE])
        agg = sb("agg", [P, TILES, ST])
        one4 = sb("one4", [P, 4, TILES])
        gate = sb("gate", [P, TILES, EXPERTS])
        w1 = sb("w1", [C, EXPERTS, HID])
        w2 = sb("w2", [P, EXPERTS, 2, C])
        b1c = sb("b1c", [P, EXPERTS, 2])
        b2r = sb("b2r", [1, EXPERTS * C])
        ones = sb("ones", [1, P])
        late = sb("late", [P, 2 * TILES * HE + 5 * TILES * HEADS])
        tnT_in = sb("tnT_in", [C, 2, TOK])
        hid_y = sb("hid_y", [P, 4, ROWS * EXPERTS * C])
        y_new = sb("y_new", [P, 2, ROWS, EXPERTS * C])
        x2_in = sb("x2_in", [P, 4, TOK])
        hid = [hid_y[:, 2 * u:2 * u + 2].rearrange("p b (a t) -> p (b a) t", t=TOK) for u in (0, 1)]
        tails = late[0:1, 0:P * ST].rearrange("p (n f) -> p n f", f=ST)
        chx = late[0:1, P * ST:(2 * P + 1) * ST].rearrange("p (n f) -> p n f", f=ST)
        chp = agg[0:1].rearrange("p t f -> p (t f)")[:, 0:P * ROW].rearrange("p (n f) -> p n f", f=ROW)
        che = pv[0:1].rearrange("p t f -> p (t f)").rearrange("p (n a h) -> p n a h", a=2, h=HEADS)
        wide = late[:, 0:2 * TILES * HE].rearrange("p (a t f) -> p a t f", a=2, f=HE)
        hx = late[:, 2 * TILES * HE:].rearrange("p (a t h) -> p a t h", a=5, h=HEADS)

        def sems(names):
            return [sem(n) for n in names.split()]

        (ident_zero, consts_made, dst_loaded, src_loaded, params_loaded, small_ready,
         bn_root, bn_ready, found_zero, zeros_stored) = sems(
            "ident_zero consts_made dst_loaded src_loaded params_loaded small_ready "
            "bn_root bn_ready found_zero zeros_stored")
        (phase_sorted, flipped, act_placed, keys_final, keys_stored, levels_stored,
         samples_loaded, ranked) = sems(
            "phase_sorted flipped act_placed keys_final keys_stored levels_stored "
            "samples_loaded ranked")
        rows_found = sems("rows_found0 rows_found1")
        (stats1, root1, normed1, turned1, xnT_ready, r_psum, rT_ready, xi_psum, xi_ready,
         w_psum, w_ready, pe_chunk, conv_done, root2, normed2, turned2, tnT_ready,
         node_psum, node_ready) = sems(
            "stats1 root1 normed1 turned1 xnT_ready r_psum rT_ready xi_psum xi_ready "
            "w_psum w_ready pe_chunk conv_done root2 normed2 turned2 tnT_ready "
            "node_psum node_ready")
        xa_in, xb_in, x2_out, tnT_out = (sems(f"{n}0 {n}1") for n in
                                         ("xa_in", "xb_in", "x2_out", "tnT_out"))
        (node_stored, ends_stored, ends_loaded, ends_ordered, ends_turned, ends_taken, counted, keys_in,
         prev_zero, border_found, border_stored, border_loaded, border_ready, adst0_loaded, sources_ready,
         grid_ready, starts_scattered, first_stored) = sems(
            "node_stored ends_stored ends_loaded ends_ordered ends_turned ends_taken counted keys_in "
            "prev_zero border_found border_stored border_loaded border_ready adst0_loaded sources_ready "
            "grid_ready starts_scattered first_stored")
        dch_in, dch_used, rows_in, state_out, tnT_back, y_out = (
            sems(f"{n}0 {n}1") for n in ("dch_in", "dch_used", "rows_in", "state_out", "tnT_back", "y_out"))
        (scored, weighed, state_ready, tails_stored, tails_loaded, chain_scored, chain_weighed,
         chain_ready, chain_stored, cprev_loaded, end_found, fix_placed, fix_got, fix_scored,
         fix_weighed, fix_ready, fix_stored, agg_cleared, agg_got) = sems(
            "scored weighed state_ready tails_stored tails_loaded chain_scored chain_weighed "
            "chain_ready chain_stored cprev_loaded end_found fix_placed fix_got fix_scored "
            "fix_weighed fix_ready fix_stored agg_cleared agg_got")
        (ones_ready, late_loaded, joined, join_weighed, agg_var, agg_root, top_ready, top_weighed, gates_ready,
         hid_psum, hid_ready, y_psum, y_taken, mixed) = sems(
            "ones_ready late_loaded joined join_weighed agg_var agg_root top_ready top_weighed gates_ready "
            "hid_psum hid_ready y_psum y_taken mixed")
        tokens_in, out_stored = (sems(f"{n}0 {n}1 {n}2 {n}3") for n in ("tokens_in", "out_stored"))

        def pair_rows(t, q, i2, c):
            return t[2 * q + i2, ds(c * ROWS, ROWS), :, :].rearrange("r x f -> x r f")

        def by_tile(t, i):
            return t.rearrange("(q a y x) -> q y a x", q=PAIRS, a=2, x=NX)[i]

        starts_runs = starts_d.rearrange("(p c) h -> p c h", p=P)
        state_runs = state_d.rearrange("(p c) f -> p c f", p=P)
        key_rows = keys_d.rearrange("(r k) -> r k", k=LV)
        step_rows = keys_d.bitcast(I32).rearrange("(r k) -> r k", k=2 * T)
        out_v, x_v = out, x

        def over(row, n, where=1):
            v = row.unsqueeze(where)
            shape = list(v.shape)
            shape[where] = n
            return v.to_broadcast(shape)

        def sort_plan():
            steps, before = LOG_C * (LOG_C - 1) // 2 + 1 + LOG_C, []
            for k in range(LOG_C + 1, LOG_E + 1):
                before.append(steps % 2)
                steps += 1 + k - LOG_C
                before.append(steps % 2)
                steps += 1 + LOG_C
            return before, steps % 2

        key_before, key_at_end = sort_plan()
        sorted_keys = key_bufs[key_at_end]

        def params():
            col = [(bn[:, k:k + 1], v.unsqueeze(1)) for k, v in enumerate((br, gamma, beta, mean, var))]
            return col + [
                (wr[:, :], Wr), (ws[0:CR, :], Ws), (ws[CR:CR + 1, :], bs.unsqueeze(0)), (wi[:, :], Wi),
                (wgat[:, 0:HE], W_gat),
                (att[:, 0], att_src.rearrange("h e -> (h e)").partition_broadcast(P)),
                (att[:, 1], att_dst.rearrange("h e -> (h e)").partition_broadcast(P)),
            ] + [(bi3[j:j + 1, j * C:(j + 1) * C], bi.unsqueeze(0)) for j in range(3)]

        def late_params():
            return ([(gat_p[:, k], v.partition_broadcast(P)) for k, v in enumerate((b_gat, ln_gamma, ln_beta))]
                    + [(w1[:, e], W1[e]) for e in range(EXPERTS)]
                    + [(w2[:, e], W2[e].rearrange("(a p) f -> p a f", a=2)) for e in range(EXPERTS)]
                    + [(b2r[:, :], b2.rearrange("e f -> (e f)").unsqueeze(0))]
                    + [(b1c[:, e], b1[e].rearrange("(a p) -> p a", a=2)) for e in range(EXPERTS)])

        def more(i, n):
            return not isinstance(i, int) or i + n < PAIRS * CHUNKS

        def after(q, c, n):
            if isinstance(c, int) and c + n >= CHUNKS:
                return q + 1, c + n - CHUNKS
            return q, c + n

        def over_chunks(engine, step, first, end):
            half = CHUNKS // 2
            q, a, b = first // half, first % half, (end - 1) % half + 1
            lo, hi = max(a, 1 if q == 0 else 0), min(b, half - 2)
            if a < lo:
                for u in (0, 1):
                    step(q, a, u)
            if lo < hi:
                with engine.Fori(lo, hi) as c2:
                    for u in (0, 1):
                        step(q, c2, u)
            for c in range(2 * max(a, hi), 2 * b):
                step(q, c // 2, c % 2)

        halfway, ends_turn, all_chunks = CHUNKS // 2, CHUNKS // 2 + CHUNKS // 4, CHUNKS

        def halves(ap, g):
            return ap.rearrange("p (h d l) -> p h d l", d=2, l=1 << g)

        block = ctx.enter_context(nc.Block())

        @block.sync
        def _(sp):
            def put(to, of, s):
                sp.dma_start(to, of).then_inc(s, 16)

            put(key_bufs[0].bitcast(I32), edge_index[1].rearrange("(p c) -> p c", p=P), dst_loaded)
            put(key_bufs[1].bitcast(I32), edge_index[0].rearrange("(p c) -> p c", p=P), src_loaded)
            sp.wait_ge(ident_zero, 3)
            with nc.allow_non_contiguous_dma(reason="columns of a few numbers"):
                for to, of in params():
                    put(to, of, params_loaded)

            def load_xa(q, c, u):
                for i2 in (0, 1):
                    put(xa[i2::2, u], pair_rows(x_v, q, i2, c), xa_in[u])

            def load_xb(q, c, u):
                for i2 in (0, 1):
                    put(xb[i2::2, u], pair_rows(x_v, q, i2, c), xb_in[u])

            for u in (0, 1):
                load_xa(0, u, u)
                load_xb(0, u, u)

            sp.wait_ge(keys_final, 1)
            sk = sorted_keys
            put(keys_d[0:EDGES].rearrange("(p c) -> p c", p=P), sk, keys_stored)
            put(keys_d[EDGES:EDGES + COLS].unsqueeze(0), sk[P - 1:P, :], keys_stored)
            with nc.allow_non_contiguous_dma(reason="one key per partition"):
                put(level1_d.unsqueeze(1), sk[:, COLS - 1:COLS], levels_stored)
            put(level2_d, lvl2[:, :], levels_stored)
            sp.wait_ge(levels_stored, 32)
            put(samples[:, :], level1_d.partition_broadcast(P), samples_loaded)

            def step(q, c2, u):
                c, i = 2 * c2 + u, CHUNKS * q + 2 * c2 + u
                turn = CHUNKS // 2 * q + c2
                if more(i, 4):
                    sp.wait_ge(normed1, i + 3)
                    load_xa(*after(q, c, 4), u)
                sp.wait_ge(conv_done, i + 1)
                put(x2_d[ds(i, 1)].squeeze(0), xb[:, u].rearrange("p r f -> p (r f)"), x2_out[u])
                sp.wait_ge(tnT_ready, i + 1)
                put(tnT_d[ds(i, 1)].squeeze(0), tnT[:, u], tnT_out[u])
                if more(i, 2):
                    sp.wait_ge(normed2, i + 1)
                    sp.wait_ge(x2_out[u], 16 * (turn + 1))
                    load_xb(*after(q, c, 2), u)

            for u in (0, 1):
                sp.wait_ge(normed1, u + 1)
                load_xa(0, 2 + u, u)
            over_chunks(sp, step, 0, halfway)

            def store_nodes(q):
                sp.wait_ge(node_ready, CHUNKS * (q + 1))
                for i2 in (0, 1):
                    b = (2 * q + i2) * NY * NX
                    part_of = node[i2::2, q * NY:(q + 1) * NY]
                    put(node_d[b:b + NY * NX].rearrange("(y x) f -> x y f", x=NX),
                        part_of[:, :, 0:ROW], node_stored)
                    put(adst_d[b:b + NY * NX].rearrange("(y x) f -> x y f", x=NX),
                        part_of[:, :, ROW:NODE], node_stored)

            def turn_ends(k):
                sp.wait_ge(ranked, 4 * k + 5)
                put(ends_d[k, 1:M + 1].rearrange("(p c) -> p c", p=P), ends[:, k], ends_stored)
                if k == 0:
                    put(ends_d[0, 0:1].unsqueeze(0), zero[:, :], ends_stored)
                    put(ends_d[1, 0:1].unsqueeze(0), ends[P - 1:P, 0, P - 1:P], ends_stored)
                else:
                    sp.wait_ge(ends_ordered, 1)
                sp.wait_ge(ends_stored, 48 if k == 0 else 64)
                if k == 0:
                    put(cnt[:, 0:1], ends_d[0, M:M + 1].partition_broadcast(P), ends_loaded)
                for a, v in enumerate((ends_d[k, 1:M + 1], ends_d[k, 0:M])):
                    for q in range(PAIRS):
                        put(endT[q * NY:(q + 1) * NY, a].rearrange("p (a x) -> p a x", a=2),
                            by_tile(v, q), ends_loaded)

            turn_ends(0)
            store_nodes(0)
            over_chunks(sp, step, halfway, all_chunks)
            store_nodes(1)
            turn_ends(1)
            steps = sp.value_load(cnti[0:1, 0:1], min_val=MIN_STEPS, max_val=COLS // (2 * T))
            sp.wait_ge(border_found, 48)
            put(borders_d, edge_i[:, 0:2], border_stored)
            sp.wait_ge(border_stored, 16)
            with nc.allow_non_contiguous_dma(reason="one key per run"):
                put(chk[0:1, 0:2], borders_d.rearrange("p a -> a p").unsqueeze(0), border_loaded)
            sp.wait_ge(node_stored, 16 * 8)
            put(last_row[:, :], node_d[M - 1].partition_broadcast(P), late_loaded)
            with nc.allow_non_contiguous_dma(reason="columns of a few numbers"):
                for to, of in late_params():
                    put(to, of, late_loaded)
            sp.wait_ge(adst0_loaded, 16)
            sp.wait_ge(starts_scattered, 16 * TILES)
            put(starts_runs[:, 0], adst0[:, :], first_stored)
            sp.wait_ge(first_stored, 16)

            def edge_step(k):
                for u in (0, 1):
                    if some(k):
                        sp.wait_ge(dch_used[u], k)
                    put(dch[:, u], starts_runs[:, ds((2 * k + u) * T, T)], dch_in[u])
                for u in (0, 1):
                    sp.wait_ge(state_ready, 2 * k + u + 1)
                    put(state_runs[:, ds((2 * k + u) * T, T)], state[:, u, 1:], state_out[u])

            edge_step(0)
            with sp.Fori(1, steps) as k:
                edge_step(k)
            for u in (0, 1):
                sp.wait_ge(state_out[u], 16 * steps)
            put(tails_d, state[:, 1, T], tails_stored)
            sp.wait_ge(tails_stored, 16)
            put(tails, tails_d.unsqueeze(0), tails_loaded)
            sp.wait_ge(chain_ready, 1)
            put(chain_d.unsqueeze(0), chx, chain_stored)
            sp.wait_ge(chain_stored, 16)
            put(cprev[:, :], chain_d[0:P], cprev_loaded)

            for u in (0, 1):
                sp.wait_ge(y_out[u], 16 * PAIRS * CHUNKS // 2)
            for b in range(4):
                put(hid_y[:, b], y_d[b], tokens_in[b])
                put(x2_in[:, b], x2_d[b], tokens_in[b])

            def store_step(q, c4, b):
                g, turn = CHUNKS * q + 4 * c4 + b, CHUNKS // 4 * q + c4
                sp.wait_ge(mixed, g + 1)
                for i2 in (0, 1):
                    put(pair_rows(out_v, q, i2, 4 * c4 + b),
                        x2_in[i2::2, b].rearrange("p (r f) -> p r f", f=C), out_stored[b])
                if more(g, 4):
                    put(hid_y[:, b], y_d[ds(g + 4, 1)].squeeze(0), tokens_in[b])
                    sp.wait_ge(out_stored[b], 32 * (turn + 1))
                    put(x2_in[:, b], x2_d[ds(g + 4, 1)].squeeze(0), tokens_in[b])

            for q in range(PAIRS):
                with sp.Fori(0, CHUNKS // 4 - 1) as c4:
                    for b in range(4):
                        store_step(q, c4, b)
                for b in range(4):
                    store_step(q, CHUNKS // 4 - 1, b)
            for b in range(4):
                sp.wait_ge(out_stored[b], 32 * PAIRS * CHUNKS // 4)

        @block.gpsimd
        def _(pool):
            pool.memset(ident[:, :], 0.0).then_inc(ident_zero, 1)
            pool.memset(valid[:, :, :], 1.0).then_inc(ident_zero, 1)
            pool.memset(bi3[:, :], 0.0).then_inc(ident_zero, 1)
            pool.iota(part[:, :], pattern=[[0, 1]], base=0, channel_multiplier=1).then_inc(consts_made, 1)
            for k in (0, 1):
                pool.iota(target[:, k], pattern=[[1, P]], base=1 + KEY_BASE + k * SINK,
                          channel_multiplier=P).then_inc(consts_made, 1)
            pool.wait_ge(ident_zero, 3)
            pool.affine_select(out=ident[:, :], in_=ident[:, :], compare_op=ALU.not_equal, fill=1.0,
                               base=0, pattern=[[-1, P]], channel_multiplier=1).then_inc(consts_made, 1)
            pool.affine_select(out=valid[:, :, :], in_=valid[:, :, :], compare_op=ALU.not_equal,
                               fill=0.0, base=0, pattern=[[1, NX], [0, 2]],
                               channel_multiplier=NX).then_inc(ident_zero, 1)
            pool.wait_ge(ident_zero, 4)
            pool.affine_select(out=valid[:, :, :], in_=valid[:, :, :], compare_op=ALU.not_equal,
                               fill=0.0, base=-(3 * NX - 1), pattern=[[1, NX], [0, 2]],
                               channel_multiplier=NX).then_inc(consts_made, 1)

            pool.memset(found[:, :], 0.0).then_inc(found_zero, 1)
            pool.wait_ge(found_zero, 1)
            for flat in (starts_d, state_d):
                flat = flat.rearrange("(p c) h -> p (c h)", p=P)
                for k in range(0, flat.shape[1], P * LV):
                    pool.dma_start(flat[:, k:k + P * LV], found[:, :]).then_inc(zeros_stored, 16)
            zeros = COLS * (HEADS + ST) // (P * LV)

            def gather(to, table, index, s, bound=None):
                kw = {} if bound is None else dict(bounds_check=bound, oob_is_err=False)
                pool.indirect_dma_start(to, None, table, bass.IndirectOffsetOnAxis(ap=index, axis=0),
                                        **kw).then_inc(s, 16)

            def scatter(table, index, of, s, bound):
                pool.indirect_dma_start(table, bass.IndirectOffsetOnAxis(ap=index, axis=0), of, None,
                                        bounds_check=bound, oob_is_err=False).then_inc(s, 16)

            pool.wait_ge(levels_stored, 32)
            pool.wait_ge(keys_stored, 32)
            for n in range(8):
                level, k, h = n // 2 % 2, n // 4, n % 2
                pool.wait_ge(ranked, max(1, n))
                table, index = (level2_d, row1) if level == 0 else (key_rows, row2)
                for c in range(h * P // 2, (h + 1) * P // 2):
                    gather(found[:, c * LV:(c + 1) * LV], table, index[:, k, c:c + 1], rows_found[h])

            pool.wait_ge(counted, 1)
            gather(keyb[:, 1:], step_rows, keys_at[:, :], keys_in)
            pool.wait_ge(grid_ready, 1)
            pool.wait_ge(zeros_stored, 16 * zeros)
            for t in range(TILES):
                if t % ROWS == 0:
                    pool.wait_ge(node_ready, t // ROWS + 1)
                scatter(starts_d, posi[:, 1, t:t + 1], node[:, t, ROW:NODE], starts_scattered, EDGES - 1)
            pool.wait_ge(prev_zero, 1)
            one_key = keys_d.bitcast(I32).unsqueeze(1)
            pool.memset(no_offset[:, :], 0).then_inc(consts_made, 1)
            pool.wait_ge(consts_made, 6)
            pool.wait_ge(keys_in, 16)
            gather(edge_i[:, 0:1], step_rows, keys_at[:, :], border_found)
            gather(edge_i[:, 1:2], one_key, border_at[:, 0:1], border_found)
            gather(edge_i[:, 2:3], one_key, border_at[:, 1:2], border_found, EDGES - 1)
            pool.wait_ge(border_ready, 1)
            pool.wait_ge(node_stored, 16 * 8)
            gather(adst0[:, :], adst_d, edge_i[:, 6:7], adst0_loaded)
            gather(endf[:, :], ends_d[0].unsqueeze(1), edge_i[:, 8:9], end_found)
            steps = pool.value_load(cnti[0:1, 0:1], min_val=MIN_STEPS, max_val=COLS // (2 * T))
            with pool.Fori(0, steps) as k:
                for u in (0, 1):
                    pool.wait_ge(sources_ready, 2 * k + u + 1)
                    pool.tensor_tensor(step_i[:, u], srcs[:, u], no_offset[:, :], ALU.add)
                    pool.drain()
                    if u == 1:
                        gather(keyb[:, 1:], step_rows, keys_at[:, :], keys_in)
                    for j in range(T):
                        gather(rows_g[:, u, j], node_d, step_i[:, u, j:j + 1], rows_in[u])
            pool.wait_ge(end_found, 16)
            pool.wait_ge(fix_placed, 1)
            pool.wait_ge(cprev_loaded, 16)
            gather(fixs[:, :], state_d, edge_i[:, 7:8], fix_got, EDGES - 1)
            pool.wait_ge(fix_ready, 1)
            scatter(state_d, edge_i[:, 7:8], fixo[:, :], fix_stored, EDGES - 1)
            pool.wait_ge(fix_stored, 16)
            pool.wait_ge(agg_cleared, 1)
            for t in range(TILES):
                gather(agg[:, t], state_d, posi[:, 0, t:t + 1], agg_got, EDGES - 1)

        @block.tensor
        def _(pe):
            pe.wait_ge(consts_made, 5)
            for n in range(2 * (LOG_E - LOG_C)):
                pe.wait_ge(phase_sorted, n + 1)
                src = key_bufs[key_before[n]]
                for b in range(8):
                    for m in range(4):
                        last = pe.transpose(bank[b][:, m * P:(m + 1) * P],
                                            src[:, (4 * b + m) * P:(4 * b + m + 1) * P], ident[:, :])
                    last.then_inc(flipped, 1)

            pe.wait_ge(params_loaded, 16 * len(params()))
            pe.wait_ge(bn_ready, 2)

            def turn_conv(i, u):
                pe.wait_ge(normed1, i + 1)
                if some(i):
                    pe.wait_ge(xnT_ready, i)
                for r in range(ROWS):
                    last = pe.transpose(bank[0][:, r * P:(r + 1) * P], xn[:, u, r], ident[:, :])
                last.then_inc(turned1, 1)

            def conv_products(i, u):
                pe.wait_ge(xnT_ready, i + 1)
                if some(i):
                    pe.wait_ge(rT_ready, i)
                pe.matmul(bank[1][0:CR, :], wr[:, :], xnT[:, u, :, 2:P + 2],
                          start=TR, stop=TR).then_inc(r_psum, 1)
                for r in range(ROWS):
                    po = bank[4 + r % 2]
                    if some(ROWS * i + r - 1):
                        pe.wait_ge(xi_ready, ROWS * i + r - 1)
                    pe.matmul(po[:, 0:3 * C], valid[:, :, :].rearrange("p x a -> p (x a)"), bi3[:, :], start=TR, stop=FA)
                    for j in range(3):
                        last = pe.matmul(po[:, j * C:(j + 1) * C], xnT[:, u, r, 2 * j:2 * j + P], wi[:, :],
                                         start=FA, stop=j == 2)
                    last.then_inc(xi_psum, 1)
                pe.wait_ge(rT_ready, i + 1)
                if some(i):
                    pe.wait_ge(w_ready, i)
                for r in range(ROWS):
                    po = bank[2 + r // 2][:, r % 2 * KK * GROUPS:(r % 2 + 1) * KK * GROUPS]
                    last = pe.matmul(po, rT[:, u, r * P:(r + 1) * P], ws[:, :], start=TR, stop=TR)
                last.then_inc(w_psum, 1)

            def turn_tokens(i):
                pe.wait_ge(normed2, i + 1)
                if some(i):
                    pe.wait_ge(tnT_ready, i)
                for r in range(ROWS):
                    last = pe.transpose(bank[6][:, r * P:(r + 1) * P], tn[:, r], ident[:, :])
                last.then_inc(turned2, 1)

            def node_products(i, u):
                pe.wait_ge(tnT_ready, i + 1)
                if some(i):
                    pe.wait_ge(node_ready, i)
                for r in range(ROWS):
                    last = pe.matmul(bank[7][:, r * NODE:(r + 1) * NODE], tnT[:, u, r * P:(r + 1) * P],
                                     wgat[:, :], start=TR, stop=TR)
                last.then_inc(node_psum, 1)

            def chunk_products(q, c2, u):
                i = CHUNKS * q + 2 * c2 + u
                if some(i):
                    turn_tokens(i - 1)
                if more(i, 2):
                    turn_conv(i + 2, u)
                if some(i):
                    node_products(i - 1, 1 - u)
                if more(i, 2):
                    conv_products(i + 2, u)

            for u in (0, 1):
                turn_conv(u, u)
                conv_products(u, u)
            def turn_ends(k):
                pe.wait_ge(ends_ordered, k + 1)
                pe.wait_ge(node_ready, PAIRS * CHUNKS if k else 2 * ends_turn - 1)
                for a in (0, 1):
                    last = pe.transpose(bank[7][:, (2 + a) * P:(3 + a) * P], endO[:, a], ident[:, :])
                last.then_inc(ends_turned, 1)
                pe.wait_ge(ends_taken, k + 1)

            over_chunks(pe, chunk_products, 0, halfway)
            over_chunks(pe, chunk_products, halfway, ends_turn)
            turn_ends(0)
            over_chunks(pe, chunk_products, ends_turn, all_chunks)
            turn_tokens(PAIRS * CHUNKS - 1)
            node_products(PAIRS * CHUNKS - 1, 1)
            turn_ends(1)

            pe.wait_ge(late_loaded, 16 * (1 + len(late_params())))
            pe.wait_ge(ones_ready, 1)

            def experts(g, u, turn):
                pe.wait_ge(tnT_back[u], 16 * (turn + 1))
                for e in range(EXPERTS):
                    for a in (0, 1):
                        n = 2 * e + a
                        if some(8 * g + n - 3):
                            pe.wait_ge(hid_ready, 8 * g + n - 3)
                        pe.matmul(bank[n % 4][:, :], w1[:, e, a * P:(a + 1) * P], tnT_in[:, u],
                                  start=TR, stop=TR).then_inc(hid_psum, 1)
                pe.wait_ge(hid_ready, 8 * g + 8)
                for r in range(ROWS):
                    if some(g):
                        pe.wait_ge(y_taken, ROWS * (g - 1) + r + 1)
                    po = bank[4 + r]
                    pe.matmul(po[:, :], ones[:, :], b2r[:, :], start=TR, stop=FA)
                    for e in range(EXPERTS):
                        for a in (0, 1):
                            last = pe.matmul(po[:, e * C:(e + 1) * C],
                                             hid[u][:, 2 * e + a, r * P:(r + 1) * P], w2[:, e, a],
                                             start=FA, stop=e == EXPERTS - 1 and a == 1)
                    last.then_inc(y_psum, 1)

            experts(0, 0, 0)
            experts(1, 1, 0)
            with pe.Fori(1, PAIRS * CHUNKS // 2) as g2:
                for u in (0, 1):
                    experts(2 * g2 + u, u, g2)

        @block.scalar
        def _(act):
            act.wait_ge(params_loaded, 16 * len(params()))
            act.wait_ge(small_ready, 1)
            act.activation(bn[:, 5:6], bn[:, 4:5], ACT.Sqrt, bias=eps[0:CR, 2:3]).then_inc(bn_root, 1)
            n = 0
            for k in range(LOG_C + 1, LOG_E + 1):
                for way in (0, 1):
                    to = key_bufs[1 - key_before[n]]
                    for b in range(0, 8, 2):
                        act.wait_ge(flipped, 8 * n + b + 1)
                        blk = to[:, b * 512:(b + 1) * 512]
                        if way == 0:
                            for d in (0, 1):
                                last = act.activation(halves(blk, k - 1 - LOG_C)[:, :, d],
                                                      halves(bank[b][:, :], k - 1 - LOG_C)[:, :, d],
                                                      ACT.Copy, scale=1.0 - 2 * d)
                            last.then_inc(act_placed, 1)
                        elif k < LOG_E:
                            act.activation(blk, bank[b][:, :], ACT.Copy,
                                           scale=signs[:, k - LOG_C:k - LOG_C + 1]).then_inc(act_placed, 1)
                        else:
                            act.activation(blk, bank[b][:, :], ACT.Copy).then_inc(act_placed, 1)
                    n += 1

            act.wait_ge(bn_ready, 2)

            def first_root(i):
                act.wait_ge(stats1, i + 1)
                act.activation(sd[:, 0], mv[:, 0, :, 1], ACT.Sqrt, bias=eps[:, 0:1]).then_inc(root1, 1)

            def take_conv(i, u):
                act.wait_ge(turned1, i + 1)
                if some(i - 1):
                    act.wait_ge(w_psum, i - 1)
                act.activation(xnT[:, u, :, 2:P + 2], bank[0][:, :].rearrange("p (r t) -> p r t", t=P),
                               ACT.Copy).then_inc(xnT_ready, 1)

            def conv_copies(q, c, u, ahead):
                i = CHUNKS * q + c
                act.wait_ge(r_psum, i + 1)
                act.activation(rT[0:CR, u], bank[1][0:CR, :], ACT.Relu, bias=bn[:, 6:7],
                               scale=bn[:, 5:6]).then_inc(rT_ready, 1)
                for r in range(ROWS):
                    act.wait_ge(xi_psum, ROWS * i + r + 1)
                    if q:
                        act.wait_ge(conv_done, CHUNKS * (q - 1) + c + 2)
                    act.activation(xi[:, ds((ROWS * c + r + 1) * 3 * C, 3 * C)],
                                   bank[4 + r % 2][:, 0:3 * C], ACT.Copy).then_inc(xi_ready, 1)
                if ahead:
                    first_root(i + 1)
                act.wait_ge(w_psum, i + 1)
                if some(i - 1):
                    act.wait_ge(conv_done, i - 1)
                for b in (0, 1):
                    last = act.activation(wv[:, u, 2 * b:2 * b + 2].rearrange("p r k -> p (r k)"),
                                          bank[2 + b][:, 0:2 * KK * GROUPS], ACT.Copy)
                last.then_inc(w_ready, 1)

            def take_tokens(i, u, turn):
                act.wait_ge(conv_done, i + 1)
                act.activation(sd[:, 1], mv[:, 1, :, 1], ACT.Sqrt, bias=eps[:, 1:2]).then_inc(root2, 1)
                act.wait_ge(turned2, i + 1)
                if some(i - 1):
                    act.wait_ge(node_psum, i - 1)
                if some(turn):
                    act.wait_ge(tnT_out[u], 16 * turn)
                act.activation(tnT[:, u], bank[6][:, :], ACT.Copy).then_inc(tnT_ready, 1)

            def node_copies(i):
                act.wait_ge(node_psum, i + 1)
                act.activation(node[:, ds(ROWS * i, ROWS)].rearrange("p r f -> p (r f)"),
                               bank[7][:, 0:ROWS * NODE], ACT.Copy).then_inc(node_ready, 1)

            def chunk_copies(q, c2, u):
                c, i, turn = 2 * c2 + u, CHUNKS * q + 2 * c2 + u, CHUNKS // 2 * q + c2
                if some(i):
                    take_tokens(i - 1, 1 - u, turn if u else turn - 1)
                if more(i, 2):
                    take_conv(i + 2, u)
                if some(i):
                    node_copies(i - 1)
                if more(i, 2):
                    conv_copies(*after(q, c, 2), u, more(i, 3))

            first_root(0)
            first_root(1)
            for u in (0, 1):
                take_conv(u, u)
                conv_copies(0, u, u, u == 1)
            def take_ends(k):
                act.wait_ge(ends_turned, k + 1)
                act.activation(endG[:, 2 * k:2 * k + 2].rearrange("p a t -> p (a t)"),
                               bank[7][:, 2 * P:4 * P], ACT.Copy).then_inc(ends_taken, 1)

            over_chunks(act, chunk_copies, 0, halfway)
            over_chunks(act, chunk_copies, halfway, ends_turn)
            take_ends(0)
            over_chunks(act, chunk_copies, ends_turn, all_chunks)
            take_tokens(PAIRS * CHUNKS - 1, 1, PAIRS * CHUNKS // 2 - 1)
            node_copies(PAIRS * CHUNKS - 1)
            take_ends(1)

            act.wait_ge(late_loaded, 16 * (1 + len(late_params())))
            for u in (0, 1):
                act.wait_ge(tnT_out[u], 16 * PAIRS * CHUNKS // 2)
                act.dma_start(tnT_in[:, u], tnT_d[u]).then_inc(tnT_back[u], 16)

            def expert_copies(g, v, turn, ahead):
                for n in range(8):
                    act.wait_ge(hid_psum, 8 * g + n + 1)
                    if n == 0 and some(g - 1):
                        act.wait_ge(y_psum, ROWS * (g - 1))
                    act.activation(hid[v][:, n], bank[n % 4][:, :], ACT.Gelu,
                                   bias=b1c[:, n // 2, n % 2:n % 2 + 1]).then_inc(hid_ready, 1)
                if ahead:
                    act.dma_start(tnT_in[:, v], tnT_d[ds(g + 2, 1)].squeeze(0)).then_inc(tnT_back[v], 16)
                if some(turn):
                    act.wait_ge(y_out[v], 16 * turn)
                for r in range(ROWS):
                    act.wait_ge(y_psum, ROWS * g + r + 1)
                    act.activation(y_new[:, v, r], bank[4 + r][:, :], ACT.Copy).then_inc(y_taken, 1)
                act.wait_ge(y_taken, ROWS * (g + 1))
                act.dma_start(y_d[ds(g, 1)].squeeze(0), y_new[:, v].rearrange("p r f -> p (r f)")).then_inc(y_out[v], 16)

            def edge_exponentials(k, u):
                act.wait_ge(scored, 2 * k + u + 1)
                act.activation(ex[:, :, :, :], ex[:, :, :, :], ACT.Exp).then_inc(weighed, 1)

            def both(k):
                for u in (0, 1):
                    for v in (0, 1):
                        expert_copies(4 * k + 2 * u + v, v, 2 * k + u, True)
                    edge_exponentials(k, u)

            steps = act.value_load(cnti[0:1, 0:1], min_val=MIN_STEPS, max_val=COLS // (2 * T))
            shared = act.value_load(cnti[0:1, 2:3], min_val=MIN_STEPS - 1, max_val=PAIRS * CHUNKS // 4 - 1)
            both(0)
            with act.Fori(1, shared) as k:
                both(k)
            with act.Fori(shared, steps) as k:
                for u in (0, 1):
                    edge_exponentials(k, u)
            past_first = act.value_load(cnti[0:1, 3:4], min_val=MIN_STEPS - 2, max_val=PAIRS * CHUNKS // 4 - 2)
            with act.Fori(2 * past_first + 2, PAIRS * CHUNKS // 2 - 1) as g2:
                for v in (0, 1):
                    expert_copies(2 * g2 + v, v, g2, True)
            for v in (0, 1):
                expert_copies(PAIRS * CHUNKS - 2 + v, v, PAIRS * CHUNKS // 2 - 1, False)
            act.wait_ge(chain_scored, 1)
            act.activation(che, che, ACT.Exp).then_inc(chain_weighed, 1)
            act.wait_ge(fix_scored, 1)
            act.activation(fixe[:, :, :], fixe[:, :, :], ACT.Exp).then_inc(fix_weighed, 1)
            act.wait_ge(joined, 1)
            act.activation(hx[:, 0:3], hx[:, 0:3], ACT.Exp).then_inc(join_weighed, 1)
            act.wait_ge(agg_var, 1)
            act.activation(one4[:, 1], one4[:, 0], ACT.Sqrt, bias=eps[:, 1:2]).then_inc(agg_root, 1)
            act.wait_ge(top_ready, 1)
            act.activation(one4[:, 1], one4[:, 0], ACT.Exp).then_inc(top_weighed, 1)


        @block.vector
        def _(dve):
            flush = dve.drain

            dve.wait_ge(consts_made, 5)
            for k in range(LOG_E - LOG_C):
                dve.tensor_scalar(sign_i[:, k:k + 1], part[:, :], k, 1,
                                  ALU.logical_shift_right, ALU.bitwise_and)
            dve.tensor_copy(partf[:, :], part[:, :])
            for k, v in enumerate((1e-6, 1e-5, 1e-3)):
                dve.memset(eps[:, k:k + 1], v)
            dve.memset(zero[:, :], 0.0)
            dve.memset(keyb[:, 0:1], 0)
            for k in (0, 1):
                dve.tensor_scalar(target[:, k], target[:, k], SRC_BITS, None, ALU.logical_shift_left)
            flush()
            dve.tensor_scalar(signs[:, :], sign_i[:, :], -2.0, 1.0, ALU.mult, ALU.add).then_inc(small_ready, 1)

            dve.wait_ge(dst_loaded, 16)
            dve.wait_ge(src_loaded, 16)
            dst, src = key_bufs[0].bitcast(I32), key_bufs[1].bitcast(I32)
            cls, gone = tmp_a.bitcast(I32), tmp_b.bitcast(I32)
            dve.tensor_scalar(src, src, 0, M - 1, ALU.max, ALU.min)
            dve.tensor_scalar(gone, dst, M, DROPPED, ALU.is_ge, ALU.mult)
            flush()
            dve.tensor_scalar(dst, dst, M, None, ALU.min)
            dve.tensor_scalar(cls, src, M - 1, SINK, ALU.is_ge, ALU.mult)
            flush()
            dve.scalar_tensor_tensor(out=dst, in0=dst, scalar=KEY_BASE, in1=cls, op0=ALU.add, op1=ALU.add)
            flush()
            dve.tensor_tensor(dst, dst, gone, ALU.max)
            flush()
            dve.tensor_scalar(dst, dst, SRC_BITS, None, ALU.logical_shift_left)
            flush()
            dve.tensor_tensor(dst, dst, src, ALU.bitwise_or)
            flush()
            bufs = list(key_bufs)

            def compare(cmp_bit, dir_bit):
                a, b = bufs
                if dir_bit is None:
                    va, vb = halves(a, cmp_bit), halves(b, cmp_bit)
                    dve.tensor_tensor(vb[:, :, 0], va[:, :, 0], va[:, :, 1], ALU.min)
                    last = dve.tensor_tensor(vb[:, :, 1], va[:, :, 0], va[:, :, 1], ALU.max)
                else:
                    cut = dict(d=2, m=1 << (dir_bit - 1 - cmp_bit), c=2, l=1 << cmp_bit)
                    va, vb = (z.rearrange("p (h d m c l) -> p h d m c l", **cut) for z in (a, b))
                    for d in (0, 1):
                        for c in (0, 1):
                            last = dve.tensor_tensor(vb[:, :, d, :, c], va[:, :, d, :, 0], va[:, :, d, :, 1],
                                                     ALU.min if c == d else ALU.max)
                bufs.reverse()
                return last

            for k in range(1, LOG_C):
                for j in reversed(range(k)):
                    compare(j, k)
                    flush()
            dve.tensor_scalar(bufs[1], bufs[0], signs[:, 0:1], None, ALU.mult)
            bufs.reverse()
            flush()
            for j in reversed(range(LOG_C)):
                last = compare(j, None)
                if j:
                    flush()
            n = 0
            for k in range(LOG_C + 1, LOG_E + 1):
                for way in (0, 1):
                    assert bufs[0] is key_bufs[key_before[n]]
                    last.then_inc(phase_sorted, 1)
                    for b in range(1, 8, 2):
                        dve.wait_ge(flipped, 8 * n + b + 1)
                        blk = bufs[1][:, b * 512:(b + 1) * 512]
                        if way == 0:
                            for d in (0, 1):
                                dve.tensor_scalar(halves(blk, k - 1 - LOG_C)[:, :, d],
                                                  halves(bank[b][:, :], k - 1 - LOG_C)[:, :, d],
                                                  1.0 - 2 * d, None, ALU.mult)
                        elif k < LOG_E:
                            dve.tensor_scalar(blk, bank[b][:, :], signs[:, k - LOG_C:k - LOG_C + 1],
                                              None, ALU.mult)
                        else:
                            dve.tensor_copy(blk, bank[b][:, :])
                    n += 1
                    bufs.reverse()
                    dve.wait_ge(act_placed, 4 * n)
                    flush()
                    if way == 0:
                        for j in reversed(range(LOG_C, k)):
                            last = compare(j - LOG_C, k - LOG_C if k < LOG_E else None)
                            if j > LOG_C:
                                flush()
                    else:
                        for j in reversed(range(LOG_C)):
                            last = compare(j, None)
                            if j:
                                flush()
            assert bufs[0] is sorted_keys
            flush()
            dve.tensor_copy(lvl2[:, :], sorted_keys[:, LV - 1:COLS:LV]).then_inc(keys_final, 1)

            dve.wait_ge(params_loaded, 16 * len(params()))
            for k in (0, 1):
                dve.tensor_tensor(prod[:, k * HE:(k + 1) * HE], att[:, k], wgat[:, 0:HE], ALU.mult)
            dve.wait_ge(bn_root, 1)
            dve.reciprocal(bn[:, 5:6], bn[:, 5:6])
            flush()
            for k in (0, 1):
                dve.tensor_reduce(wgat[:, HE + k * HEADS:HE + (k + 1) * HEADS],
                                  prod[:, k * HE:(k + 1) * HE].rearrange("p (h e) -> p h e", e=EXPERTS), AX.X, ALU.add)
            dve.tensor_tensor(bn[:, 5:6], bn[:, 5:6], bn[:, 1:2], ALU.mult)
            dve.tensor_tensor(bn[:, 6:7], bn[:, 0:1], bn[:, 3:4], ALU.subtract)
            flush()
            dve.tensor_tensor(bn[:, 6:7], bn[:, 6:7], bn[:, 5:6], ALU.mult)
            flush()
            dve.tensor_tensor(bn[:, 6:7], bn[:, 6:7], bn[:, 2:3], ALU.add).then_inc(bn_ready, 1)

            dve.wait_ge(samples_loaded, 16)
            dve.wait_ge(zeros_stored, 16 * (COLS * (HEADS + ST) // (P * LV)))
            half = P * LV // P
            for k in (0, 1):
                tg = target[:, k].bitcast(F32)
                for s in range(P // half):
                    v = found[:, :].rearrange("p (c s) -> p c s", s=P)
                    dve.tensor_tensor(v, over(samples[:, :], half), over(tg[:, s * half:(s + 1) * half], P, 2),
                                      ALU.is_lt)
                    flush()
                    dve.tensor_reduce(rank1[:, k, s * half:(s + 1) * half], v, AX.X, ALU.add)
                    flush()
            dve.tensor_scalar(rank1[:, :], rank1[:, :], float(P - 1), None, ALU.min)
            flush()
            dve.tensor_copy(row1[:, :], rank1[:, :]).then_inc(ranked, 1)

            def rank(n):
                level, k, h = n // 2 % 2, n // 4, n % 2
                cols = slice(h * P // 2, (h + 1) * P // 2)
                tg = target[:, k, cols].bitcast(F32)
                v = found[:, h * P // 2 * LV:(h + 1) * P // 2 * LV].rearrange("p (c s) -> p c s", s=LV)
                dve.wait_ge(rows_found[h], 16 * P // 2 * (n // 2 + 1))
                dve.tensor_tensor(v, v, over(tg, LV, 2), ALU.is_lt)
                flush()
                dve.tensor_reduce(rank2[:, k, cols], v, AX.X, ALU.add)
                flush()
                if level == 0:
                    dve.tensor_scalar(rank2[:, k, cols], rank2[:, k, cols], float(LV - 1), None, ALU.min)
                    flush()
                    dve.scalar_tensor_tensor(out=rank1[:, k, cols], in0=rank1[:, k, cols], scalar=float(LV),
                                             in1=rank2[:, k, cols], op0=ALU.mult, op1=ALU.add)
                    flush()
                    dve.tensor_copy(row2[:, k, cols], rank1[:, k, cols]).then_inc(ranked, 1)
                else:
                    dve.scalar_tensor_tensor(out=ends[:, k, cols], in0=rank1[:, k, cols], scalar=float(LV),
                                             in1=rank2[:, k, cols], op0=ALU.mult, op1=ALU.add).then_inc(ranked, 1)

            dve.wait_ge(keys_stored, 32)
            dve.wait_ge(levels_stored, 32)
            dve.memset(xi[:, 0:3 * C], 0.0)
            dve.memset(xi[:, (NY + 1) * 3 * C:], 0.0)
            for side in (0, P + 2):
                dve.memset(xnT[:, :, :, side:side + 2], 0.0)
            dve.memset(rT[CR:CR + 1], 1.0).then_inc(bn_ready, 1)
            flush()

            def statistics(k, rows, done):
                for r in range(ROWS):
                    dve.bn_stats(stats[:, k, r], rows(r))
                flush()
                for r in range(ROWS):
                    last = dve.bn_aggr(mv[:, k, r], stats[:, k, r])
                last.then_inc(done, 1)

            def first_stats(i, u, turn):
                dve.wait_ge(xa_in[u], 32 * (turn + 1))
                statistics(0, lambda r: xa[:, u, r], stats1)

            def first_norm(i, u):
                dve.wait_ge(root1, i + 1)
                dve.reciprocal(rstd[:, 0], sd[:, 0])
                flush()
                if some(i - 1):
                    dve.wait_ge(turned1, i - 1)
                for r in range(ROWS):
                    last = dve.tensor_scalar(xn[:, u, r], xa[:, u, r], mv[:, 0, r, 0:1],
                                             rstd[:, 0, r:r + 1], ALU.subtract, ALU.mult)
                last.then_inc(normed1, 1)

            def involve(c, u, r):
                patch = xi[:, ds((ROWS * c + r) * 3 * C, TAPS)]
                dve.tensor_tensor(prod[:, r % 2 * TAPS:(r % 2 + 1) * TAPS].rearrange("p (g f k) -> p g f k", g=GROUPS, k=KK),
                                  patch.rearrange("p (g f k) -> p g f k", g=GROUPS, k=KK),
                                  over(wv[:, u, r].rearrange("p (g k) -> p g k", k=KK), C // GROUPS, 2),
                                  ALU.mult)
                flush()
                dve.tensor_reduce(inv[:, r], prod[:, r % 2 * TAPS:(r % 2 + 1) * TAPS].rearrange("p (o k) -> p o k", k=KK),
                                  AX.X, ALU.add)

            def second_norm(i, u):
                dve.wait_ge(root2, i + 1)
                dve.reciprocal(rstd[:, 1], sd[:, 1])
                flush()
                if some(i):
                    dve.wait_ge(turned2, i)
                for r in range(ROWS):
                    last = dve.tensor_scalar(tn[:, r], xb[:, u, r], mv[:, 1, r, 0:1],
                                             rstd[:, 1, r:r + 1], ALU.subtract, ALU.mult)
                last.then_inc(normed2, 1)

            def conv_step(q, c2, u):
                c, i, turn = 2 * c2 + u, CHUNKS * q + 2 * c2 + u, CHUNKS // 2 * q + c2
                dve.wait_ge(xi_ready, ROWS * (i + 1) + (1 if more(i, 1) else 0))
                dve.wait_ge(w_ready, i + 1)
                involve(c, u, 0)
                if some(i):
                    second_norm(i - 1, 1 - u)
                if more(i, 2):
                    first_norm(i + 2, u)
                if more(i, 3):
                    first_stats(i + 3, 1 - u, turn + 1 + u)
                for r in range(1, ROWS):
                    involve(c, u, r)
                flush()
                dve.wait_ge(xb_in[u], 32 * (turn + 1))
                dve.tensor_tensor(xb[:, u], xb[:, u], inv[:, :], ALU.add)
                flush()
                statistics(1, lambda r: xb[:, u, r], conv_done)

            def c_(k):
                return cnt[:, k:k + 1]

            def order_ends(k):
                dve.wait_ge(ends_loaded, 16 * (5 + 4 * k))
                for a in (0, 1):
                    last = dve.tensor_copy(endO[:, a].rearrange("p (x a) -> p a x", a=2),
                                           endT[:, a].rearrange("p (a x) -> p a x", a=2))
                last.then_inc(ends_ordered, 1)

            def find_positions():
                dve.wait_ge(ends_taken, 1)
                per_step = float(2 * T * P)

                dve.tensor_scalar(cnti[:, 0:1], c_(0), 1.0 / per_step, None, ALU.mult)
                flush()
                dve.tensor_copy(c_(2), cnti[:, 0:1])
                flush()
                dve.scalar_tensor_tensor(out=c_(3), in0=c_(2), scalar=per_step, in1=c_(0), op0=ALU.mult, op1=ALU.is_lt)
                flush()
                dve.tensor_tensor(c_(2), c_(2), c_(3), ALU.add)
                flush()
                dve.tensor_scalar(c_(4), c_(2), 1.0, per_step, ALU.subtract, ALU.mult)
                flush()
                dve.tensor_tensor(c_(3), c_(4), c_(0), ALU.is_ge)
                flush()
                dve.tensor_tensor(c_(2), c_(2), c_(3), ALU.subtract)
                flush()
                dve.tensor_scalar(c_(2), c_(2), float(MIN_STEPS), None, ALU.max)
                flush()
                dve.tensor_scalar(c_(4), c_(2), float(2 * T), None, ALU.mult)
                flush()
                dve.tensor_scalar(c_(5), c_(4), -1.0, float(COLS), ALU.mult, ALU.add)
                dve.reciprocal(c_(6), c_(4))
                dve.tensor_copy(cnti[:, 0:1], c_(2))
                dve.tensor_scalar(cnti[:, 2:3], c_(2), float(PAIRS * CHUNKS // 4), -1.0, ALU.min, ALU.add)
                dve.tensor_scalar(cnti[:, 3:4], c_(2), float(PAIRS * CHUNKS // 4), -2.0, ALU.min, ALU.add)
                dve.tensor_scalar(keys_at[:, :], partf[:, :], c_(2), None, ALU.mult)
                dve.tensor_scalar(border_f[:, 0:1], partf[:, :], 1.0, c_(4), ALU.add, ALU.mult)
                dve.tensor_scalar(border_f[:, 1:2], partf[:, :], c_(4), None, ALU.mult)
                dve.tensor_scalar(c_(7), partf[:, :], 0.0, SKIP, ALU.is_equal, ALU.mult)
                flush()
                dve.tensor_scalar(border_at[:, 0:1], border_f[:, 0:1], -1.0, None, ALU.add)
                dve.scalar_tensor_tensor(out=border_at[:, 1:2], in0=border_f[:, 1:2], scalar=-1.0, in1=c_(7),
                                         op0=ALU.add, op1=ALU.add).then_inc(counted, 1)
                dve.tensor_tensor(nonempty[:, 0], endG[:, 0], endG[:, 1], ALU.is_gt)
                dve.tensor_scalar(pos[:, 0], endG[:, 0], 1.0, None, ALU.subtract)
                dve.tensor_copy(pos[:, 1], endG[:, 1])
                flush()
                dve.tensor_scalar(quoi[:, :], pos[:, :], c_(6), None, ALU.mult)
                flush()
                dve.tensor_copy(quo[:, :], quoi[:, :])
                flush()
                dve.scalar_tensor_tensor(out=fit[:, :], in0=quo[:, :], scalar=c_(4), in1=pos[:, :], op0=ALU.mult, op1=ALU.is_gt)
                flush()
                dve.tensor_tensor(quo[:, :], quo[:, :], fit[:, :], ALU.subtract)
                flush()
                dve.tensor_scalar(fit[:, :], quo[:, :], 1.0, c_(4), ALU.add, ALU.mult)
                flush()
                dve.tensor_tensor(fit[:, :], fit[:, :], pos[:, :], ALU.is_le)
                flush()
                dve.tensor_tensor(quo[:, :], quo[:, :], fit[:, :], ALU.add)
                flush()
                dve.scalar_tensor_tensor(out=pos[:, :], in0=quo[:, :], scalar=c_(5), in1=pos[:, :], op0=ALU.mult, op1=ALU.add)
                flush()
                dve.scalar_tensor_tensor(out=pos[:, :], in0=pos[:, :], scalar=-SKIP,
                                         in1=over(nonempty[:, 0], 2), op0=ALU.add, op1=ALU.mult)
                flush()
                dve.tensor_scalar(posi[:, :], pos[:, :], SKIP, None, ALU.add).then_inc(grid_ready, 1)

            for u in (0, 1):
                first_stats(u, u, 0)
                first_norm(u, u)
            first_stats(2, 0, 1)
            for n in range(8):
                over_chunks(dve, conv_step, 2 * n, 2 * n + 2)
                if n == 7:
                    second_norm(PAIRS * CHUNKS - 1, 1)
                rank(n)
                if n == 4:
                    order_ends(0)
                if n == 5:
                    find_positions()
                    flush()

            dve.memset(edge_i[:, 2:3], 0).then_inc(prev_zero, 1)
            dve.memset(ones[:, :], 1.0).then_inc(ones_ready, 1)

            def new_sources(k, u):
                if u == 0:
                    dve.wait_ge(keys_in, 16 * (k + 1))
                dve.tensor_scalar(srcs[:, u], keyb[:, 1 + u * T:1 + (u + 1) * T], M - 1, None, ALU.bitwise_and)
                dve.tensor_scalar(clsi[:, :], keyb[:, u * T:1 + (u + 1) * T], SRC_BITS, None, ALU.logical_shift_right)
                if u == 1:
                    dve.tensor_copy(keyb[:, 0:1], keyb[:, 2 * T:])
                    dve.tensor_scalar(keys_at[:, :], keys_at[:, :], 1, None, ALU.add)
                flush()
                dve.tensor_tensor(same[:, u], clsi[:, 1:], clsi[:, :T], ALU.is_equal)
                flush()
                dve.tensor_scalar(reset[:, u], same[:, u], -1.0, BIG, ALU.add, ALU.mult).then_inc(sources_ready, 1)

            order_ends(1)
            dve.wait_ge(border_found, 48)
            dve.wait_ge(border_loaded, 16)
            dve.tensor_scalar(edge_i[:, 3:6], edge_i[:, 0:3], SRC_BITS, None, ALU.logical_shift_right)
            dve.tensor_scalar(chk[:, :], chk[:, :], SRC_BITS, None, ALU.logical_shift_right)
            flush()

            def e_(k):
                return edge_f[:, k:k + 1]

            dve.tensor_scalar(edge_f[:, 0:3], edge_i[:, 3:6], float(-KEY_BASE), None, ALU.add)
            dve.tensor_copy(chf[:, 0:2], chk[:, :])
            flush()
            dve.tensor_scalar(edge_i[:, 8:9], e_(0), 1.0, float(M), ALU.add, ALU.min)
            dve.tensor_scalar(edge_i[:, 6:7], e_(0), float(M - 1), None, ALU.min).then_inc(border_ready, 1)
            for u in (0, 1):
                new_sources(0, u)
            dve.memset(df[:, T], 0.0)
            dve.memset(state[:, 1, T, 0:HEADS], -BIG)
            dve.memset(state[:, 1, T, HEADS:ST], 0.0)
            flush()

            steps = dve.value_load(cnti[0:1, 0:1], min_val=MIN_STEPS, max_val=COLS // (2 * T))

            def edge_scans(k):
                for u in (0, 1):
                    dve.tensor_copy(df[:, 0], df[:, T])
                    if some(k):
                        dve.wait_ge(state_out[u], 16 * k)
                    dve.tensor_copy(state[:, u, 0], state[:, 1 - u, T])
                    flush()
                    dve.wait_ge(dch_in[u], 16 * (k + 1))
                    for h in range(HEADS):
                        last = dve.tensor_tensor_scan(df[:, 1:, h], same[:, u], dch[:, u, :, h],
                                                      df[:, 0, h:h + 1], ALU.mult, ALU.add)
                    last.then_inc(dch_used[u], 1)
                    flush()
                    dve.wait_ge(rows_in[u], 16 * T * (k + 1))
                    dve.tensor_tensor(score[:, :, :], rows_g[:, u, :, HE:ROW], df[:, 1:], ALU.add)
                    flush()
                    dve.scalar_tensor_tensor(out=score[:, :, :], in0=score[:, :, :], scalar=0.2,
                                             in1=score[:, :, :], op0=ALU.mult, op1=ALU.max)
                    flush()
                    for h in range(HEADS):
                        dve.tensor_tensor_scan(state[:, u, 1:, h], reset[:, u], score[:, :, h],
                                               state[:, u, 0, h:h + 1], ALU.add, ALU.max)
                    flush()
                    dve.tensor_tensor(ex[:, :, 0], state[:, u, 0:T, 0:HEADS], state[:, u, 1:, 0:HEADS], ALU.subtract)
                    dve.tensor_tensor(ex[:, :, 1], score[:, :, :], state[:, u, 1:, 0:HEADS], ALU.subtract)
                    flush()
                    dve.tensor_tensor(ex[:, :, 0], ex[:, :, 0], over(reset[:, u], HEADS, 2),
                                      ALU.add).then_inc(scored, 1)
                    dve.wait_ge(weighed, 2 * k + u + 1)
                    dve.tensor_tensor(pv[:, :, :].rearrange("p t (h e) -> p t h e", e=EXPERTS),
                                      rows_g[:, u, :, 0:HE].rearrange("p t (h e) -> p t h e", e=EXPERTS),
                                      over(ex[:, :, 1], EXPERTS, 3), ALU.mult)
                    flush()
                    for h in range(HEADS):
                        for e in range(-1, EXPERTS):
                            f = HEADS + h if e < 0 else 2 * HEADS + EXPERTS * h + e
                            new = ex[:, :, 1, h] if e < 0 else pv[:, :, EXPERTS * h + e]
                            last = dve.tensor_tensor_scan(state[:, u, 1:, f], ex[:, :, 0, h], new,
                                                          state[:, u, 0, f:f + 1], ALU.mult, ALU.add)
                    last.then_inc(state_ready, 1)
                    flush()
                    new_sources(k + 1, u)

            edge_scans(0)
            with dve.Fori(1, steps) as k:
                edge_scans(k)

            dve.tensor_tensor(chf[:, 2], chf[:, 0], chf[:, 1], ALU.is_equal)
            dve.memset(chf[:, 3, 0:1], 0.0)
            dve.tensor_tensor(chf[:, 3, 1:], chf[:, 0, 1:], chf[:, 1, :P - 1], ALU.is_equal)
            flush()
            dve.tensor_tensor(chf[:, 2], chf[:, 2], chf[:, 3], ALU.mult)
            flush()
            dve.tensor_scalar(chf[:, 4], chf[:, 2], -1.0, BIG, ALU.add, ALU.mult)
            dve.wait_ge(tails_loaded, 16)
            dve.memset(chx[:, 0, 0:HEADS], -BIG)
            dve.memset(chx[:, 0, HEADS:ST], 0.0)
            flush()
            for h in range(HEADS):
                dve.tensor_tensor_scan(chx[:, 1:, h], chf[:, 4], tails[:, :, h], chx[:, 0, h:h + 1],
                                       ALU.add, ALU.max)
            flush()
            dve.tensor_tensor(che[:, :, 0], chx[:, 0:P, 0:HEADS], chx[:, 1:, 0:HEADS], ALU.subtract)
            dve.tensor_tensor(che[:, :, 1], tails[:, :, 0:HEADS], chx[:, 1:, 0:HEADS], ALU.subtract)
            flush()
            dve.tensor_tensor(che[:, :, 0], che[:, :, 0], over(chf[:, 4], HEADS, 2), ALU.add).then_inc(chain_scored, 1)
            dve.wait_ge(chain_weighed, 1)
            dve.tensor_tensor(chp[:, :, 0:HEADS], tails[:, :, HEADS:2 * HEADS], che[:, :, 1], ALU.mult)
            dve.tensor_tensor(chp[:, :, HEADS:].rearrange("p t (h e) -> p t h e", e=EXPERTS),
                              tails[:, :, 2 * HEADS:].rearrange("p t (h e) -> p t h e", e=EXPERTS),
                              over(che[:, :, 1], EXPERTS, 3), ALU.mult)
            flush()
            for h in range(HEADS):
                for e in range(-1, EXPERTS):
                    f = HEADS + h if e < 0 else 2 * HEADS + EXPERTS * h + e
                    last = dve.tensor_tensor_scan(chx[:, 1:, f], che[:, :, 0, h], chp[:, :, f - HEADS],
                                                  chx[:, 0, f:f + 1], ALU.mult, ALU.add)
            last.then_inc(chain_ready, 1)

            dve.memset(fixs[:, :], 0.0)
            dve.wait_ge(end_found, 16)
            dve.tensor_scalar(e_(3), endf[:, :], 1.0, None, ALU.subtract)
            dve.tensor_tensor(e_(4), e_(0), e_(2), ALU.is_equal)
            dve.tensor_scalar(e_(5), e_(0), float(M), None, ALU.is_lt)
            dve.tensor_scalar(e_(6), partf[:, :], 1.0, c_(4), ALU.add, ALU.mult)
            dve.tensor_scalar(e_(7), partf[:, :], c_(5), None, ALU.mult)
            flush()
            dve.tensor_tensor(e_(4), e_(4), e_(5), ALU.mult)
            dve.tensor_tensor(e_(6), e_(3), e_(6), ALU.is_lt)
            dve.scalar_tensor_tensor(out=e_(7), in0=e_(3), scalar=-SKIP, in1=e_(7), op0=ALU.add, op1=ALU.add)
            flush()
            dve.tensor_tensor(e_(4), e_(4), e_(6), ALU.mult)
            flush()
            dve.tensor_tensor(e_(7), e_(7), e_(4), ALU.mult)
            flush()
            dve.tensor_scalar(edge_i[:, 7:8], e_(7), SKIP, None, ALU.add).then_inc(fix_placed, 1)
            dve.memset(agg[:, :, 0:HEADS], -BIG)
            dve.memset(agg[:, :, HEADS:ST], 0.0).then_inc(agg_cleared, 1)
            dve.wait_ge(fix_got, 16)
            dve.wait_ge(cprev_loaded, 16)
            dve.tensor_tensor(fixo[:, 0:HEADS], cprev[:, 0:HEADS], fixs[:, 0:HEADS], ALU.max)
            flush()
            dve.tensor_tensor(fixe[:, 0], cprev[:, 0:HEADS], fixo[:, 0:HEADS], ALU.subtract)
            dve.tensor_tensor(fixe[:, 1], fixs[:, 0:HEADS], fixo[:, 0:HEADS], ALU.subtract).then_inc(fix_scored, 1)
            dve.wait_ge(fix_weighed, 1)
            for z, a in ((cprev, 0), (fixs, 1)):
                dve.tensor_tensor(z[:, HEADS:2 * HEADS], z[:, HEADS:2 * HEADS], fixe[:, a], ALU.mult)
                dve.tensor_tensor(z[:, 2 * HEADS:].rearrange("p (h e) -> p h e", e=EXPERTS),
                                  z[:, 2 * HEADS:].rearrange("p (h e) -> p h e", e=EXPERTS),
                                  over(fixe[:, a], EXPERTS, 2), ALU.mult)
            flush()
            dve.tensor_tensor(fixo[:, HEADS:], cprev[:, HEADS:], fixs[:, HEADS:], ALU.add).then_inc(fix_ready, 1)

            dve.wait_ge(late_loaded, 16 * (1 + len(late_params())))
            a_src, a_dst, h_all = node[:, :, HE:ROW], node[:, :, ROW:NODE], node[:, :, 0:HE]
            n_sink, lone = one4[:, 2], one4[:, 3]
            dve.tensor_tensor(hx[:, 1], a_src, a_dst, ALU.add)
            dve.tensor_tensor(hx[:, 2], a_dst, over(last_row[:, HE:ROW], TILES), ALU.add)
            dve.tensor_tensor(n_sink, endG[:, 2], endG[:, 3], ALU.subtract)
            flush()
            for k in (1, 2):
                dve.scalar_tensor_tensor(out=hx[:, k], in0=hx[:, k], scalar=0.2, in1=hx[:, k],
                                         op0=ALU.mult, op1=ALU.max)
            dve.tensor_scalar(lone, n_sink, 0.0, -BIG, ALU.is_equal, ALU.mult)
            flush()
            dve.tensor_tensor(hx[:, 2], hx[:, 2], over(lone, HEADS, 2), ALU.add)
            flush()
            dve.tensor_tensor(hx[:, 3], hx[:, 1], hx[:, 2], ALU.max)
            dve.wait_ge(agg_got, 16 * TILES)
            flush()
            dve.tensor_tensor(hx[:, 3], hx[:, 3], agg[:, :, 0:HEADS], ALU.max)
            flush()
            dve.tensor_tensor(hx[:, 0], agg[:, :, 0:HEADS], hx[:, 3], ALU.subtract)
            dve.tensor_tensor(hx[:, 1], hx[:, 1], hx[:, 3], ALU.subtract)
            dve.tensor_tensor(hx[:, 2], hx[:, 2], hx[:, 3], ALU.subtract).then_inc(joined, 1)
            dve.wait_ge(join_weighed, 1)
            dve.tensor_tensor(hx[:, 2], hx[:, 2], over(n_sink, HEADS, 2), ALU.mult)
            dve.tensor_tensor(hx[:, 3], hx[:, 0], agg[:, :, HEADS:2 * HEADS], ALU.mult)

            def heads(v):
                return v.rearrange("p t (h e) -> p t h e", e=EXPERTS)

            dve.tensor_tensor(heads(wide[:, 0]), heads(agg[:, :, 2 * HEADS:]), over(hx[:, 0], EXPERTS, 3), ALU.mult)
            dve.tensor_tensor(heads(wide[:, 1]), heads(h_all), over(hx[:, 1], EXPERTS, 3), ALU.mult)
            flush()
            dve.tensor_tensor(wide[:, 0], wide[:, 0], wide[:, 1], ALU.add)
            dve.tensor_tensor(hx[:, 3], hx[:, 3], hx[:, 1], ALU.add)
            flush()
            dve.tensor_tensor(heads(wide[:, 1]), heads(over(last_row[:, 0:HE], TILES)), over(hx[:, 2], EXPERTS, 3), ALU.mult)
            dve.scalar_tensor_tensor(out=hx[:, 3], in0=hx[:, 3], scalar=1e-16, in1=hx[:, 2], op0=ALU.add, op1=ALU.add)
            flush()
            dve.tensor_tensor(wide[:, 0], wide[:, 0], wide[:, 1], ALU.add)
            dve.reciprocal(hx[:, 3], hx[:, 3])
            flush()
            dve.tensor_tensor(heads(wide[:, 0]), heads(wide[:, 0]), over(hx[:, 3], EXPERTS, 3), ALU.mult)
            flush()
            dve.tensor_tensor(wide[:, 0], wide[:, 0], over(gat_p[:, 0], TILES), ALU.add)
            flush()
            dve.tensor_reduce(one4[:, 0], wide[:, 0], AX.X, ALU.add)
            flush()
            dve.tensor_scalar(one4[:, 0], one4[:, 0], 1.0 / HE, None, ALU.mult)
            flush()
            dve.tensor_tensor(wide[:, 0], wide[:, 0], over(one4[:, 0], HE, 2), ALU.subtract)
            flush()
            dve.tensor_tensor(wide[:, 1], wide[:, 0], wide[:, 0], ALU.mult)
            flush()
            dve.tensor_reduce(one4[:, 0], wide[:, 1], AX.X, ALU.add)
            flush()
            dve.tensor_scalar(one4[:, 0], one4[:, 0], 1.0 / HE, None, ALU.mult).then_inc(agg_var, 1)
            dve.wait_ge(agg_root, 1)
            dve.reciprocal(one4[:, 1], one4[:, 1])
            flush()
            dve.tensor_tensor(wide[:, 0], wide[:, 0], over(one4[:, 1], HE, 2), ALU.mult)
            flush()
            dve.tensor_tensor(wide[:, 0], wide[:, 0], over(gat_p[:, 1], TILES), ALU.mult)
            flush()
            dve.tensor_tensor(wide[:, 0], wide[:, 0], over(gat_p[:, 2], TILES), ALU.add)
            flush()
            dve.tensor_reduce(hx[:, 0], wide[:, 0].rearrange("p t (h e) -> p t e h", e=EXPERTS), AX.X, ALU.add)
            flush()
            dve.tensor_scalar(hx[:, 0], hx[:, 0], 1.0 / HEADS, None, ALU.mult)
            flush()

            def pick(scores, best, chosen, taken):
                dve.tensor_reduce(best, scores, AX.X, ALU.max)
                flush()
                dve.tensor_tensor(chosen, scores, over(best, EXPERTS, 2), ALU.is_equal)
                dve.memset(taken, 1.0)
                flush()
                for e in range(EXPERTS):
                    dve.tensor_tensor(chosen[:, :, e], chosen[:, :, e], taken, ALU.mult)
                    flush()
                    dve.tensor_tensor(taken, taken, chosen[:, :, e], ALU.subtract)
                    flush()

            pick(hx[:, 0], one4[:, 1], hx[:, 1], one4[:, 2])
            dve.scalar_tensor_tensor(out=hx[:, 0], in0=hx[:, 1], scalar=-BIG, in1=hx[:, 0], op0=ALU.mult, op1=ALU.add)
            flush()
            pick(hx[:, 0], one4[:, 0], hx[:, 2], one4[:, 2])
            dve.tensor_tensor(one4[:, 0], one4[:, 0], one4[:, 1], ALU.subtract).then_inc(top_ready, 1)
            dve.wait_ge(top_weighed, 1)
            dve.tensor_scalar(one4[:, 2], one4[:, 1], 1.0, None, ALU.add)
            flush()
            dve.reciprocal(one4[:, 2], one4[:, 2])
            flush()
            dve.tensor_tensor(one4[:, 3], one4[:, 1], one4[:, 2], ALU.mult)
            dve.tensor_tensor(hx[:, 1], hx[:, 1], over(one4[:, 2], EXPERTS, 2), ALU.mult)
            flush()
            dve.tensor_tensor(hx[:, 2], hx[:, 2], over(one4[:, 3], EXPERTS, 2), ALU.mult)
            flush()
            dve.tensor_tensor(gate[:, :, :], hx[:, 1], hx[:, 2], ALU.add).then_inc(gates_ready, 1)
            flush()

            def mix(g, b, turn):
                dve.wait_ge(tokens_in[b], 32 * (turn + 1))
                for e in range(EXPERTS):
                    for r in range(ROWS):
                        acc = x2_in[:, b, r * C:(r + 1) * C]
                        last = dve.scalar_tensor_tensor(
                            out=acc, in0=hid_y[:, b, (r * EXPERTS + e) * C:(r * EXPERTS + e + 1) * C],
                            scalar=gate[:, ds(ROWS * g + r, 1), e], in1=acc, op0=ALU.mult, op1=ALU.add)
                    if e < EXPERTS - 1:
                        flush()
                last.then_inc(mixed, 1)

            with dve.Fori(0, PAIRS * CHUNKS // 4) as g4:
                for b in range(4):
                    mix(4 * g4 + b, b, g4)


_NAMES = ['x', 'L0_conv_Wr', 'L0_conv_br', 'L0_conv_gamma', 'L0_conv_beta', 'L0_conv_mean',
          'L0_conv_var', 'L0_conv_Ws', 'L0_conv_bs', 'L0_conv_Wi', 'L0_conv_bi', 'L0_ffn_W_gat',
          'L0_ffn_att_src', 'L0_ffn_att_dst', 'L0_ffn_b_gat', 'L0_ffn_ln_gamma',
          'L0_ffn_ln_beta', 'L0_ffn_W1', 'L0_ffn_b1', 'L0_ffn_W2', 'L0_ffn_b2',
          'L0_ffn_edge_index']


def kernel(**inputs):
    import numpy as np
    import concourse.bacc as bacc
    from concourse.bass_utils import run_bass_kernel_spmd

    nc = bacc.Bacc("TRN2", target_bir_lowering=False, num_devices=1)
    arrays, args = {}, []
    for name in _NAMES:
        a = np.ascontiguousarray(inputs[name])
        arrays[f"in_{name}"] = a
        args.append(nc.dram_tensor(f"in_{name}", a.shape, mybir.dt.from_np(a.dtype),
                                   kind="ExternalInput").ap())
    out = nc.dram_tensor("out_x", (NB, NY, NX, C), F32, kind="ExternalOutput").ap()
    metaformer_block(nc, *args, out)
    result = run_bass_kernel_spmd(nc, [arrays], core_ids=[0])
    return result.results[0]["out_x"]
```

```python
from contextlib import ExitStack

import concourse.bass as bass
from concourse import mybir

F32 = mybir.dt.float32
BF16 = mybir.dt.bfloat16
I32 = mybir.dt.int32
ALU = mybir.AluOpType
ACT = mybir.ActivationFunctionType
AX = mybir.AxisListType

P = 128
NB, NY, NX, C = 4, 64, 64, 128
M = NB * NY * NX
PAIRS = NB // 2
TILES = M // P
EDGES = 524288
COLS = EDGES // P
LOG_E, LOG_C = 19, 12
SRC_BITS = 14
SINK = M
KEY_BASE = 2 * M
DROPPED = 3 * M
KK, GROUPS = 9, 16
TAPS = KK * C
CR = 32
HEADS, EXPERTS, HID = 4, 4, 256
HE = HEADS * EXPERTS
ROW = HE + HEADS
NODE = ROW + HEADS
ST = 2 * HEADS + HE
QUARTER = COLS // 4
QUARTERS = (0, 2, 1, 3)
T = 64
MIN_STEPS = 3
MOST_SHARED = 6
ROUTES = 4
SCALED = 2
BIG = 1.0e30
ROWS = 4
CHUNKS = NY // ROWS
TOK = ROWS * P
LV = 64
SKIP = float(1 << 20)
TR, FA = True, False


def some(n):
    return not isinstance(n, int) or n > 0


def metaformer_block(nc, x, Wr, br, gamma, beta, mean, var, Ws, bs, Wi, bi,
                     W_gat, att_src, att_dst, b_gat, ln_gamma, ln_beta,
                     W1, b1, W2, b2, edge_index, out):
    ctx = ExitStack()
    with ctx:
        def sb(name, shape, dt=F32, where=ctx):
            return where.enter_context(nc.sbuf_tensor("sb_" + name, shape, dt))

        def dram(name, shape, dt=F32):
            return nc.dram_tensor("scr_" + name, shape, dt, kind="Internal").ap()

        def sem(name):
            return ctx.enter_context(nc.semaphore(name))

        ds = bass.ds

        keys_d = dram("keys", [EDGES + COLS])
        borders_d = dram("borders", [P, 2], I32)
        level1_d = dram("level1", [P])
        level2_d = dram("level2", [P, LV])
        ends_d = dram("ends", [2, M + 1])
        node_d = dram("node", [M, ROW])
        adst_d = dram("adst", [M, HEADS])
        starts_d = dram("adst_at_starts", [EDGES, HEADS])
        state_d = dram("state", [EDGES, ST])
        tails_d = dram("tails", [P, ST])
        chain_d = dram("chain", [P + 1, ST])
        x2_d = dram("x2", [PAIRS * CHUNKS, P, TOK])
        tnT_d = dram("tnT", [PAIRS * CHUNKS + 2, C, TOK])
        y_d = dram("expert_out", [PAIRS * CHUNKS, P, ROWS * EXPERTS * C])

        ident = sb("ident", [P, P])
        node = sb("node", [P, TILES, NODE])
        part = sb("part", [P, 1], I32)
        partf = sb("partf", [P, 1])
        sign_i = sb("sign_i", [P, LOG_E - LOG_C], I32)
        signs = sb("signs", [P, LOG_E - LOG_C])
        wr = sb("wr", [C, CR])
        ws = sb("ws", [CR + 1, KK * GROUPS])
        wi = sb("wi", [C, C])
        valid = sb("valid", [3, NX, 2])
        valid9 = sb("valid9", [9, NX * 2], BF16)
        bi9 = sb("bi9", [9, 3 * C], BF16)
        bn = sb("bn", [CR, 8])
        wgat = sb("wgat", [C, NODE])
        att = sb("att", [P, 2, HE])
        eps = sb("eps", [P, 3])
        ends = sb("ends", [P, 2, P])
        endT = sb("endT", [P, 2, P])
        endO = sb("endO", [P, 2, P])
        endG = sb("endG", [P, 4, TILES])
        posi = sb("posi", [P, 2, TILES], I32)
        cnt = sb("cnt", [P, 8])
        cnti = sb("cnti", [P, 4], I32)
        keys_at = sb("keys_at", [P, 1], I32)
        border_f = sb("border_f", [P, 2])
        border_at = sb("border_at", [P, 2], I32)
        srcs = sb("srcs", [P, 2, T], I32)
        step_i = sb("step_i", [P, 2, T], I32)
        no_offset = sb("no_offset", [P, T], I32)
        clsi = sb("clsi", [P, T + 1], I32)
        same = sb("same", [P, 2, T])
        reset = sb("reset", [P, 2, T])
        edge_i = sb("edge_i", [P, 10], I32)
        edge_f = sb("edge_f", [P, 12])
        adst0 = sb("adst0", [P, HEADS])
        endf = sb("endf", [P, 1])
        keyb = sb("keyb", [P, 1 + 2 * T], I32)

        bank = [ctx.enter_context(nc.psum_tensor(f"bank{i}", [P, 512], F32)) for i in range(8)]

        early = ExitStack()
        xi = sb("xi", [P, (NY + 2) * 3 * C], F32, early)
        xa = sb("xa", [P, 2, ROWS, C], F32, early)
        xb = sb("xb", [P, 2, ROWS, C], F32, early)
        xn = sb("xn", [P, 2, ROWS, C], F32, early)
        xnT = sb("xnT", [C, 2, ROWS, P + 4], F32, early)
        rT = sb("rT", [CR + 1, 2, TOK], F32, early)
        wv = sb("wv", [P, 2, ROWS, KK * GROUPS], F32, early)
        prod2 = sb("prod", [P, 2 * TAPS], F32, early)
        prod = prod2[:, :]
        prod_pe = sb("prod_pe", [P, TAPS], F32, early)
        inv = sb("inv", [P, ROWS, C], F32, early)
        tn = sb("tn", [P, ROWS, C], F32, early)
        tnT = sb("tnT", [C, 2, TOK], F32, early)
        stats = sb("stats", [P, 2, ROWS, 6], F32, early)
        mv = sb("mv", [P, 2, ROWS, 2], F32, early)
        sd = sb("sd", [P, 2, ROWS], F32, early)
        rstd = sb("rstd", [P, 2, ROWS], F32, early)
        found = sb("found", [P, P * LV], F32, early)
        samples = sb("samples", [P, P], F32, early)
        target = sb("target", [P, 2, P], I32, early)
        rank1 = sb("rank1", [P, 2, P], F32, early)
        row_at = sb("row_at", [P, 2, P], I32, early)
        lvl2 = sb("lvl2", [P, LV], F32, early)
        zero = sb("zero", [1, 1], F32, early)
        key_bufs = [xi[:, 0:COLS], xi[:, COLS:2 * COLS]]
        tmp_a, tmp_b = xi[:, 2 * COLS:3 * COLS], xi[:, 3 * COLS:4 * COLS]
        bi3 = tn[0:3].rearrange("p r f -> p (r f)")[:, 0:3 * C]
        valid_b = tnT[0:3, 0, 0:P // 2].bitcast(BF16)
        bi_parts = [tnT[0:3, 1, 192 * k:192 * (k + 1)].bitcast(BF16) for k in range(2)] + [
            tnT[0:3, 0, 128:320].bitcast(BF16)]
        bi_left = prod2[0:3, 128:128 + 3 * C]
        pos, quo, fit = (prod[:, 2 * TILES * k:2 * TILES * (k + 1)].rearrange("p (a t) -> p a t", a=2)
                         for k in range(3))
        quoi = prod[:, 6 * TILES:8 * TILES].bitcast(I32).rearrange("p (a t) -> p a t", a=2)
        nonempty = prod[:, 8 * TILES:9 * TILES].unsqueeze(1)
        early.close()

        rows_g = sb("rows_g", [P, 2, T, ROW])
        dch = sb("dch", [P, 2, T, HEADS])
        df = sb("df", [P, T + 1, HEADS])
        score = sb("score", [P, T, HEADS])
        ex = sb("ex", [P, T, 2, HEADS])
        pv = sb("pv", [P, T, HE])
        state = sb("state", [P, 2, T + 1, ST])
        chk = sb("chk", [1, 2, P], I32)
        chf = sb("chf", [1, 5, P])
        cprev = sb("cprev", [P, ST])
        fixs = sb("fixs", [P, ST])
        fixo = sb("fixo", [P, ST])
        fixe = sb("fixe", [P, 2, HEADS])
        last_row = sb("last_row", [P, ROW])
        gat_p = sb("gat_p", [P, 3, HE])
        agg = sb("agg", [P, TILES, ST])
        one4 = sb("one4", [P, 4, TILES])
        gate = sb("gate", [P, TILES, EXPERTS])
        w1 = sb("w1", [C, EXPERTS, HID])
        w2 = sb("w2", [P, EXPERTS, 2, C])
        b1c = sb("b1c", [P, EXPERTS, 2])
        b2r = sb("b2r", [1, EXPERTS * C])
        ones = sb("ones", [1, P])
        late = sb("late", [P, 2 * TILES * HE + 5 * TILES * HEADS])
        tnT_in = sb("tnT_in", [C, 2, TOK])
        hid_y = sb("hid_y", [P, 4, ROWS * EXPERTS * C])
        y_new = sb("y_new", [P, 2, ROWS, EXPERTS * C])
        x2_in = sb("x2_in", [P, 4, TOK])
        hid = [hid_y[:, 2 * u:2 * u + 2].rearrange("p b (a t) -> p (b a) t", t=TOK) for u in (0, 1)]
        tails = late[0:1, 0:P * ST].rearrange("p (n f) -> p n f", f=ST)
        chx = late[0:1, P * ST:(2 * P + 1) * ST].rearrange("p (n f) -> p n f", f=ST)
        chp = agg[0:1].rearrange("p t f -> p (t f)")[:, 0:P * ROW].rearrange("p (n f) -> p n f", f=ROW)
        che = pv[0:1].rearrange("p t f -> p (t f)").rearrange("p (n a h) -> p n a h", a=2, h=HEADS)
        wide = late[:, 0:2 * TILES * HE].rearrange("p (a t f) -> p a t f", a=2, f=HE)
        hx = late[:, 2 * TILES * HE:].rearrange("p (a t h) -> p a t h", a=5, h=HEADS)

        def sems(names):
            return [sem(n) for n in names.split()]

        (ident_zero, consts_made, dst_loaded, src_loaded, params_loaded, small_ready,
         bn_root, bn_ready, found_zero, zeros_stored, bias_split, bias_placed) = sems(
            "ident_zero consts_made dst_loaded src_loaded params_loaded small_ready "
            "bn_root bn_ready found_zero zeros_stored bias_split bias_placed")
        (phase_sorted, flipped, act_placed, keys_final, keys_stored, levels_stored,
         samples_loaded, ranked) = sems(
            "phase_sorted flipped act_placed keys_final keys_stored levels_stored "
            "samples_loaded ranked")
        rows_found = sems("rows_found0 rows_found1")
        (row0_ready, sum_psum, sum_ready, stats1, root1, normed1, turned1, xnT_ready, r_psum, rT_ready, xi_psum, xi_ready,
         w_psum, w_ready, conv_done, root2, normed2, turned2, tnT_ready,
         node_psum, node_ready) = sems(
            "row0_ready sum_psum sum_ready stats1 root1 normed1 turned1 xnT_ready r_psum rT_ready xi_psum xi_ready "
            "w_psum w_ready conv_done root2 normed2 turned2 tnT_ready "
            "node_psum node_ready")
        xa_in, xb_in, x2_out, tnT_out = (sems(f"{n}0 {n}1") for n in
                                         ("xa_in", "xb_in", "x2_out", "tnT_out"))
        (node_stored, ends_stored, ends_loaded, ends_ordered, ends_turned, ends_taken, counted, keys_in,
         prev_zero, border_found, border_stored, border_loaded, border_ready, adst0_loaded, sources_ready,
         grid_ready, starts_scattered, first_stored) = sems(
            "node_stored ends_stored ends_loaded ends_ordered ends_turned ends_taken counted keys_in "
            "prev_zero border_found border_stored border_loaded border_ready adst0_loaded sources_ready "
            "grid_ready starts_scattered first_stored")
        dch_in, dch_used, rows_in, state_out, tnT_back, y_out = (
            sems(f"{n}0 {n}1") for n in ("dch_in", "dch_used", "rows_in", "state_out", "tnT_back", "y_out"))
        (scored, weighed, state_ready, tails_stored, tails_loaded, chain_scored, chain_weighed,
         chain_ready, chain_stored, cprev_loaded, end_found, fix_placed, fix_got, fix_scored,
         fix_weighed, fix_ready, fix_stored, agg_cleared) = sems(
            "scored weighed state_ready tails_stored tails_loaded chain_scored chain_weighed "
            "chain_ready chain_stored cprev_loaded end_found fix_placed fix_got fix_scored "
            "fix_weighed fix_ready fix_stored agg_cleared")
        agg_got = [sem(f"agg_got{q}") for q in range(ROUTES)]
        (ones_ready, own_scored, own_weighed, late_loaded, joined, join_weighed, agg_var, agg_root, top_ready, top_weighed,
         hid_psum, hid_ready, y_psum, y_taken, y_scaled, routed, mixed) = sems(
            "ones_ready own_scored own_weighed late_loaded joined join_weighed agg_var agg_root top_ready top_weighed "
            "hid_psum hid_ready y_psum y_taken y_scaled routed mixed")
        tokens_in, out_stored = (sems(f"{n}0 {n}1 {n}2 {n}3") for n in ("tokens_in", "out_stored"))

        def pair_rows(t, q, i2, c):
            return t[2 * q + i2, ds(c * ROWS, ROWS), :, :].rearrange("r x f -> x r f")

        def by_tile(t, i):
            return t.rearrange("(q a y x) -> q y a x", q=PAIRS, a=2, x=NX)[i]

        starts_runs = starts_d.rearrange("(p c) h -> p c h", p=P)
        state_runs = state_d.rearrange("(p c) f -> p c f", p=P)
        key_rows = keys_d.rearrange("(r k) -> r k", k=LV)
        step_rows = keys_d.bitcast(I32).rearrange("(r k) -> r k", k=2 * T)
        out_v, x_v = out, x

        def over(row, n, where=1):
            v = row.unsqueeze(where)
            shape = list(v.shape)
            shape[where] = n
            return v.to_broadcast(shape)

        def sort_plan():
            steps, before = LOG_C * (LOG_C - 1) // 2 + 1 + LOG_C, []
            for k in range(LOG_C + 1, LOG_E + 1):
                before.append(steps % 2)
                steps += 1 + k - LOG_C
                before.append(steps % 2)
                steps += 1 + LOG_C
            return before, steps % 2

        key_before, key_at_end = sort_plan()
        sorted_keys = key_bufs[key_at_end]

        def params():
            col = [(bn[:, k:k + 1], v.unsqueeze(1)) for k, v in enumerate((br, gamma, beta, mean, var))]
            return col + [
                (wr[:, :], Wr), (ws[0:CR, :], Ws), (ws[CR:CR + 1, :], bs.unsqueeze(0)), (wi[:, :], Wi),
                (wgat[:, 0:HE], W_gat),
                (att[:, 0], att_src.rearrange("h e -> (h e)").partition_broadcast(P)),
                (att[:, 1], att_dst.rearrange("h e -> (h e)").partition_broadcast(P)),
            ] + [(bi3[j:j + 1, j * C:(j + 1) * C], bi.unsqueeze(0)) for j in range(3)]

        def late_params():
            return ([(gat_p[:, k], v.partition_broadcast(P)) for k, v in enumerate((b_gat, ln_gamma, ln_beta))]
                    + [(w1[:, e], W1[e]) for e in range(EXPERTS)]
                    + [(w2[:, e], W2[e].rearrange("(a p) f -> p a f", a=2)) for e in range(EXPERTS)]
                    + [(b2r[:, :], b2.rearrange("e f -> (e f)").unsqueeze(0))]
                    + [(b1c[:, e], b1[e].rearrange("(a p) -> p a", a=2)) for e in range(EXPERTS)])

        def more(i, n):
            return not isinstance(i, int) or i + n < PAIRS * CHUNKS

        def after(q, c, n):
            if isinstance(c, int) and c + n >= CHUNKS:
                return q + 1, c + n - CHUNKS
            return q, c + n

        def over_chunks(engine, step, first, end):
            half = CHUNKS // 2
            q, a, b = first // half, first % half, (end - 1) % half + 1
            lo, hi = max(a, 1 if q == 0 else 0), min(b, half - 2)
            if a < lo:
                for u in (0, 1):
                    step(q, a, u)
            if lo < hi:
                with engine.Fori(lo, hi) as c2:
                    for u in (0, 1):
                        step(q, c2, u)
            for c in range(2 * max(a, hi), 2 * b):
                step(q, c // 2, c % 2)

        halfway, ends_turn, all_chunks = CHUNKS // 2, CHUNKS // 2 + 1, CHUNKS

        def by_expert(b):
            return hid_y[:, b].rearrange("p (r e f) -> p r e f", e=EXPERTS, f=C)

        def halves(ap, g):
            return ap.rearrange("p (h d l) -> p h d l", d=2, l=1 << g)

        block = ctx.enter_context(nc.Block())

        @block.sync
        def _(sp):
            def put(to, of, s):
                sp.dma_start(to, of).then_inc(s, 16)

            put(key_bufs[0].bitcast(I32), edge_index[1].rearrange("(p c) -> p c", p=P), dst_loaded)
            put(key_bufs[1].bitcast(I32), edge_index[0].rearrange("(p c) -> p c", p=P), src_loaded)
            sp.wait_ge(ident_zero, 3)
            with nc.allow_non_contiguous_dma(reason="columns of a few numbers"):
                for to, of in params():
                    put(to, of, params_loaded)

            def load_xa(q, c, u):
                for i2 in (0, 1):
                    put(xa[i2::2, u], pair_rows(x_v, q, i2, c), xa_in[u])

            def load_xb(q, c, u):
                for i2 in (0, 1):
                    put(xb[i2::2, u], pair_rows(x_v, q, i2, c), xb_in[u])

            for u in (0, 1):
                load_xa(0, u, u)
                load_xb(0, u, u)

            sp.wait_ge(keys_final, 1)
            sk = sorted_keys
            put(keys_d[0:EDGES].rearrange("(p c) -> p c", p=P), sk, keys_stored)
            put(keys_d[EDGES:EDGES + COLS].unsqueeze(0), sk[P - 1:P, :], keys_stored)
            with nc.allow_non_contiguous_dma(reason="one key per partition"):
                put(level1_d.unsqueeze(1), sk[:, COLS - 1:COLS], levels_stored)
            put(level2_d, lvl2[:, :], levels_stored)
            sp.wait_ge(levels_stored, 32)
            put(samples[:, :], level1_d.partition_broadcast(P), samples_loaded)
            sp.wait_ge(bias_split, 1)
            for k in range(3):
                put(valid9[3 * k:3 * k + 3], valid_b, bias_placed)
                put(bi9[3 * k:3 * k + 3], bi_parts[k], bias_placed)

            def step(q, c2, u):
                c, i = 2 * c2 + u, CHUNKS * q + 2 * c2 + u
                turn = CHUNKS // 2 * q + c2
                if more(i, 4):
                    sp.wait_ge(normed1, i + 3)
                    load_xa(*after(q, c, 4), u)
                sp.wait_ge(conv_done, i + 1)
                put(x2_d[ds(i, 1)].squeeze(0), xb[:, u].rearrange("p r f -> p (r f)"), x2_out[u])
                sp.wait_ge(tnT_ready, i + 1)
                put(tnT_d[ds(i, 1)].squeeze(0), tnT[:, u], tnT_out[u])
                if more(i, 2):
                    sp.wait_ge(normed2, i + 1)
                    sp.wait_ge(x2_out[u], 16 * (turn + 1))
                    load_xb(*after(q, c, 2), u)

            for u in (0, 1):
                sp.wait_ge(normed1, u + 1)
                load_xa(0, 2 + u, u)
            over_chunks(sp, step, 0, halfway - 1)

            def store_nodes(q):
                sp.wait_ge(node_ready, CHUNKS * (q + 1))
                for i2 in (0, 1):
                    b = (2 * q + i2) * NY * NX
                    part_of = node[i2::2, q * NY:(q + 1) * NY]
                    put(node_d[b:b + NY * NX].rearrange("(y x) f -> x y f", x=NX),
                        part_of[:, :, 0:ROW], node_stored)
                    put(adst_d[b:b + NY * NX].rearrange("(y x) f -> x y f", x=NX),
                        part_of[:, :, ROW:NODE], node_stored)

            def turn_ends(k):
                sp.wait_ge(ranked, 4 * k + 6)
                put(ends_d[k, 1:M + 1].rearrange("(p c) -> p c", p=P), ends[:, k], ends_stored)
                if k == 0:
                    put(ends_d[0, 0:1].unsqueeze(0), zero[:, :], ends_stored)
                    put(ends_d[1, 0:1].unsqueeze(0), ends[P - 1:P, 0, P - 1:P], ends_stored)
                else:
                    sp.wait_ge(ends_ordered, 1)
                sp.wait_ge(ends_stored, 48 if k == 0 else 64)
                if k == 0:
                    put(cnt[:, 0:1], ends_d[0, M:M + 1].partition_broadcast(P), ends_loaded)
                for a, v in enumerate((ends_d[k, 1:M + 1], ends_d[k, 0:M])):
                    for q in range(PAIRS):
                        put(endT[q * NY:(q + 1) * NY, a].rearrange("p (a x) -> p a x", a=2),
                            by_tile(v, q), ends_loaded)

            turn_ends(0)
            over_chunks(sp, step, halfway - 1, halfway)
            store_nodes(0)
            over_chunks(sp, step, halfway, all_chunks)
            for u in (0, 1):
                put(tnT_d[PAIRS * CHUNKS + u], tnT[:, u], tnT_out[u])
            store_nodes(1)
            turn_ends(1)
            steps = sp.value_load(cnti[0:1, 0:1], min_val=MIN_STEPS, max_val=COLS // (2 * T))
            sp.wait_ge(border_found, 48)
            put(borders_d, edge_i[:, 0:2], border_stored)
            sp.wait_ge(border_stored, 16)
            with nc.allow_non_contiguous_dma(reason="one key per run"):
                put(chk[0:1, 0:2], borders_d.rearrange("p a -> a p").unsqueeze(0), border_loaded)
            sp.wait_ge(node_stored, 16 * 8)
            put(last_row[:, :], node_d[M - 1].partition_broadcast(P), late_loaded)
            with nc.allow_non_contiguous_dma(reason="columns of a few numbers"):
                for to, of in late_params():
                    put(to, of, late_loaded)
            sp.wait_ge(adst0_loaded, 16)
            sp.wait_ge(starts_scattered, 16 * TILES)
            put(starts_runs[:, 0], adst0[:, :], first_stored)
            sp.wait_ge(first_stored, 16)

            def edge_step(k):
                for u in (0, 1):
                    if some(k):
                        sp.wait_ge(dch_used[u], k)
                    put(dch[:, u], starts_runs[:, ds((2 * k + u) * T, T)], dch_in[u])
                for u in (0, 1):
                    sp.wait_ge(state_ready, 2 * k + u + 1)
                    put(state_runs[:, ds((2 * k + u) * T, T)], state[:, u, 1:], state_out[u])

            edge_step(0)
            with sp.Fori(1, steps) as k:
                edge_step(k)
            put(tails_d, state[:, 1, T], tails_stored)
            for u in (0, 1):
                sp.wait_ge(state_out[u], 16 * steps)
            sp.wait_ge(tails_stored, 16)
            put(tails, tails_d.unsqueeze(0), tails_loaded)
            sp.wait_ge(chain_ready, 1)
            put(chain_d.unsqueeze(0), chx, chain_stored)
            sp.wait_ge(chain_stored, 16)
            put(cprev[:, :], chain_d[0:P], cprev_loaded)

            for u in (0, 1):
                sp.wait_ge(y_out[u], 16 * PAIRS * CHUNKS // 2)
            for b in range(4):
                put(hid_y[:, b], y_d[b], tokens_in[b])
                put(x2_in[:, b], x2_d[b], tokens_in[b])

            def store_step(q, c4, b):
                g, turn = CHUNKS * q + 4 * c4 + b, CHUNKS // 4 * q + c4
                sp.wait_ge(mixed, g + 1)
                for i2 in (0, 1):
                    put(pair_rows(out_v, q, i2, 4 * c4 + b),
                        x2_in[i2::2, b].rearrange("p (r f) -> p r f", f=C), out_stored[b])
                if more(g, 4):
                    put(hid_y[:, b], y_d[ds(g + 4, 1)].squeeze(0), tokens_in[b])
                    sp.wait_ge(out_stored[b], 32 * (turn + 1))
                    put(x2_in[:, b], x2_d[ds(g + 4, 1)].squeeze(0), tokens_in[b])

            for q in range(PAIRS):
                with sp.Fori(0, CHUNKS // 4 - 1) as c4:
                    for b in range(4):
                        store_step(q, c4, b)
                for b in range(4):
                    store_step(q, CHUNKS // 4 - 1, b)
            for b in range(4):
                sp.wait_ge(out_stored[b], 32 * PAIRS * CHUNKS // 4)

        @block.gpsimd
        def _(pool):
            pool.memset(ident[:, :], 0.0).then_inc(ident_zero, 1)
            pool.memset(valid[:, :, :], 1.0).then_inc(ident_zero, 1)
            pool.memset(bi3, 0.0).then_inc(ident_zero, 1)
            pool.iota(part[:, :], pattern=[[0, 1]], base=0, channel_multiplier=1).then_inc(consts_made, 1)
            for k in (0, 1):
                pool.iota(target[:, k], pattern=[[1, P]], base=1 + KEY_BASE + k * SINK,
                          channel_multiplier=P).then_inc(consts_made, 1)
            pool.wait_ge(ident_zero, 3)
            pool.affine_select(out=ident[:, :], in_=ident[:, :], compare_op=ALU.not_equal, fill=1.0,
                               base=0, pattern=[[-1, P]], channel_multiplier=1).then_inc(consts_made, 1)
            pool.affine_select(out=valid[:, :, :], in_=valid[:, :, :], compare_op=ALU.not_equal,
                               fill=0.0, base=0, pattern=[[1, NX], [0, 2]],
                               channel_multiplier=NX).then_inc(ident_zero, 1)
            pool.wait_ge(ident_zero, 4)
            pool.affine_select(out=valid[:, :, :], in_=valid[:, :, :], compare_op=ALU.not_equal,
                               fill=0.0, base=-(3 * NX - 1), pattern=[[1, NX], [0, 2]],
                               channel_multiplier=NX).then_inc(consts_made, 1)

            pool.memset(found[:, :], 0.0).then_inc(found_zero, 1)
            pool.wait_ge(found_zero, 1)
            pool.wait_ge(src_loaded, 16)
            for flat in (starts_d, state_d):
                flat = flat.rearrange("(p c) h -> p (c h)", p=P)
                for k in range(0, flat.shape[1], P * LV):
                    pool.dma_start(flat[:, k:k + P * LV], found[:, :]).then_inc(zeros_stored, 16)
            zeros = COLS * (HEADS + ST) // (P * LV)

            def gather(to, table, index, s, bound=None):
                kw = {} if bound is None else dict(bounds_check=bound, oob_is_err=False)
                pool.indirect_dma_start(to, None, table, bass.IndirectOffsetOnAxis(ap=index, axis=0),
                                        **kw).then_inc(s, 16)

            def scatter(table, index, of, s, bound):
                pool.indirect_dma_start(table, bass.IndirectOffsetOnAxis(ap=index, axis=0), of, None,
                                        bounds_check=bound, oob_is_err=False).then_inc(s, 16)

            pool.wait_ge(levels_stored, 32)
            pool.wait_ge(keys_stored, 32)
            pool.wait_ge(zeros_stored, 16 * zeros)
            for n in range(8):
                level, k, h = n // 2 % 2, n // 4, n % 2
                pool.wait_ge(ranked, n + 1)
                table = level2_d if level == 0 else key_rows
                for c in range(h * P // 2, (h + 1) * P // 2):
                    gather(found[:, c * LV:(c + 1) * LV], table, row_at[:, k, c:c + 1], rows_found[h])

            pool.wait_ge(counted, 1)
            gather(keyb[:, 1:], step_rows, keys_at[:, :], keys_in)
            pool.memset(no_offset[:, :], 0).then_inc(consts_made, 1)
            pool.wait_ge(prev_zero, 1)
            one_key = keys_d.bitcast(I32).unsqueeze(1)
            gather(edge_i[:, 0:1], step_rows, keys_at[:, :], border_found)
            gather(edge_i[:, 1:2], one_key, border_at[:, 0:1], border_found)
            gather(edge_i[:, 2:3], one_key, border_at[:, 1:2], border_found, EDGES - 1)
            pool.wait_ge(grid_ready, 1)
            for t in range(TILES):
                if t % ROWS == 0:
                    pool.wait_ge(node_ready, t // ROWS + 1)
                scatter(starts_d, posi[:, 1, t:t + 1], node[:, t, ROW:NODE], starts_scattered, EDGES - 1)
            pool.wait_ge(consts_made, 6)
            pool.wait_ge(border_ready, 1)
            pool.wait_ge(node_stored, 16 * 8)
            gather(adst0[:, :], adst_d, edge_i[:, 6:7], adst0_loaded)
            gather(endf[:, :], ends_d[0].unsqueeze(1), edge_i[:, 8:9], end_found)
            steps = pool.value_load(cnti[0:1, 0:1], min_val=MIN_STEPS, max_val=COLS // (2 * T))
            with pool.Fori(0, steps) as k:
                for u in (0, 1):
                    pool.wait_ge(sources_ready, 2 * k + u + 1)
                    pool.tensor_tensor(step_i[:, u], srcs[:, u], no_offset[:, :], ALU.add)
                    pool.drain()
                    if u == 1:
                        gather(keyb[:, 1:], step_rows, keys_at[:, :], keys_in)
                    for j in range(T):
                        gather(rows_g[:, u, j], node_d, step_i[:, u, j:j + 1], rows_in[u])
            pool.wait_ge(tails_loaded, 16)
            pool.wait_ge(end_found, 16)
            pool.wait_ge(fix_placed, 1)
            gather(fixs[:, :], state_d, edge_i[:, 7:8], fix_got, EDGES - 1)
            pool.wait_ge(fix_ready, 1)
            scatter(state_d, edge_i[:, 7:8], fixo[:, :], fix_stored, EDGES - 1)
            pool.wait_ge(fix_stored, 16)
            pool.wait_ge(agg_cleared, 1)
            for t in range(TILES):
                gather(agg[:, t], state_d, posi[:, 0, t:t + 1], agg_got[t // (TILES // ROUTES)], EDGES - 1)

        @block.tensor
        def _(pe):
            pe.wait_ge(consts_made, 5)
            for n in range(2 * (LOG_E - LOG_C)):
                src = key_bufs[key_before[n]]
                for i, b in enumerate(2 * quarter + h for quarter in QUARTERS for h in (0, 1)):
                    if i % 2 == 0:
                        pe.wait_ge(phase_sorted, 4 * n + i // 2 + 1)
                    for m in range(4):
                        last = pe.transpose(bank[b][:, m * P:(m + 1) * P],
                                            src[:, (4 * b + m) * P:(4 * b + m + 1) * P], ident[:, :])
                    last.then_inc(flipped, 1)

            pe.wait_ge(params_loaded, 16 * len(params()))
            pe.wait_ge(bn_ready, 2)
            pe.wait_ge(bias_placed, 16 * 6)

            def turn_conv(i, u):
                pe.wait_ge(normed1, i + 1)
                if some(i):
                    pe.wait_ge(xnT_ready, i)
                for r in range(ROWS):
                    last = pe.transpose(bank[0][:, r * P:(r + 1) * P], xn[:, u, r], ident[:, :])
                last.then_inc(turned1, 1)

            def conv_products(i, u):
                pe.wait_ge(xnT_ready, i + 1)
                if some(i):
                    pe.wait_ge(rT_ready, i)
                pe.matmul(bank[1][0:CR, :], wr[:, :], xnT[:, u, :, 2:P + 2],
                          start=TR, stop=TR).then_inc(r_psum, 1)
                for r in range(ROWS):
                    po = bank[4 + r % 2]
                    if some(ROWS * i + r - 1):
                        pe.wait_ge(xi_ready, ROWS * i + r - 1)
                    pe.matmul(po[:, 0:3 * C], valid9[:, :], bi9[:, :], start=TR, stop=FA)
                    for j in range(3):
                        last = pe.matmul(po[:, j * C:(j + 1) * C], xnT[:, u, r, 2 * j:2 * j + P], wi[:, :],
                                         start=FA, stop=j == 2)
                    last.then_inc(xi_psum, 1)
                pe.wait_ge(rT_ready, i + 1)
                if some(i):
                    pe.wait_ge(w_ready, i)
                for r in range(ROWS):
                    po = bank[2 + r // 2][:, r % 2 * KK * GROUPS:(r % 2 + 1) * KK * GROUPS]
                    last = pe.matmul(po, rT[:, u, r * P:(r + 1) * P], ws[:, :], start=TR, stop=TR)
                last.then_inc(w_psum, 1)

            def turn_tokens(i):
                pe.wait_ge(normed2, i + 1)
                if some(i):
                    pe.wait_ge(tnT_ready, i)
                for r in range(ROWS):
                    last = pe.transpose(bank[6][:, r * P:(r + 1) * P], tn[:, r], ident[:, :])
                last.then_inc(turned2, 1)

            def node_products(i, u):
                pe.wait_ge(tnT_ready, i + 1)
                if some(i):
                    pe.wait_ge(node_ready, i)
                for r in range(ROWS):
                    last = pe.matmul(bank[7][:, r * NODE:(r + 1) * NODE], tnT[:, u, r * P:(r + 1) * P],
                                     wgat[:, :], start=TR, stop=TR)
                last.then_inc(node_psum, 1)

            def row0_sums(i):
                pe.wait_ge(row0_ready, i + 1)
                if some(i):
                    pe.wait_ge(sum_ready, i)
                if some(i - 1):
                    pe.wait_ge(node_ready, i - 1)
                for k in range(KK):
                    last = pe.matmul(bank[7][:, P:2 * P], ident[:, :],
                                     prod_pe[:, :].rearrange("p (o k) -> p o k", k=KK)[:, :, k],
                                     start=k == 0, stop=k == KK - 1)
                last.then_inc(sum_psum, 1)

            def chunk_products(q, c2, u):
                i = CHUNKS * q + 2 * c2 + u
                if some(i):
                    turn_tokens(i - 1)
                if more(i, 2):
                    turn_conv(i + 2, u)
                row0_sums(i)
                if some(i):
                    node_products(i - 1, 1 - u)
                if more(i, 2):
                    conv_products(i + 2, u)

            for u in (0, 1):
                turn_conv(u, u)
                conv_products(u, u)
            def turn_ends(k):
                pe.wait_ge(ends_ordered, k + 1)
                pe.wait_ge(node_ready, PAIRS * CHUNKS if k else 2 * ends_turn - 1)
                pe.wait_ge(sum_ready, PAIRS * CHUNKS if k else 2 * ends_turn)
                for a in (0, 1):
                    last = pe.transpose(bank[7][:, (2 + a) * P:(3 + a) * P], endO[:, a], ident[:, :])
                last.then_inc(ends_turned, 1)
                pe.wait_ge(ends_taken, k + 1)

            over_chunks(pe, chunk_products, 0, halfway)
            over_chunks(pe, chunk_products, halfway, ends_turn)
            turn_ends(0)
            over_chunks(pe, chunk_products, ends_turn, all_chunks)
            turn_tokens(PAIRS * CHUNKS - 1)
            node_products(PAIRS * CHUNKS - 1, 1)
            turn_ends(1)

            pe.wait_ge(late_loaded, 16 * (1 + len(late_params())))
            pe.wait_ge(ones_ready, 1)

            def experts(g, u, turn):
                pe.wait_ge(tnT_back[u], 16 * (turn + 1))
                for e in range(EXPERTS):
                    for a in (0, 1):
                        n = 2 * e + a
                        if some(8 * g + n - 3):
                            pe.wait_ge(hid_ready, 8 * g + n - 3)
                        pe.matmul(bank[n % 4][:, :], w1[:, e, a * P:(a + 1) * P], tnT_in[:, u],
                                  start=TR, stop=TR).then_inc(hid_psum, 1)
                pe.wait_ge(hid_ready, 8 * g + 8)
                for r in range(ROWS):
                    if some(g):
                        pe.wait_ge(y_taken, ROWS * (g - 1) + r + 1)
                    po = bank[4 + r]
                    pe.matmul(po[:, :], ones[:, :], b2r[:, :], start=TR, stop=FA)
                    for e in range(EXPERTS):
                        for a in (0, 1):
                            last = pe.matmul(po[:, e * C:(e + 1) * C],
                                             hid[u][:, 2 * e + a, r * P:(r + 1) * P], w2[:, e, a],
                                             start=FA, stop=e == EXPERTS - 1 and a == 1)
                    last.then_inc(y_psum, 1)

            experts(0, 0, 0)
            experts(1, 1, 0)
            with pe.Fori(1, PAIRS * CHUNKS // 2) as g2:
                for u in (0, 1):
                    experts(2 * g2 + u, u, g2)

        @block.scalar
        def _(act):
            act.wait_ge(params_loaded, 16 * len(params()))
            act.wait_ge(small_ready, 1)
            act.activation(bn[:, 5:6], bn[:, 4:5], ACT.Sqrt, bias=eps[0:CR, 2:3]).then_inc(bn_root, 1)
            n = 0
            for k in range(LOG_C + 1, LOG_E + 1):
                for way in (0, 1):
                    to = key_bufs[1 - key_before[n]]
                    for i, b in enumerate(2 * quarter + h for quarter in QUARTERS for h in (0, 1)):
                        act.wait_ge(flipped, 8 * n + i + 1)
                        blk = to[:, b * 512:(b + 1) * 512]
                        if way == 0:
                            for d in (0, 1):
                                last = act.activation(halves(blk, k - 1 - LOG_C)[:, :, d],
                                                      halves(bank[b][:, :], k - 1 - LOG_C)[:, :, d],
                                                      ACT.Copy, scale=1.0 - 2 * d)
                            last.then_inc(act_placed, 1)
                        elif k < LOG_E:
                            act.activation(blk, bank[b][:, :], ACT.Copy,
                                           scale=signs[:, k - LOG_C:k - LOG_C + 1]).then_inc(act_placed, 1)
                        else:
                            act.activation(blk, bank[b][:, :], ACT.Copy).then_inc(act_placed, 1)
                    n += 1

            act.wait_ge(bn_ready, 2)

            def first_root(i):
                act.wait_ge(stats1, i + 1)
                act.activation(sd[:, 0], mv[:, 0, :, 1], ACT.Sqrt, bias=eps[:, 0:1]).then_inc(root1, 1)

            def take_conv(i, u):
                act.wait_ge(turned1, i + 1)
                if some(i - 1):
                    act.wait_ge(w_psum, i - 1)
                act.activation(xnT[:, u, :, 2:P + 2], bank[0][:, :].rearrange("p (r t) -> p r t", t=P),
                               ACT.Copy).then_inc(xnT_ready, 1)

            def conv_copies(q, c, u, ahead):
                i = CHUNKS * q + c
                act.wait_ge(r_psum, i + 1)
                act.activation(rT[0:CR, u], bank[1][0:CR, :], ACT.Relu, bias=bn[:, 6:7],
                               scale=bn[:, 5:6]).then_inc(rT_ready, 1)
                for r in range(ROWS):
                    act.wait_ge(xi_psum, ROWS * i + r + 1)
                    if q:
                        act.wait_ge(conv_done, CHUNKS * (q - 1) + c + 2)
                    act.activation(xi[:, ds((ROWS * c + r + 1) * 3 * C, 3 * C)],
                                   bank[4 + r % 2][:, 0:3 * C], ACT.Copy).then_inc(xi_ready, 1)
                if ahead:
                    first_root(i + 1)

            def weight_copies(i, u):
                act.wait_ge(w_psum, i + 1)
                if some(i - 1):
                    act.wait_ge(conv_done, i - 1)
                for b in (0, 1):
                    last = act.activation(wv[:, u, 2 * b:2 * b + 2].rearrange("p r k -> p (r k)"),
                                          bank[2 + b][:, 0:2 * KK * GROUPS], ACT.Copy)
                last.then_inc(w_ready, 1)

            def second_root(i):
                act.wait_ge(conv_done, i + 1)
                act.activation(sd[:, 1], mv[:, 1, :, 1], ACT.Sqrt, bias=eps[:, 1:2]).then_inc(root2, 1)

            def take_tokens(i, u, turn):
                act.wait_ge(turned2, i + 1)
                if some(i - 1):
                    act.wait_ge(node_psum, i - 1)
                if some(turn):
                    act.wait_ge(tnT_out[u], 16 * turn)
                act.activation(tnT[:, u], bank[6][:, :], ACT.Copy).then_inc(tnT_ready, 1)

            def node_copies(i):
                act.wait_ge(node_psum, i + 1)
                act.activation(node[:, ds(ROWS * i, ROWS)].rearrange("p r f -> p (r f)"),
                               bank[7][:, 0:ROWS * NODE], ACT.Copy).then_inc(node_ready, 1)

            def sum_copies(i):
                act.wait_ge(sum_psum, i + 1)
                act.activation(inv[:, 0], bank[7][:, P:2 * P], ACT.Copy).then_inc(sum_ready, 1)

            def chunk_copies(q, c2, u):
                c, i, turn = 2 * c2 + u, CHUNKS * q + 2 * c2 + u, CHUNKS // 2 * q + c2
                if some(i):
                    second_root(i - 1)
                if more(i, 1):
                    weight_copies(i + 1, 1 - u)
                if some(i):
                    take_tokens(i - 1, 1 - u, turn if u else turn - 1)
                if more(i, 2):
                    take_conv(i + 2, u)
                if some(i):
                    node_copies(i - 1)
                sum_copies(i)
                if more(i, 2):
                    conv_copies(*after(q, c, 2), u, more(i, 3))

            first_root(0)
            first_root(1)
            for u in (0, 1):
                take_conv(u, u)
                conv_copies(0, u, u, u == 1)
                if u == 0:
                    weight_copies(0, 0)
            def take_ends(k):
                act.wait_ge(ends_turned, k + 1)
                act.activation(endG[:, 2 * k:2 * k + 2].rearrange("p a t -> p (a t)"),
                               bank[7][:, 2 * P:4 * P], ACT.Copy).then_inc(ends_taken, 1)

            over_chunks(act, chunk_copies, 0, halfway)
            over_chunks(act, chunk_copies, halfway, ends_turn)
            take_ends(0)
            over_chunks(act, chunk_copies, ends_turn, all_chunks)
            second_root(PAIRS * CHUNKS - 1)
            take_tokens(PAIRS * CHUNKS - 1, 1, PAIRS * CHUNKS // 2 - 1)
            node_copies(PAIRS * CHUNKS - 1)
            take_ends(1)

            act.wait_ge(late_loaded, 16 * (1 + len(late_params())))
            for u in (0, 1):
                act.wait_ge(tnT_out[u], 16 * (PAIRS * CHUNKS // 2 + 1))
                act.dma_start(tnT_in[:, u], tnT_d[u]).then_inc(tnT_back[u], 16)

            def expert_copies(g, v, turn):
                for n in range(8):
                    act.wait_ge(hid_psum, 8 * g + n + 1)
                    if n == 0 and some(g - 1):
                        act.wait_ge(y_psum, ROWS * (g - 1))
                    act.activation(hid[v][:, n], bank[n % 4][:, :], ACT.Gelu,
                                   bias=b1c[:, n // 2, n % 2:n % 2 + 1]).then_inc(hid_ready, 1)
                act.dma_start(tnT_in[:, v], tnT_d[ds(g + 2, 1)].squeeze(0)).then_inc(tnT_back[v], 16)
                if some(turn):
                    act.wait_ge(y_out[v], 16 * turn)
                for r in range(ROWS):
                    act.wait_ge(y_psum, ROWS * g + r + 1)
                    act.activation(y_new[:, v, r], bank[4 + r][:, :], ACT.Copy).then_inc(y_taken, 1)
                act.wait_ge(y_taken, ROWS * (g + 1))
                act.dma_start(y_d[ds(g, 1)].squeeze(0), y_new[:, v].rearrange("p r f -> p (r f)")).then_inc(y_out[v], 16)

            def edge_exponentials(k, u):
                act.wait_ge(scored, 2 * k + u + 1)
                act.activation(ex[:, :, :, :], ex[:, :, :, :], ACT.Exp).then_inc(weighed, 1)

            steps = act.value_load(cnti[0:1, 0:1], min_val=MIN_STEPS, max_val=COLS // (2 * T))
            shared = act.value_load(cnti[0:1, 2:3], min_val=MIN_STEPS - 1, max_val=MOST_SHARED)
            for g in range(4):
                expert_copies(g, g % 2, g // 2)
            act.wait_ge(own_scored, 1)
            act.activation(hx[:, 0:2], hx[:, 0:2], ACT.Exp).then_inc(own_weighed, 1)
            with act.Fori(0, shared) as k:
                for u in (0, 1):
                    for v in (0, 1):
                        expert_copies(4 + 4 * k + 2 * u + v, v, 2 + 2 * k + u)
                    edge_exponentials(k, u)
            past_first = act.value_load(cnti[0:1, 3:4], min_val=MIN_STEPS - 2, max_val=MOST_SHARED - 1)
            with act.Fori(2 * past_first + 4, PAIRS * CHUNKS // 2) as g2:
                for v in (0, 1):
                    expert_copies(2 * g2 + v, v, g2)
            with act.Fori(shared, steps) as k:
                for u in (0, 1):
                    edge_exponentials(k, u)
            for v in (0, 1):
                act.wait_ge(tnT_back[v], 16 * (PAIRS * CHUNKS // 2 + 1))
            act.wait_ge(chain_scored, 1)
            act.activation(che, che, ACT.Exp).then_inc(chain_weighed, 1)
            act.wait_ge(fix_scored, 1)
            act.activation(fixe[:, :, :], fixe[:, :, :], ACT.Exp).then_inc(fix_weighed, 1)
            for q in range(ROUTES):
                t = slice(q * TILES // ROUTES, (q + 1) * TILES // ROUTES)
                act.wait_ge(joined, q + 1)
                act.activation(hx[:, 0:2, t], hx[:, 0:2, t], ACT.Exp).then_inc(join_weighed, 1)
                act.wait_ge(agg_var, q + 1)
                act.activation(one4[:, 1, t], one4[:, 0, t], ACT.Sqrt, bias=eps[:, 1:2]).then_inc(agg_root, 1)
                act.wait_ge(top_ready, q + 1)
                act.activation(one4[:, 1, t], one4[:, 0, t], ACT.Exp).then_inc(top_weighed, 1)
                act.wait_ge(routed, q + 1)
                per = PAIRS * CHUNKS // (4 * ROUTES)
                with act.Fori(q * per, (q + 1) * per) as g4:
                    for b in range(4):
                        act.wait_ge(tokens_in[b], 32 * (g4 + 1))
                        for e in range(SCALED):
                            for r in range(ROWS):
                                y = by_expert(b)[:, r, e]
                                last = act.activation(y, y, ACT.Copy,
                                                      scale=gate[:, ds(ROWS * (4 * g4 + b) + r, 1), e])
                        last.then_inc(y_scaled, 1)


        @block.vector
        def _(dve):
            flush = dve.drain

            dve.wait_ge(consts_made, 5)
            for k in range(LOG_E - LOG_C):
                dve.tensor_scalar(sign_i[:, k:k + 1], part[:, :], k, 1,
                                  ALU.logical_shift_right, ALU.bitwise_and)
            dve.tensor_copy(partf[:, :], part[:, :])
            for k, v in enumerate((1e-6, 1e-5, 1e-3)):
                dve.memset(eps[:, k:k + 1], v)
            dve.memset(zero[:, :], 0.0)
            dve.memset(keyb[:, 0:1], 0)
            dve.memset(edge_i[:, 2:3], 0).then_inc(prev_zero, 1)
            for k in (0, 1):
                dve.tensor_scalar(target[:, k], target[:, k], SRC_BITS, None, ALU.logical_shift_left)
            flush()
            dve.tensor_scalar(signs[:, :], sign_i[:, :], -2.0, 1.0, ALU.mult, ALU.add).then_inc(small_ready, 1)

            dve.wait_ge(dst_loaded, 16)
            dst, src = key_bufs[0].bitcast(I32), key_bufs[1].bitcast(I32)
            cls, gone = tmp_a.bitcast(I32), tmp_b.bitcast(I32)
            dve.tensor_scalar(gone, dst, M, DROPPED, ALU.is_ge, ALU.mult)
            flush()
            dve.tensor_scalar(dst, dst, M, KEY_BASE, ALU.min, ALU.add)
            flush()
            dve.tensor_tensor(dst, dst, gone, ALU.add)
            dve.wait_ge(src_loaded, 16)
            dve.tensor_scalar(src, src, 0, M - 1, ALU.max, ALU.min)
            flush()
            dve.tensor_scalar(cls, src, M - 1, SINK, ALU.is_ge, ALU.mult)
            flush()
            dve.tensor_tensor(dst, dst, cls, ALU.add)
            flush()
            dve.scalar_tensor_tensor(out=dst, in0=dst, scalar=SRC_BITS, in1=src,
                                     op0=ALU.logical_shift_left, op1=ALU.bitwise_or)
            flush()
            bufs = list(key_bufs)

            def compare(cmp_bit, dir_bit, quarter=None):
                a, b = bufs
                if quarter is not None and cmp_bit < LOG_C - 1:
                    a, b = (z[:, quarter * QUARTER:(quarter + 1) * QUARTER] for z in (a, b))
                if dir_bit is None:
                    va, vb = halves(a, cmp_bit), halves(b, cmp_bit)
                    if quarter is not None and cmp_bit == LOG_C - 1:
                        va, vb = (z[:, :, :, quarter * QUARTER:(quarter + 1) * QUARTER] for z in (va, vb))
                    dve.tensor_tensor(vb[:, :, 0], va[:, :, 0], va[:, :, 1], ALU.min)
                    last = dve.tensor_tensor(vb[:, :, 1], va[:, :, 0], va[:, :, 1], ALU.max)
                else:
                    cut = dict(d=2, m=1 << (dir_bit - 1 - cmp_bit), c=2, l=1 << cmp_bit)
                    va, vb = (z.rearrange("p (h d m c l) -> p h d m c l", **cut) for z in (a, b))
                    for d in (0, 1):
                        for c in (0, 1):
                            last = dve.tensor_tensor(vb[:, :, d, :, c], va[:, :, d, :, 0], va[:, :, d, :, 1],
                                                     ALU.min if c == d else ALU.max)
                return last

            def merge(bits, dir_bit):
                for j in bits[:-1]:
                    compare(j, dir_bit)
                    bufs.reverse()
                    flush()
                for quarter in QUARTERS:
                    compare(bits[-1], dir_bit, quarter).then_inc(phase_sorted, 1)
                bufs.reverse()

            for k in range(1, LOG_C):
                for j in reversed(range(k)):
                    compare(j, k)
                    bufs.reverse()
                    flush()
            dve.tensor_scalar(bufs[1], bufs[0], signs[:, 0:1], None, ALU.mult)
            bufs.reverse()
            flush()
            low_bits = list(reversed(range(LOG_C)))
            merge(low_bits, None)
            n = 0
            for k in range(LOG_C + 1, LOG_E + 1):
                for way in (0, 1):
                    assert bufs[0] is key_bufs[key_before[n]]
                    bits = low_bits if way else list(reversed(range(k - LOG_C)))
                    dir_bit = k - LOG_C if way == 0 and k < LOG_E else None
                    for i, quarter in enumerate(QUARTERS):
                        if way == 0 or i % 2 == 1:
                            dve.wait_ge(act_placed, 8 * n + 2 * (i + 1))
                            flush()
                            bufs.reverse()
                            last = compare(bits[0], dir_bit, i // 2 if way else quarter)
                            bufs.reverse()
                            if len(bits) == 1:
                                last.then_inc(phase_sorted, 1)
                    if len(bits) > 1:
                        flush()
                        merge(bits[1:], dir_bit)
                    n += 1
            flush()
            assert bufs[0] is sorted_keys
            dve.tensor_copy(lvl2[:, :], sorted_keys[:, LV - 1:COLS:LV]).then_inc(keys_final, 1)

            def first_level(k, first, end, space):
                tg = target[:, k].bitcast(F32)
                n = space.shape[1] // P
                v = space.rearrange("p (c s) -> p c s", s=P)
                for c in range(first, end, n):
                    dve.tensor_tensor(v, over(samples[:, :], n), over(tg[:, c:c + n], P, 2), ALU.is_lt)
                    flush()
                    dve.tensor_reduce(rank1[:, k, c:c + n], v, AX.X, ALU.add)
                    flush()
                dve.tensor_scalar(rank1[:, k, first:end], rank1[:, k, first:end], float(P - 1), None, ALU.min)
                flush()
                return dve.tensor_copy(row_at[:, k, first:end], rank1[:, k, first:end])

            def rank(n):
                level, k, h = n // 2 % 2, n // 4, n % 2
                cols = slice(h * P // 2, (h + 1) * P // 2)
                tg = target[:, k, cols].bitcast(F32)
                v = found[:, h * P // 2 * LV:(h + 1) * P // 2 * LV].rearrange("p (c s) -> p c s", s=LV)
                dve.wait_ge(rows_found[h], 16 * P // 2 * (n // 2 + 1))
                dve.tensor_tensor(v, v, over(tg, LV, 2), ALU.is_lt)
                flush()
                dve.tensor_reduce(ends[:, k, cols], v, AX.X, ALU.add)
                flush()
                if level == 0:
                    dve.tensor_scalar(ends[:, k, cols], ends[:, k, cols], float(LV - 1), None, ALU.min)
                    flush()
                    dve.scalar_tensor_tensor(out=rank1[:, k, cols], in0=rank1[:, k, cols], scalar=float(LV),
                                             in1=ends[:, k, cols], op0=ALU.mult, op1=ALU.add)
                    flush()
                    dve.tensor_copy(row_at[:, k, cols], rank1[:, k, cols]).then_inc(ranked, 1)
                else:
                    dve.scalar_tensor_tensor(out=ends[:, k, cols], in0=rank1[:, k, cols], scalar=float(LV),
                                             in1=ends[:, k, cols], op0=ALU.mult, op1=ALU.add).then_inc(ranked, 1)

            dve.wait_ge(params_loaded, 16 * len(params()))
            dve.tensor_copy(valid_b, valid[:, :, :].rearrange("p x a -> p (x a)"))
            left = bi3
            for k in range(3):
                last = dve.tensor_copy(bi_parts[k], left)
                flush()
                if k < 2:
                    dve.tensor_tensor(bi_left, left, bi_parts[k], ALU.subtract)
                    left = bi_left
                    flush()
            last.then_inc(bias_split, 1)
            for k in (0, 1):
                dve.tensor_tensor(prod[:, k * HE:(k + 1) * HE], att[:, k], wgat[:, 0:HE], ALU.mult)
            dve.wait_ge(bn_root, 1)
            dve.reciprocal(bn[:, 5:6], bn[:, 5:6])
            flush()
            for k in (0, 1):
                dve.tensor_reduce(wgat[:, HE + k * HEADS:HE + (k + 1) * HEADS],
                                  prod[:, k * HE:(k + 1) * HE].rearrange("p (h e) -> p h e", e=EXPERTS), AX.X, ALU.add)
            dve.tensor_tensor(bn[:, 5:6], bn[:, 5:6], bn[:, 1:2], ALU.mult)
            dve.tensor_tensor(bn[:, 6:7], bn[:, 0:1], bn[:, 3:4], ALU.subtract)
            flush()
            dve.tensor_tensor(bn[:, 6:7], bn[:, 6:7], bn[:, 5:6], ALU.mult)
            flush()
            dve.tensor_tensor(bn[:, 6:7], bn[:, 6:7], bn[:, 2:3], ALU.add).then_inc(bn_ready, 1)

            dve.wait_ge(samples_loaded, 16)
            space = xi[:, 2 * COLS:2 * COLS + P // 2 * P]
            first_level(0, 0, P // 2, space).then_inc(ranked, 1)

            dve.wait_ge(keys_stored, 32)
            dve.wait_ge(levels_stored, 32)
            dve.memset(xi[:, 0:3 * C], 0.0)
            dve.memset(xi[:, (NY + 1) * 3 * C:], 0.0)
            for side in (0, P + 2):
                dve.memset(xnT[:, :, :, side:side + 2], 0.0)
            dve.memset(rT[CR:CR + 1], 1.0).then_inc(bn_ready, 1)
            flush()

            def sums(k, rows):
                for r in range(ROWS):
                    dve.bn_stats(stats[:, k, r], rows[:, r])

            def moments(k, done):
                for r in range(ROWS):
                    last = dve.bn_aggr(mv[:, k, r], stats[:, k, r])
                last.then_inc(done, 1)

            def inverse(k, i):
                dve.wait_ge((root1, root2)[k], i + 1)
                dve.reciprocal(rstd[:, k], sd[:, k])

            def first_norm(i, u):
                if some(i - 1):
                    dve.wait_ge(turned1, i - 1)
                for r in range(ROWS):
                    last = dve.tensor_scalar(xn[:, u, r], xa[:, u, r], mv[:, 0, r, 0:1],
                                             rstd[:, 0, r:r + 1], ALU.subtract, ALU.mult)
                last.then_inc(normed1, 1)

            def second_norm(i, u):
                if some(i):
                    dve.wait_ge(turned2, i)
                for r in range(ROWS):
                    last = dve.tensor_scalar(tn[:, r], xb[:, u, r], mv[:, 1, r, 0:1],
                                             rstd[:, 1, r:r + 1], ALU.subtract, ALU.mult)
                last.then_inc(normed2, 1)

            def products(c, u, r):
                patch = xi[:, ds((ROWS * c + r) * 3 * C, TAPS)]
                to = prod[:, r % 2 * TAPS:(r % 2 + 1) * TAPS] if r else prod_pe[:, :]
                return dve.tensor_tensor(to.rearrange("p (g f k) -> p g f k", g=GROUPS, k=KK),
                                         patch.rearrange("p (g f k) -> p g f k", g=GROUPS, k=KK),
                                         over(wv[:, u, r].rearrange("p (g k) -> p g k", k=KK), C // GROUPS, 2),
                                         ALU.mult)

            def reduction(r):
                dve.tensor_reduce(inv[:, r], prod[:, r % 2 * TAPS:(r % 2 + 1) * TAPS].rearrange("p (o k) -> p o k", k=KK),
                                  AX.X, ALU.add)

            def conv_step(q, c2, u):
                c, i, turn = 2 * c2 + u, CHUNKS * q + 2 * c2 + u, CHUNKS // 2 * q + c2
                dve.wait_ge(xi_ready, ROWS * (i + 1) + (1 if more(i, 1) else 0))
                dve.wait_ge(w_ready, i + 1)
                if some(i):
                    dve.wait_ge(sum_psum, i)
                products(c, u, 0).then_inc(row0_ready, 1)
                if some(i):
                    inverse(1, i - 1)
                if more(i, 2):
                    inverse(0, i + 2)
                flush()
                if some(i):
                    second_norm(i - 1, 1 - u)
                if more(i, 2):
                    first_norm(i + 2, u)
                products(c, u, 1)
                if more(i, 3):
                    dve.wait_ge(xa_in[1 - u], 32 * (turn + 2 + u))
                    sums(0, xa[:, 1 - u])
                flush()
                if more(i, 3):
                    moments(0, stats1)
                reduction(1)
                products(c, u, 2)
                flush()
                reduction(2)
                products(c, u, 3)
                flush()
                reduction(3)
                flush()
                dve.wait_ge(xb_in[u], 32 * (turn + 1))
                dve.wait_ge(sum_ready, i + 1)
                dve.tensor_tensor(xb[:, u], xb[:, u], inv[:, :], ALU.add)
                flush()
                sums(1, xb[:, u])
                flush()
                moments(1, conv_done)

            def c_(k):
                return cnt[:, k:k + 1]

            def order_ends(k):
                dve.wait_ge(ends_loaded, 16 * (5 + 4 * k))
                for a in (0, 1):
                    last = dve.tensor_copy(endO[:, a].rearrange("p (x a) -> p a x", a=2),
                                           endT[:, a].rearrange("p (a x) -> p a x", a=2))
                last.then_inc(ends_ordered, 1)

            def new_sources(k, u):
                if u == 0:
                    dve.wait_ge(keys_in, 16 * (k + 1))
                dve.tensor_scalar(srcs[:, u], keyb[:, 1 + u * T:1 + (u + 1) * T], M - 1, None, ALU.bitwise_and)
                dve.tensor_scalar(clsi[:, :], keyb[:, u * T:1 + (u + 1) * T], SRC_BITS, None, ALU.logical_shift_right)
                if u == 1:
                    dve.tensor_copy(keyb[:, 0:1], keyb[:, 2 * T:])
                    dve.tensor_scalar(keys_at[:, :], keys_at[:, :], 1, None, ALU.add)
                flush()
                dve.tensor_tensor(same[:, u], clsi[:, 1:], clsi[:, :T], ALU.is_equal)
                flush()
                dve.tensor_scalar(reset[:, u], same[:, u], -1.0, BIG, ALU.add, ALU.mult).then_inc(sources_ready, 1)

            def e_(k):
                return edge_f[:, k:k + 1]

            def borders():
                dve.wait_ge(border_found, 48)
                dve.tensor_scalar(edge_i[:, 3:6], edge_i[:, 0:3], SRC_BITS, None, ALU.logical_shift_right)
                flush()
                dve.tensor_scalar(edge_f[:, 0:3], edge_i[:, 3:6], float(-KEY_BASE), None, ALU.add)
                flush()
                dve.tensor_scalar(edge_i[:, 8:9], e_(0), 1.0, float(M), ALU.add, ALU.min)
                dve.tensor_scalar(edge_i[:, 6:7], e_(0), float(M - 1), None, ALU.min).then_inc(border_ready, 1)

            def find_positions():
                dve.wait_ge(ends_taken, 1)
                per_step = float(2 * T * P)

                dve.tensor_scalar(cnti[:, 0:1], c_(0), 1.0 / per_step, None, ALU.mult)
                flush()
                dve.tensor_copy(c_(2), cnti[:, 0:1])
                flush()
                dve.scalar_tensor_tensor(out=c_(3), in0=c_(2), scalar=per_step, in1=c_(0), op0=ALU.mult, op1=ALU.is_lt)
                flush()
                dve.tensor_tensor(c_(2), c_(2), c_(3), ALU.add)
                flush()
                dve.tensor_scalar(c_(4), c_(2), 1.0, per_step, ALU.subtract, ALU.mult)
                flush()
                dve.tensor_tensor(c_(3), c_(4), c_(0), ALU.is_ge)
                flush()
                dve.tensor_tensor(c_(2), c_(2), c_(3), ALU.subtract)
                flush()
                dve.tensor_scalar(c_(2), c_(2), float(MIN_STEPS), None, ALU.max)
                flush()
                dve.tensor_scalar(c_(4), c_(2), float(2 * T), None, ALU.mult)
                flush()
                dve.tensor_scalar(c_(5), c_(4), -1.0, float(COLS), ALU.mult, ALU.add)
                dve.reciprocal(c_(6), c_(4))
                dve.tensor_copy(cnti[:, 0:1], c_(2))
                dve.tensor_scalar(cnti[:, 2:3], c_(2), float(MOST_SHARED + 1), -1.0, ALU.min, ALU.add)
                dve.tensor_scalar(cnti[:, 3:4], c_(2), float(MOST_SHARED + 1), -2.0, ALU.min, ALU.add)
                dve.tensor_scalar(keys_at[:, :], partf[:, :], c_(2), None, ALU.mult)
                dve.tensor_scalar(border_f[:, 0:1], partf[:, :], 1.0, c_(4), ALU.add, ALU.mult)
                dve.tensor_scalar(border_f[:, 1:2], partf[:, :], c_(4), None, ALU.mult)
                dve.tensor_scalar(c_(7), partf[:, :], 0.0, SKIP, ALU.is_equal, ALU.mult)
                flush()
                dve.tensor_scalar(border_at[:, 0:1], border_f[:, 0:1], -1.0, None, ALU.add)
                dve.scalar_tensor_tensor(out=border_at[:, 1:2], in0=border_f[:, 1:2], scalar=-1.0, in1=c_(7),
                                         op0=ALU.add, op1=ALU.add).then_inc(counted, 1)
                dve.tensor_tensor(nonempty[:, 0], endG[:, 0], endG[:, 1], ALU.is_gt)
                dve.tensor_scalar(pos[:, 0], endG[:, 0], 1.0, None, ALU.subtract)
                dve.tensor_copy(pos[:, 1], endG[:, 1])
                flush()
                dve.tensor_scalar(quoi[:, :], pos[:, :], c_(6), None, ALU.mult)
                flush()
                dve.tensor_copy(quo[:, :], quoi[:, :])
                flush()
                dve.scalar_tensor_tensor(out=fit[:, :], in0=quo[:, :], scalar=c_(4), in1=pos[:, :], op0=ALU.mult, op1=ALU.is_gt)
                flush()
                dve.tensor_tensor(quo[:, :], quo[:, :], fit[:, :], ALU.subtract)
                flush()
                dve.tensor_scalar(fit[:, :], quo[:, :], 1.0, c_(4), ALU.add, ALU.mult)
                flush()
                dve.tensor_tensor(fit[:, :], fit[:, :], pos[:, :], ALU.is_le)
                flush()
                dve.tensor_tensor(quo[:, :], quo[:, :], fit[:, :], ALU.add)
                flush()
                dve.scalar_tensor_tensor(out=pos[:, :], in0=quo[:, :], scalar=c_(5), in1=pos[:, :], op0=ALU.mult, op1=ALU.add)
                flush()
                dve.scalar_tensor_tensor(out=pos[:, :], in0=pos[:, :], scalar=-SKIP,
                                         in1=over(nonempty[:, 0], 2), op0=ALU.add, op1=ALU.mult)
                flush()
                dve.tensor_scalar(posi[:, :], pos[:, :], SKIP, None, ALU.add).then_inc(grid_ready, 1)

            for i in range(3):
                dve.wait_ge(xa_in[i % 2], 32 * (i // 2 + 1))
                sums(0, xa[:, i % 2])
                flush()
                moments(0, stats1)
                if i < 2:
                    inverse(0, i)
                    flush()
                    first_norm(i, i)
            first_level(0, P // 2, P, space).then_inc(ranked, 1)
            flush()
            slots = (0, 2, 3, 5, 6, 8, 9, 11, 13)
            for n in range(8):
                over_chunks(dve, conv_step, slots[n], slots[n + 1])
                rank(n)
                if n < 3:
                    flush()
                    first_level(1, 48 * n, min(48 * (n + 1), P), prod[:, 0:16 * P])
                    flush()
                if n == 4:
                    order_ends(0)
                if n == 5:
                    find_positions()
                    flush()
            borders()
            for u in (0, 1):
                new_sources(0, u)
            flush()
            over_chunks(dve, conv_step, slots[8], all_chunks)
            inverse(1, PAIRS * CHUNKS - 1)
            flush()
            second_norm(PAIRS * CHUNKS - 1, 1)

            dve.memset(ones[:, :], 1.0).then_inc(ones_ready, 1)

            order_ends(1)
            dve.wait_ge(border_loaded, 16)
            dve.tensor_scalar(chk[:, :], chk[:, :], SRC_BITS, None, ALU.logical_shift_right)
            flush()
            dve.tensor_copy(chf[:, 0:2], chk[:, :])

            def heads(v):
                return v.rearrange("p t (h e) -> p t h e", e=EXPERTS)

            n_sink, lone = one4[:, 2], one4[:, 3]
            a_src, a_dst, h_all = node[:, :, HE:ROW], node[:, :, ROW:NODE], node[:, :, 0:HE]
            dve.wait_ge(late_loaded, 16 * (1 + len(late_params())))
            dve.tensor_tensor(hx[:, 0], a_src, a_dst, ALU.add)
            dve.tensor_tensor(hx[:, 1], a_dst, over(last_row[:, HE:ROW], TILES), ALU.add)
            dve.wait_ge(ends_taken, 2)
            dve.tensor_tensor(n_sink, endG[:, 2], endG[:, 3], ALU.subtract)
            flush()
            for k in (0, 1):
                dve.scalar_tensor_tensor(out=hx[:, k], in0=hx[:, k], scalar=0.2, in1=hx[:, k],
                                         op0=ALU.mult, op1=ALU.max)
            dve.tensor_scalar(lone, n_sink, 0.0, -BIG, ALU.is_equal, ALU.mult)
            flush()
            dve.tensor_tensor(hx[:, 1], hx[:, 1], over(lone, HEADS, 2), ALU.add)
            flush()
            dve.tensor_tensor(hx[:, 2], hx[:, 0], hx[:, 1], ALU.max)
            flush()
            for k in (0, 1):
                last = dve.tensor_tensor(hx[:, k], hx[:, k], hx[:, 2], ALU.subtract)
            last.then_inc(own_scored, 1)
            dve.wait_ge(own_weighed, 1)
            dve.tensor_tensor(hx[:, 1], hx[:, 1], over(n_sink, HEADS, 2), ALU.mult)
            dve.tensor_tensor(heads(wide[:, 0]), heads(h_all), over(hx[:, 0], EXPERTS, 3), ALU.mult)
            dve.wait_ge(node_stored, 16 * 8)
            dve.wait_ge(starts_scattered, 16 * TILES)
            dve.tensor_copy(a_src, hx[:, 2])
            flush()
            dve.tensor_tensor(heads(wide[:, 1]), heads(over(last_row[:, 0:HE], TILES)),
                              over(hx[:, 1], EXPERTS, 3), ALU.mult)
            dve.tensor_tensor(a_dst, hx[:, 0], hx[:, 1], ALU.add)
            flush()
            dve.tensor_tensor(h_all, wide[:, 0], wide[:, 1], ALU.add)
            dve.memset(df[:, T], 0.0)
            dve.memset(state[:, 1, T, 0:HEADS], -BIG)
            dve.memset(state[:, 1, T, HEADS:ST], 0.0)
            flush()

            dve.memset(fixs[:, :], 0.0)
            dve.wait_ge(end_found, 16)
            dve.tensor_scalar(e_(3), endf[:, :], 1.0, None, ALU.subtract)
            dve.tensor_tensor(e_(4), e_(0), e_(2), ALU.is_equal)
            dve.tensor_scalar(e_(5), e_(0), float(M), None, ALU.is_lt)
            dve.tensor_scalar(e_(6), partf[:, :], 1.0, c_(4), ALU.add, ALU.mult)
            dve.tensor_scalar(e_(7), partf[:, :], c_(5), None, ALU.mult)
            flush()
            dve.tensor_tensor(e_(4), e_(4), e_(5), ALU.mult)
            dve.tensor_tensor(e_(6), e_(3), e_(6), ALU.is_lt)
            dve.scalar_tensor_tensor(out=e_(7), in0=e_(3), scalar=-SKIP, in1=e_(7), op0=ALU.add, op1=ALU.add)
            flush()
            dve.tensor_tensor(e_(4), e_(4), e_(6), ALU.mult)
            flush()
            dve.tensor_tensor(e_(7), e_(7), e_(4), ALU.mult)
            flush()
            dve.tensor_scalar(edge_i[:, 7:8], e_(7), SKIP, None, ALU.add).then_inc(fix_placed, 1)
            flush()

            steps = dve.value_load(cnti[0:1, 0:1], min_val=MIN_STEPS, max_val=COLS // (2 * T))

            def edge_scans(k):
                for u in (0, 1):
                    dve.tensor_copy(df[:, 0], df[:, T])
                    if some(k):
                        dve.wait_ge(state_out[u], 16 * k)
                    dve.tensor_copy(state[:, u, 0], state[:, 1 - u, T])
                    flush()
                    dve.wait_ge(dch_in[u], 16 * (k + 1))
                    for h in range(HEADS):
                        last = dve.tensor_tensor_scan(df[:, 1:, h], same[:, u], dch[:, u, :, h],
                                                      df[:, 0, h:h + 1], ALU.mult, ALU.add)
                    last.then_inc(dch_used[u], 1)
                    flush()
                    dve.wait_ge(rows_in[u], 16 * T * (k + 1))
                    dve.tensor_tensor(score[:, :, :], rows_g[:, u, :, HE:ROW], df[:, 1:], ALU.add)
                    flush()
                    dve.scalar_tensor_tensor(out=score[:, :, :], in0=score[:, :, :], scalar=0.2,
                                             in1=score[:, :, :], op0=ALU.mult, op1=ALU.max)
                    flush()
                    for h in range(HEADS):
                        dve.tensor_tensor_scan(state[:, u, 1:, h], reset[:, u], score[:, :, h],
                                               state[:, u, 0, h:h + 1], ALU.add, ALU.max)
                    flush()
                    dve.tensor_tensor(ex[:, :, 0], state[:, u, 0:T, 0:HEADS], state[:, u, 1:, 0:HEADS], ALU.subtract)
                    dve.tensor_tensor(ex[:, :, 1], score[:, :, :], state[:, u, 1:, 0:HEADS], ALU.subtract)
                    flush()
                    dve.tensor_tensor(ex[:, :, 0], ex[:, :, 0], over(reset[:, u], HEADS, 2),
                                      ALU.add).then_inc(scored, 1)
                    dve.wait_ge(weighed, 2 * k + u + 1)
                    dve.tensor_tensor(pv[:, :, :].rearrange("p t (h e) -> p t h e", e=EXPERTS),
                                      rows_g[:, u, :, 0:HE].rearrange("p t (h e) -> p t h e", e=EXPERTS),
                                      over(ex[:, :, 1], EXPERTS, 3), ALU.mult)
                    flush()
                    for h in range(HEADS):
                        for e in range(-1, EXPERTS):
                            f = HEADS + h if e < 0 else 2 * HEADS + EXPERTS * h + e
                            new = ex[:, :, 1, h] if e < 0 else pv[:, :, EXPERTS * h + e]
                            last = dve.tensor_tensor_scan(state[:, u, 1:, f], ex[:, :, 0, h], new,
                                                          state[:, u, 0, f:f + 1], ALU.mult, ALU.add)
                    last.then_inc(state_ready, 1)
                    flush()
                    new_sources(k + 1, u)

            edge_scans(0)
            with dve.Fori(1, steps) as k:
                edge_scans(k)

            dve.tensor_tensor(chf[:, 2], chf[:, 0], chf[:, 1], ALU.is_equal)
            dve.memset(chf[:, 3, 0:1], 0.0)
            dve.tensor_tensor(chf[:, 3, 1:], chf[:, 0, 1:], chf[:, 1, :P - 1], ALU.is_equal)
            flush()
            dve.tensor_tensor(chf[:, 2], chf[:, 2], chf[:, 3], ALU.mult)
            flush()
            dve.tensor_scalar(chf[:, 4], chf[:, 2], -1.0, BIG, ALU.add, ALU.mult)
            dve.wait_ge(tails_loaded, 16)
            dve.memset(chx[:, 0, 0:HEADS], -BIG)
            dve.memset(chx[:, 0, HEADS:ST], 0.0)
            flush()
            for h in range(HEADS):
                dve.tensor_tensor_scan(chx[:, 1:, h], chf[:, 4], tails[:, :, h], chx[:, 0, h:h + 1],
                                       ALU.add, ALU.max)
            flush()
            dve.tensor_tensor(che[:, :, 0], chx[:, 0:P, 0:HEADS], chx[:, 1:, 0:HEADS], ALU.subtract)
            dve.tensor_tensor(che[:, :, 1], tails[:, :, 0:HEADS], chx[:, 1:, 0:HEADS], ALU.subtract)
            flush()
            dve.tensor_tensor(che[:, :, 0], che[:, :, 0], over(chf[:, 4], HEADS, 2), ALU.add).then_inc(chain_scored, 1)
            dve.wait_ge(chain_weighed, 1)
            dve.tensor_tensor(chp[:, :, 0:HEADS], tails[:, :, HEADS:2 * HEADS], che[:, :, 1], ALU.mult)
            dve.tensor_tensor(chp[:, :, HEADS:].rearrange("p t (h e) -> p t h e", e=EXPERTS),
                              tails[:, :, 2 * HEADS:].rearrange("p t (h e) -> p t h e", e=EXPERTS),
                              over(che[:, :, 1], EXPERTS, 3), ALU.mult)
            flush()
            for h in range(HEADS):
                for e in range(-1, EXPERTS):
                    f = HEADS + h if e < 0 else 2 * HEADS + EXPERTS * h + e
                    last = dve.tensor_tensor_scan(chx[:, 1:, f], che[:, :, 0, h], chp[:, :, f - HEADS],
                                                  chx[:, 0, f:f + 1], ALU.mult, ALU.add)
            last.then_inc(chain_ready, 1)

            flush()
            dve.memset(agg[:, :, 0:HEADS], -BIG)
            dve.memset(agg[:, :, HEADS:ST], 0.0).then_inc(agg_cleared, 1)
            dve.wait_ge(fix_got, 16)
            dve.wait_ge(cprev_loaded, 16)
            dve.tensor_tensor(fixo[:, 0:HEADS], cprev[:, 0:HEADS], fixs[:, 0:HEADS], ALU.max)
            flush()
            dve.tensor_tensor(fixe[:, 0], cprev[:, 0:HEADS], fixo[:, 0:HEADS], ALU.subtract)
            dve.tensor_tensor(fixe[:, 1], fixs[:, 0:HEADS], fixo[:, 0:HEADS], ALU.subtract).then_inc(fix_scored, 1)
            dve.wait_ge(fix_weighed, 1)
            for z, a in ((cprev, 0), (fixs, 1)):
                dve.tensor_tensor(z[:, HEADS:2 * HEADS], z[:, HEADS:2 * HEADS], fixe[:, a], ALU.mult)
                dve.tensor_tensor(z[:, 2 * HEADS:].rearrange("p (h e) -> p h e", e=EXPERTS),
                                  z[:, 2 * HEADS:].rearrange("p (h e) -> p h e", e=EXPERTS),
                                  over(fixe[:, a], EXPERTS, 2), ALU.mult)
            flush()
            dve.tensor_tensor(fixo[:, HEADS:], cprev[:, HEADS:], fixs[:, HEADS:], ALU.add).then_inc(fix_ready, 1)

            def route(q):
                t = slice(q * TILES // ROUTES, (q + 1) * TILES // ROUTES)
                n = TILES // ROUTES
                w0, w1_, f0, f1 = wide[:, 0, t], wide[:, 1, t], one4[:, 0, t], one4[:, 1, t]
                a_, b_, top, den, own = (hx[:, k, t] for k in range(5))
                dve.wait_ge(agg_got[q], 16 * n)
                dve.tensor_tensor(top, agg[:, t, 0:HEADS], node[:, t, HE:ROW], ALU.max)
                flush()
                dve.tensor_tensor(a_, agg[:, t, 0:HEADS], top, ALU.subtract)
                dve.tensor_tensor(b_, node[:, t, HE:ROW], top, ALU.subtract).then_inc(joined, 1)
                dve.wait_ge(join_weighed, q + 1)
                dve.tensor_tensor(den, a_, agg[:, t, HEADS:2 * HEADS], ALU.mult)
                dve.tensor_tensor(own, b_, node[:, t, ROW:NODE], ALU.mult)
                dve.tensor_tensor(heads(w0), heads(agg[:, t, 2 * HEADS:]), over(a_, EXPERTS, 3), ALU.mult)
                dve.tensor_tensor(heads(w1_), heads(node[:, t, 0:HE]), over(b_, EXPERTS, 3), ALU.mult)
                flush()
                dve.tensor_tensor(w0, w0, w1_, ALU.add)
                dve.scalar_tensor_tensor(out=den, in0=den, scalar=1e-16, in1=own, op0=ALU.add, op1=ALU.add)
                flush()
                dve.reciprocal(den, den)
                flush()
                dve.tensor_tensor(heads(w0), heads(w0), over(den, EXPERTS, 3), ALU.mult)
                flush()
                dve.tensor_tensor(w0, w0, over(gat_p[:, 0], n), ALU.add)
                flush()
                dve.tensor_reduce(f0, w0, AX.X, ALU.add)
                flush()
                dve.tensor_scalar(f0, f0, 1.0 / HE, None, ALU.mult)
                flush()
                dve.tensor_tensor(w0, w0, over(f0, HE, 2), ALU.subtract)
                flush()
                dve.tensor_tensor(w1_, w0, w0, ALU.mult)
                flush()
                dve.tensor_reduce(f0, w1_, AX.X, ALU.add)
                flush()
                dve.tensor_scalar(f0, f0, 1.0 / HE, None, ALU.mult).then_inc(agg_var, 1)
                dve.tensor_tensor(w0, w0, over(gat_p[:, 1], n), ALU.mult)
                dve.wait_ge(agg_root, q + 1)
                dve.reciprocal(f1, f1)
                flush()
                dve.tensor_tensor(w0, w0, over(f1, HE, 2), ALU.mult)
                flush()
                dve.tensor_tensor(w0, w0, over(gat_p[:, 2], n), ALU.add)
                flush()
                dve.tensor_reduce(a_, w0.rearrange("p t (h e) -> p t e h", e=EXPERTS), AX.X, ALU.add)
                flush()
                dve.tensor_scalar(a_, a_, 1.0 / HEADS, None, ALU.mult)
                flush()

                def pick(scores, best, chosen, taken):
                    dve.tensor_reduce(best, scores, AX.X, ALU.max)
                    dve.memset(taken, 1.0)
                    flush()
                    dve.tensor_tensor(chosen, scores, over(best, EXPERTS, 2), ALU.is_equal)
                    flush()
                    for e in range(EXPERTS):
                        dve.tensor_tensor(chosen[:, :, e], chosen[:, :, e], taken, ALU.mult)
                        flush()
                        if e < EXPERTS - 1:
                            dve.tensor_tensor(taken, taken, chosen[:, :, e], ALU.subtract)
                            flush()

                f2, f3 = one4[:, 2, t], one4[:, 3, t]
                pick(a_, f1, b_, f2)
                dve.scalar_tensor_tensor(out=a_, in0=b_, scalar=-BIG, in1=a_, op0=ALU.mult, op1=ALU.add)
                flush()
                pick(a_, f0, top, f2)
                dve.tensor_tensor(f0, f0, f1, ALU.subtract).then_inc(top_ready, 1)
                dve.wait_ge(top_weighed, q + 1)
                dve.tensor_scalar(f2, f1, 1.0, None, ALU.add)
                flush()
                dve.reciprocal(f2, f2)
                flush()
                dve.tensor_tensor(f3, f1, f2, ALU.mult)
                dve.tensor_tensor(b_, b_, over(f2, EXPERTS, 2), ALU.mult)
                flush()
                dve.tensor_tensor(top, top, over(f3, EXPERTS, 2), ALU.mult)
                flush()
                dve.tensor_tensor(gate[:, t], b_, top, ALU.add).then_inc(routed, 1)
                flush()

            def mix(g, b, turn):
                dve.wait_ge(tokens_in[b], 32 * (turn + 1))
                for e in range(SCALED, EXPERTS):
                    for r in range(ROWS):
                        acc = x2_in[:, b, r * C:(r + 1) * C]
                        last = dve.scalar_tensor_tensor(
                            out=acc, in0=hid_y[:, b, (r * EXPERTS + e) * C:(r * EXPERTS + e + 1) * C],
                            scalar=gate[:, ds(ROWS * g + r, 1), e], in1=acc, op0=ALU.mult, op1=ALU.add)
                    flush()
                dve.wait_ge(y_scaled, g + 1)
                for e in range(SCALED):
                    acc = x2_in[:, b].rearrange("p (r f) -> p r f", f=C)
                    last = dve.tensor_tensor(acc, acc, by_expert(b)[:, :, e], ALU.add)
                    if e < SCALED - 1:
                        flush()
                last.then_inc(mixed, 1)

            for q in range(ROUTES):
                route(q)
                per = PAIRS * CHUNKS // (4 * ROUTES)
                with dve.Fori(q * per, (q + 1) * per) as g4:
                    for b in range(4):
                        mix(4 * g4 + b, b, g4)


_NAMES = ['x', 'L0_conv_Wr', 'L0_conv_br', 'L0_conv_gamma', 'L0_conv_beta', 'L0_conv_mean',
          'L0_conv_var', 'L0_conv_Ws', 'L0_conv_bs', 'L0_conv_Wi', 'L0_conv_bi', 'L0_ffn_W_gat',
          'L0_ffn_att_src', 'L0_ffn_att_dst', 'L0_ffn_b_gat', 'L0_ffn_ln_gamma',
          'L0_ffn_ln_beta', 'L0_ffn_W1', 'L0_ffn_b1', 'L0_ffn_W2', 'L0_ffn_b2',
          'L0_ffn_edge_index']


def kernel(**inputs):
    import numpy as np
    import concourse.bacc as bacc
    from concourse.bass_utils import run_bass_kernel_spmd

    nc = bacc.Bacc("TRN2", target_bir_lowering=False, num_devices=1)
    arrays, args = {}, []
    for name in _NAMES:
        a = np.ascontiguousarray(inputs[name])
        arrays[f"in_{name}"] = a
        args.append(nc.dram_tensor(f"in_{name}", a.shape, mybir.dt.from_np(a.dtype),
                                   kind="ExternalInput").ap())
    out = nc.dram_tensor("out_x", (NB, NY, NX, C), F32, kind="ExternalOutput").ap()
    metaformer_block(nc, *args, out)
    result = run_bass_kernel_spmd(nc, [arrays], core_ids=[0])
    return result.results[0]["out_x"]
```
